# Optimizing a Trainium2 kernel written in Bass

```python
import numpy as np
import jax
import jax.numpy as jnp

def _softmax(x, axis=-1):
    return jax.nn.softmax(x, axis=axis)

def _gelu(x):
    return jax.nn.gelu(x, approximate=True)

def _silu(x):
    return jax.nn.silu(x)

def _sigmoid(x):
    return jax.nn.sigmoid(x)

def _layernorm(x, axis=-1, eps=1e-05):
    m = jnp.mean(x, axis=axis, keepdims=True)
    v = jnp.var(x, axis=axis, keepdims=True)
    return (x - m) / jnp.sqrt(v + eps)

def _scatter_add(tgt, idx, src, axis=0):
    return tgt.at[idx].add(src)

def _segment_sum(src, seg, n):
    return jax.ops.segment_sum(src, seg, n)
kernel_name = 'mk_decoder_preln_d2_seqx_r8_d2a8e2'

def setup_inputs(seed: int=0):
    np.random.seed(seed)
    _w = jnp.asarray

    def _rec_inputs():
        import jax
        import jax.numpy as jnp
        _rk = jax.random.key(seed)
        x = -0.0003929 + 0.9999 * jax.random.normal(jax.random.fold_in(_rk, 1), (16, 128, 128), jnp.float32)
        _lenS = 128 - jax.random.randint(jax.random.fold_in(_rk, 7), (16,), 0, max(1, 128 // 4) + 1, jnp.int32)
        _lenS2 = 120 - jax.random.randint(jax.random.fold_in(_rk, 8), (16,), 0, max(1, 120 // 4) + 1, jnp.int32)
        _ctx_512P = jax.random.normal(jax.random.fold_in(_rk, 11), (16, 16, 64), jnp.float32)
        _ctx_512c = jax.random.dirichlet(jax.random.fold_in(_rk, 511), 0.3 * jnp.ones((16,), jnp.float32), (16, 120))
        _ctx_512t = jnp.einsum('bsk,bkd->bsd', _ctx_512c, _ctx_512P)
        _ctx_512t = _ctx_512t * jax.lax.rsqrt(jnp.mean(jnp.square(_ctx_512t)) + 1e-12) * 0.953939
        ctx_512 = 4.13588e-05 + 0.999923 * (_ctx_512t + 0.3 * jax.random.normal(jax.random.fold_in(_rk, 611), (16, 120, 64), jnp.float32))
        return (x, ctx_512)
    x, ctx_512 = _rec_inputs()

    def _L0_attn_setup():
        import jax, jax.numpy as jnp
        import numpy as np
        key = jax.random.key(seed)
        B, L, d_model, d_state, expand = (2, 256, 128, 16, 2)
        d_inner = expand * d_model
        ks = jax.random.split(key, 8)
        s = lambda k, shape, scale: jax.random.normal(k, shape, dtype=jnp.float32) * scale
        x = s(ks[0], (B, L, d_model), 1.0)
        W_in = s(ks[1], (d_model, 2 * d_inner), 0.02)
        W_delta = s(ks[2], (d_inner, d_inner), 0.02)
        b_delta = s(ks[3], (d_inner,), 0.02)
        W_B = s(ks[4], (d_inner, d_state), 0.02)
        W_C = s(ks[5], (d_inner, d_state), 0.02)
        A_log = jnp.log(jnp.broadcast_to(jnp.arange(1, d_state + 1, dtype=jnp.float32), (d_inner, d_state)))
        D_param = jnp.ones((d_inner,), dtype=jnp.float32)
        W_out = s(ks[6], (d_inner, d_model), 0.02)
        return dict(x=x, W_in=W_in, W_delta=W_delta, b_delta=b_delta, W_B=W_B, W_C=W_C, A_log=A_log, D_param=D_param, W_out=W_out)
    _L0_attn_all = _L0_attn_setup()
    _L0_attn_in = {k: v for k, v in _L0_attn_all.items() if k in ('W_in', 'W_delta', 'b_delta', 'W_B', 'W_C', 'A_log', 'D_param', 'W_out')}
    del _L0_attn_all

    def _L0_xattn_setup():
        import jax, jax.numpy as jnp
        import numpy as np
        B, LQ, LK = (8, 256, 256)
        QD, KD, VD = (128, 64, 64)
        key = jax.random.key(seed)
        ks = jax.random.split(key, 9)
        s = 0.02
        return {'query': jax.random.normal(ks[0], (B, LQ, QD), jnp.float32), 'key': jax.random.normal(ks[1], (B, LK, KD), jnp.float32), 'value': jax.random.normal(ks[2], (B, LK, VD), jnp.float32), 'Wq': jax.random.normal(ks[3], (QD, QD), jnp.float32) * s, 'bq': jnp.zeros((QD,), jnp.float32), 'Wk': jax.random.normal(ks[4], (KD, QD), jnp.float32) * s, 'bk': jnp.zeros((QD,), jnp.float32), 'Wv': jax.random.normal(ks[5], (VD, QD), jnp.float32) * s, 'bv': jnp.zeros((QD,), jnp.float32)}
    _L0_xattn_all = _L0_xattn_setup()
    _L0_xattn_in = {k: v for k, v in _L0_xattn_all.items() if k in ('Wq', 'bq', 'Wk', 'bk', 'Wv', 'bv')}
    del _L0_xattn_all

    def _L0_ffn_setup():
        import jax, jax.numpy as jnp
        import numpy as np
        D_MODEL = 128
        HIDDEN = 256
        N_EXPERTS = 8
        TOP_K = 2
        BATCH = 2
        SEQ = 256
        key = jax.random.key(seed)
        ks = jax.random.split(key, 9)
        s = 0.02
        return {'x': jax.random.normal(ks[0], (BATCH, SEQ, D_MODEL), dtype=jnp.float32), 'w_router': jax.random.normal(ks[1], (D_MODEL, N_EXPERTS), dtype=jnp.float32) * s, 'w1': jax.random.normal(ks[2], (N_EXPERTS, D_MODEL, HIDDEN), dtype=jnp.float32) * s, 'w3': jax.random.normal(ks[3], (N_EXPERTS, D_MODEL, HIDDEN), dtype=jnp.float32) * s, 'w2': jax.random.normal(ks[4], (N_EXPERTS, HIDDEN, D_MODEL), dtype=jnp.float32) * s, 'sw1': jax.random.normal(ks[5], (D_MODEL, HIDDEN), dtype=jnp.float32) * s, 'sw3': jax.random.normal(ks[6], (D_MODEL, HIDDEN), dtype=jnp.float32) * s, 'sw2': jax.random.normal(ks[7], (HIDDEN, D_MODEL), dtype=jnp.float32) * s}
    _L0_ffn_all = _L0_ffn_setup()
    _L0_ffn_in = {k: v for k, v in _L0_ffn_all.items() if k in ('w_router', 'w1', 'w3', 'w2', 'sw1', 'sw3', 'sw2')}
    del _L0_ffn_all

    def _L1_attn_setup():
        import jax, jax.numpy as jnp
        import numpy as np
        D_MODEL = 128
        EXPAND = 2
        D_INNER = D_MODEL * EXPAND
        C = 8
        B, T = (4, 256)
        key = jax.random.key(seed)
        ks = jax.random.split(key, 8)
        x = jax.random.normal(ks[0], (B, T, D_MODEL), jnp.float32)
        a = np.log(1.0 / np.exp(np.log(0.999) / C) - 1.0)
        b = np.log(1.0 / np.exp(np.log(0.9) / C) - 1.0)
        omega = (a + (b - a) * jax.random.uniform(ks[1], (1, 1, D_INNER))).astype(jnp.float32)
        s = 0.02
        Win = (jax.random.normal(ks[2], (2 * D_INNER, D_MODEL)) * s).astype(jnp.float32)
        Wl = (jax.random.normal(ks[3], (D_INNER, D_INNER)) * s).astype(jnp.float32)
        bl = jnp.zeros((D_INNER,), jnp.float32)
        Wv = (jax.random.normal(ks[4], (D_INNER, D_INNER)) * s).astype(jnp.float32)
        bv = jnp.zeros((D_INNER,), jnp.float32)
        Wout = (jax.random.normal(ks[5], (D_MODEL, D_INNER)) * s).astype(jnp.float32)
        return dict(x=x, omega=omega, Win=Win, Wl=Wl, bl=bl, Wv=Wv, bv=bv, Wout=Wout)
    _L1_attn_all = _L1_attn_setup()
    _L1_attn_in = {k: v for k, v in _L1_attn_all.items() if k in ('omega', 'Win', 'Wl', 'bl', 'Wv', 'bv', 'Wout')}
    del _L1_attn_all

    def _L1_xattn_setup():
        import jax, jax.numpy as jnp
        import numpy as np
        HEADS = 16
        D_MODEL = 128
        IMG_MODEL = 64
        D_K = D_MODEL // HEADS
        key = jax.random.key(seed)
        ks = jax.random.split(key, 12)
        B, LQ, LKV = (8, 256, 128)
        s_dm = 1.0 / np.sqrt(D_MODEL)
        s_im = 1.0 / np.sqrt(IMG_MODEL)
        return {'q': jax.random.normal(ks[0], (B, LQ, D_MODEL), jnp.float32), 'k': jax.random.normal(ks[1], (B, LKV, IMG_MODEL), jnp.float32), 'v': jax.random.normal(ks[2], (B, LKV, IMG_MODEL), jnp.float32), 'Wq': jax.random.normal(ks[3], (D_MODEL, D_MODEL), jnp.float32) * s_dm, 'bq': jnp.zeros((D_MODEL,), jnp.float32), 'Wk': jax.random.normal(ks[4], (IMG_MODEL, D_MODEL), jnp.float32) * s_im, 'bk': jnp.zeros((D_MODEL,), jnp.float32), 'Wv': jax.random.normal(ks[5], (IMG_MODEL, D_MODEL), jnp.float32) * s_im, 'bv': jnp.zeros((D_MODEL,), jnp.float32), 'Wo': jax.random.normal(ks[6], (D_MODEL, D_MODEL), jnp.float32) * s_dm, 'bo': jnp.zeros((D_MODEL,), jnp.float32)}
    _L1_xattn_all = _L1_xattn_setup()
    _L1_xattn_in = {k: v for k, v in _L1_xattn_all.items() if k in ('Wq', 'bq', 'Wk', 'bk', 'Wv', 'bv', 'Wo', 'bo')}
    del _L1_xattn_all

    def _L1_ffn_setup():
        import jax, jax.numpy as jnp
        import numpy as np
        B, S, H, F, E, K = (2, 256, 128, 512, 8, 2)

        def _init_w(key, shape, fan_in):
            return jax.random.normal(key, shape, jnp.float32) * fan_in ** (-0.5)

        def _ffn(x, wi, bi, wo, bo):
            return jax.nn.selu(x @ wi + bi) @ wo + bo
        key = jax.random.key(seed)
        ks = jax.random.split(key, 6)
        return {'x': jax.random.normal(ks[0], (B, S, H), jnp.float32), 'gate_wi': _init_w(ks[1], (H, F), H), 'gate_bi': jnp.zeros((F,), jnp.float32), 'gate_wo': _init_w(ks[2], (F, H), F), 'gate_bo': jnp.zeros((H,), jnp.float32), 'exp_wi': _init_w(ks[3], (E, H, F), H), 'exp_bi': jnp.zeros((E, F), jnp.float32), 'exp_wo': _init_w(ks[4], (E, F, H), F), 'exp_bo': jnp.zeros((E, H), jnp.float32)}
    _L1_ffn_all = _L1_ffn_setup()
    _L1_ffn_in = {k: v for k, v in _L1_ffn_all.items() if k in ('gate_wi', 'gate_bi', 'gate_wo', 'gate_bo', 'exp_wi', 'exp_bi', 'exp_wo', 'exp_bo')}
    del _L1_ffn_all
    return {'x': x, 'ctx_512': ctx_512, 'L0_attn_W_in': _L0_attn_in['W_in'], 'L0_attn_W_delta': _L0_attn_in['W_delta'], 'L0_attn_b_delta': _L0_attn_in['b_delta'], 'L0_attn_W_B': _L0_attn_in['W_B'], 'L0_attn_W_C': _L0_attn_in['W_C'], 'L0_attn_A_log': _L0_attn_in['A_log'], 'L0_attn_D_param': _L0_attn_in['D_param'], 'L0_attn_W_out': _L0_attn_in['W_out'], 'L0_xattn_Wq': _L0_xattn_in['Wq'], 'L0_xattn_bq': _L0_xattn_in['bq'], 'L0_xattn_Wk': _L0_xattn_in['Wk'], 'L0_xattn_bk': _L0_xattn_in['bk'], 'L0_xattn_Wv': _L0_xattn_in['Wv'], 'L0_xattn_bv': _L0_xattn_in['bv'], 'L0_ffn_w_router': _L0_ffn_in['w_router'], 'L0_ffn_w1': _L0_ffn_in['w1'], 'L0_ffn_w3': _L0_ffn_in['w3'], 'L0_ffn_w2': _L0_ffn_in['w2'], 'L0_ffn_sw1': _L0_ffn_in['sw1'], 'L0_ffn_sw3': _L0_ffn_in['sw3'], 'L0_ffn_sw2': _L0_ffn_in['sw2'], 'L1_attn_omega': _L1_attn_in['omega'], 'L1_attn_Win': _L1_attn_in['Win'], 'L1_attn_Wl': _L1_attn_in['Wl'], 'L1_attn_bl': _L1_attn_in['bl'], 'L1_attn_Wv': _L1_attn_in['Wv'], 'L1_attn_bv': _L1_attn_in['bv'], 'L1_attn_Wout': _L1_attn_in['Wout'], 'L1_xattn_Wq': _L1_xattn_in['Wq'], 'L1_xattn_bq': _L1_xattn_in['bq'], 'L1_xattn_Wk': _L1_xattn_in['Wk'], 'L1_xattn_bk': _L1_xattn_in['bk'], 'L1_xattn_Wv': _L1_xattn_in['Wv'], 'L1_xattn_bv': _L1_xattn_in['bv'], 'L1_xattn_Wo': _L1_xattn_in['Wo'], 'L1_xattn_bo': _L1_xattn_in['bo'], 'L1_ffn_gate_wi': _L1_ffn_in['gate_wi'], 'L1_ffn_gate_bi': _L1_ffn_in['gate_bi'], 'L1_ffn_gate_wo': _L1_ffn_in['gate_wo'], 'L1_ffn_gate_bo': _L1_ffn_in['gate_bo'], 'L1_ffn_exp_wi': _L1_ffn_in['exp_wi'], 'L1_ffn_exp_bi': _L1_ffn_in['exp_bi'], 'L1_ffn_exp_wo': _L1_ffn_in['exp_wo'], 'L1_ffn_exp_bo': _L1_ffn_in['exp_bo']}

def reference(x, ctx_512, L0_attn_W_in, L0_attn_W_delta, L0_attn_b_delta, L0_attn_W_B, L0_attn_W_C, L0_attn_A_log, L0_attn_D_param, L0_attn_W_out, L0_xattn_Wq, L0_xattn_bq, L0_xattn_Wk, L0_xattn_bk, L0_xattn_Wv, L0_xattn_bv, L0_ffn_w_router, L0_ffn_w1, L0_ffn_w3, L0_ffn_w2, L0_ffn_sw1, L0_ffn_sw3, L0_ffn_sw2, L1_attn_omega, L1_attn_Win, L1_attn_Wl, L1_attn_bl, L1_attn_Wv, L1_attn_bv, L1_attn_Wout, L1_xattn_Wq, L1_xattn_bq, L1_xattn_Wk, L1_xattn_bk, L1_xattn_Wv, L1_xattn_bv, L1_xattn_Wo, L1_xattn_bo, L1_ffn_gate_wi, L1_ffn_gate_bi, L1_ffn_gate_wo, L1_ffn_gate_bo, L1_ffn_exp_wi, L1_ffn_exp_bi, L1_ffn_exp_wo, L1_ffn_exp_bo):
    import jax
    import jax.numpy as jnp

    def _L0_attn_ref(x, W_in, W_delta, b_delta, W_B, W_C, A_log, D_param, W_out):
        import jax, jax.numpy as jnp
        import numpy as np
        d_inner = W_delta.shape[0]
        x_and_res = x @ W_in
        u, res = (x_and_res[..., :d_inner], x_and_res[..., d_inner:])
        u = jax.nn.silu(u)
        delta = jax.nn.softplus(u @ W_delta + b_delta)
        Bm = u @ W_B
        Cm = u @ W_C
        A = -jnp.exp(A_log)

        def step(h, inp):
            d_t, B_t, C_t, u_t = inp
            dA = jnp.exp(d_t[..., None] * A)
            h = dA * h + d_t[..., None] * B_t[:, None, :] * u_t[..., None]
            y_t = jnp.einsum('bdn,bn->bd', h, C_t)
            return (h, y_t)
        Bsz = x.shape[0]
        h0 = jnp.zeros((Bsz, d_inner, A.shape[1]), dtype=x.dtype)
        xs = (jnp.swapaxes(delta, 0, 1), jnp.swapaxes(Bm, 0, 1), jnp.swapaxes(Cm, 0, 1), jnp.swapaxes(u, 0, 1))
        _, ys = jax.lax.scan(step, h0, xs)
        y = jnp.swapaxes(ys, 0, 1) + u * D_param
        y = y * jax.nn.silu(res)
        return y @ W_out

    def _L0_xattn_ref(query, key, value, Wq, bq, Wk, bk, Wv, bv):
        import jax, jax.numpy as jnp
        import numpy as np
        B, LQ, LK = (8, 256, 256)
        QD, KD, VD = (128, 64, 64)
        q = jnp.einsum('bld,de->ble', query, Wq) + bq
        k = jnp.einsum('bld,de->ble', key, Wk) + bk
        v = jnp.einsum('bld,de->ble', value, Wv) + bv
        scores = jnp.einsum('bqe,bke->bqk', q, k)
        attn = jax.nn.softmax(scores, axis=-1)
        out = jnp.einsum('bqk,bke->bqe', attn, v)
        return out

    def _L0_ffn_ref(x, w_router, w1, w3, w2, sw1, sw3, sw2):
        import jax, jax.numpy as jnp
        import numpy as np
        D_MODEL = 128
        HIDDEN = 256
        N_EXPERTS = 8
        TOP_K = 2
        BATCH = 2
        SEQ = 256
        b, s, d = x.shape
        xf = x.reshape(b * s, d)
        probs = jax.nn.softmax(xf @ w_router, axis=-1)
        top_vals, top_idx = jax.lax.top_k(probs, TOP_K)
        gates = top_vals / jnp.sum(top_vals, axis=-1, keepdims=True)
        onehot = jax.nn.one_hot(top_idx, N_EXPERTS, dtype=xf.dtype)
        cw = jnp.einsum('tk,tke->te', gates, onehot)
        h1 = jnp.einsum('td,edh->eth', xf, w1)
        h3 = jnp.einsum('td,edh->eth', xf, w3)
        y = jnp.einsum('eth,ehd->etd', jax.nn.silu(h1) * h3, w2)
        out = jnp.einsum('etd,te->td', y, cw)
        out = out + jax.nn.silu(xf @ sw1) * (xf @ sw3) @ sw2
        return out.reshape(b, s, d)

    def _L1_attn_ref(x, omega, Win, Wl, bl, Wv, bv, Wout):
        import jax, jax.numpy as jnp
        import numpy as np
        D_MODEL = 128
        EXPAND = 2
        D_INNER = D_MODEL * EXPAND
        C = 8
        B, T = (4, 256)
        xz = jnp.einsum('btd,ed->bte', x, Win)
        xi, z = jnp.split(xz, 2, axis=-1)
        log_lam = -C * jax.nn.softplus(omega) * jax.nn.sigmoid(jnp.einsum('bti,ji->btj', xi, Wl) + bl)
        lam = jnp.exp(log_lam)
        v = jnp.einsum('bti,ji->btj', xi, Wv) + bv
        h0 = xi[:, 0]

        def step(h_prev, inp):
            x_t, v_t, lam_t = inp
            vh = jnp.sum(v_t * h_prev, axis=-1, keepdims=True)
            vv = jnp.sum(v_t * v_t, axis=-1, keepdims=True)
            Qh = h_prev - 2.0 * v_t * (vh / vv)
            h = lam_t * Qh + (1.0 - lam_t) * x_t
            return (h, h)
        xs = (jnp.swapaxes(xi[:, 1:], 0, 1), jnp.swapaxes(v[:, 1:], 0, 1), jnp.swapaxes(lam[:, 1:], 0, 1))
        _, hs = jax.lax.scan(step, h0, xs)
        h = jnp.concatenate([h0[:, None], jnp.swapaxes(hs, 0, 1)], axis=1)
        return jnp.einsum('bti,di->btd', jax.nn.silu(z) * h, Wout)

    def _L1_xattn_ref(q, k, v, Wq, bq, Wk, bk, Wv, bv, Wo, bo):
        import jax, jax.numpy as jnp
        import numpy as np
        HEADS = 16
        D_MODEL = 128
        IMG_MODEL = 64
        D_K = D_MODEL // HEADS
        B, LQ, _ = q.shape
        LKV = k.shape[1]
        qh = (q @ Wq + bq).reshape(B, LQ, HEADS, D_K).transpose(0, 2, 1, 3)
        kh = (k @ Wk + bk).reshape(B, LKV, HEADS, D_K).transpose(0, 2, 1, 3)
        vh = (v @ Wv + bv).reshape(B, LKV, HEADS, D_K).transpose(0, 2, 1, 3)
        scale = 1.0 / np.sqrt(D_K)
        scores = jnp.einsum('bhqd,bhkd->bhqk', qh, kh) * scale
        attn = jax.nn.softmax(scores, axis=-1)
        out = jnp.einsum('bhqk,bhkd->bhqd', attn, vh)
        concat = out.transpose(0, 2, 1, 3).reshape(B, LQ, D_MODEL)
        return concat @ Wo + bo

    def _L1_ffn_ref(x, gate_wi, gate_bi, gate_wo, gate_bo, exp_wi, exp_bi, exp_wo, exp_bo):
        import jax, jax.numpy as jnp
        import numpy as np
        B, S, H, F, E, K = (2, 256, 128, 512, 8, 2)

        def _init_w(key, shape, fan_in):
            return jax.random.normal(key, shape, jnp.float32) * fan_in ** (-0.5)

        def _ffn(x, wi, bi, wo, bo):
            return jax.nn.selu(x @ wi + bi) @ wo + bo
        Bb, Ss, Hh = x.shape
        xf = x.reshape(-1, Hh)
        gate_logits = _ffn(xf, gate_wi, gate_bi, gate_wo, gate_bo)
        topv, topi = jax.lax.top_k(gate_logits, K)
        topv = topv / jnp.sum(topv, axis=-1, keepdims=True)
        onehot = (topi[..., None] == jnp.arange(E)).astype(x.dtype)
        w = jnp.einsum('nk,nke->ne', topv, onehot)
        h = jax.nn.selu(jnp.einsum('nh,ehf->enf', xf, exp_wi) + exp_bi[:, None, :])
        out_e = jnp.einsum('enf,efh->enh', h, exp_wo) + exp_bo[:, None, :]
        out = jnp.einsum('enh,ne->nh', out_e, w)
        return out.reshape(Bb, Ss, Hh)
    x = x + _L0_attn_ref(_layernorm(x, axis=-1), L0_attn_W_in, L0_attn_W_delta, L0_attn_b_delta, L0_attn_W_B, L0_attn_W_C, L0_attn_A_log, L0_attn_D_param, L0_attn_W_out)
    x = x + _L0_xattn_ref(_layernorm(x, axis=-1), ctx_512, ctx_512, L0_xattn_Wq, L0_xattn_bq, L0_xattn_Wk, L0_xattn_bk, L0_xattn_Wv, L0_xattn_bv)
    x = x + _L0_ffn_ref(_layernorm(x, axis=-1), L0_ffn_w_router, L0_ffn_w1, L0_ffn_w3, L0_ffn_w2, L0_ffn_sw1, L0_ffn_sw3, L0_ffn_sw2)
    x = x + _L1_attn_ref(_layernorm(x, axis=-1), L1_attn_omega, L1_attn_Win, L1_attn_Wl, L1_attn_bl, L1_attn_Wv, L1_attn_bv, L1_attn_Wout)
    x = x + _L1_xattn_ref(_layernorm(x, axis=-1), ctx_512, ctx_512, L1_xattn_Wq, L1_xattn_bq, L1_xattn_Wk, L1_xattn_bk, L1_xattn_Wv, L1_xattn_bv, L1_xattn_Wo, L1_xattn_bo)
    x = x + _L1_ffn_ref(_layernorm(x, axis=-1), L1_ffn_gate_wi, L1_ffn_gate_bi, L1_ffn_gate_wo, L1_ffn_gate_bo, L1_ffn_exp_wi, L1_ffn_exp_bi, L1_ffn_exp_wo, L1_ffn_exp_bo)
    return x

_drawn_inputs = setup_inputs


def setup_inputs(seed=0):
    import zlib

    import numpy as np

    out = dict(_drawn_inputs(seed))
    spreads = {'L0_attn_D_param': (1.0, 0.6),
     'L0_xattn_bq': (0.0, 0.439),
     'L0_xattn_bk': (0.0, 2.0),
     'L0_xattn_bv': (0.0, 0.1),
     'L1_attn_bl': (0.0, 0.8),
     'L1_attn_bv': (0.0, 0.8),
     'L1_xattn_bq': (0.0, 0.54),
     'L1_xattn_bk': (0.0, 2.0),
     'L1_xattn_bv': (0.0, 0.1),
     'L1_xattn_bo': (0.0, 0.1),
     'L1_ffn_gate_bi': (0.0, 0.1),
     'L1_ffn_gate_bo': (0.0, 0.1),
     'L1_ffn_exp_bi': (0.0, 0.548),
     'L1_ffn_exp_bo': (0.0, 0.566)}
    factors = {'L0_attn_W_in': 3.495,
     'L0_attn_W_delta': 8.0,
     'L0_attn_b_delta': 8.0,
     'L0_attn_W_B': 8.0,
     'L0_attn_W_C': 8.0,
     'L0_attn_A_log': 8.0,
     'L0_attn_W_out': 5.248,
     'L0_ffn_w_router': 4.171,
     'L0_ffn_w1': 3.613,
     'L0_ffn_w3': 3.566,
     'L0_ffn_w2': 3.709,
     'L0_ffn_sw1': 3.221,
     'L0_ffn_sw3': 2.941,
     'L0_ffn_sw2': 4.102,
     'L1_attn_omega': 5.599,
     'L1_attn_Win': 5.285,
     'L1_attn_Wl': 8.0,
     'L1_attn_Wv': 5.067,
     'L1_attn_Wout': 3.408,
     'L0_xattn_Wq': 2.957}
    for name, (base, spread) in spreads.items():
        noise = np.random.default_rng([zlib.crc32(name.encode()), seed]).standard_normal(out[name].shape)
        drawn = base * np.exp(spread * noise) if base else spread * noise
        out[name] = jnp.asarray(drawn.astype(out[name].dtype))
    for name, factor in factors.items():
        out[name] = (out[name] * factor).astype(out[name].dtype)
    return out
```

```python
import numpy as np
import concourse.bass as bass
from concourse import mybir
from contextlib import ExitStack

F32 = mybir.dt.float32
BF16 = mybir.dt.bfloat16
ALU = mybir.AluOpType
ACT = mybir.ActivationFunctionType
AX = mybir.AxisListType

P = 128
B, T, D = 16, 128, 128
N = B * T
GB = 4
NG = B // GB
GT = GB * T
DI = 256
HI = DI // P
NS = 16
LK, DC = 120, 64
E = 8
H0 = 256
M0 = H0 // P
H1 = 512
M1 = H1 // P
NH, DK = 16, 8
HQ = 4
EPS = 1e-5
SELU_L = 1.0507009873554805
SELU_A = 1.6732632423543772
SELU_LA = SELU_L * SELU_A
NLN = 6


def decoder_program(nc, a, out):
    with ExitStack() as ctx:
        def sb(name, shape, dt=F32):
            return ctx.enter_context(nc.sbuf_tensor(name, shape, dt))

        def sem(name):
            return ctx.enter_context(nc.semaphore(name))

        ps = ctx.enter_context(nc.psum_tensor("ps", [P, 8, GT], F32))
        X = sb("X", [P, B, D])
        LN = sb("LN", [P, 2, N])
        xn = LN[:, 0, :].rearrange("p (b d) -> p b d", b=B)
        xnT = LN[:, 1, :]
        G = sb("G", [P, 6, HI, N])
        R = sb("R", [P, 4, 2, 2 * GT])
        stats = sb("stats", [P, B, 6])
        mv = sb("mv", [P, B, 2])
        rstd = sb("rstd", [P, B])
        mhalf = sb("mhalf", [P, B])
        ident = sb("ident", [P, P])
        ones = sb("ones", [P, P])
        sel = sb("sel", [3 * 32, 32, P], BF16)
        bc3 = sb("bc3", [3 * 32, N], BF16)
        hmask = sb("hmask", [P, HQ])
        tri = sb("tri", [P, E, E])
        negA = sb("negA", [P, HI, NS])
        diagD = sb("diagD", [P, HI, P])
        router = sb("router", [P, 6, B, E])
        cw0 = sb("cw0", [P, B, E + 1])
        cw1 = sb("cw1", [P, B, E])
        small = sb("small", [P, 4, B])
        coef = sb("coef", [P, 4, HI])
        bq1 = sb("bq1", [P, 1])
        ebs = sb("ebs", [P, E + 1, M1])
        mrec = sb("mrec", [P, HI, B])
        prec = sb("prec", [P, HI, B])
        rrec = sb("rrec", [P, HI, B])

        w = {}
        for name, shape in (
            ("W_in", [P, 4, P]), ("W_delta", [P, HI, DI]), ("b_delta", [P, HI]), ("W_BC", [P, HI, 2 * NS]),
            ("A_log", [P, HI, NS]), ("D_param", [P, HI]), ("W_out", [P, HI, D]),
            ("Wq0", [P, P]), ("bq0", [P, 1]), ("Wk0", [DC + 1, P]), ("Wv0", [DC + 1, P]), ("ctxT", [DC + 1, B, LK]),
            ("router0", [P, E]),
            ("omega", [P, HI]), ("Win1", [P, 4, P]), ("Wl", [P, HI, DI]), ("bl", [P, HI]), ("Wv", [P, HI, DI]),
            ("bv", [P, HI]), ("Wout1", [P, HI, D]),
            ("Wq1", [P, P]), ("bq1", [P, 1]), ("Wk1", [DC + 1, P]), ("Wv1", [DC + 1, P]), ("Wo1", [P, P]),
            ("bo1", [1, P]),
            ("gate_wi", [P, M1, P]), ("gate_bi", [P, M1]), ("gate_wo", [P, M1, D]), ("gate_bo", [1, D]),
            ("exp_bi", [P, E, M1]), ("exp_bo", [E, P]),
        ):
            w[name] = sb("w_" + name, shape)
        ew0 = sb("ew0", [P, 2, 3, M0 * P])
        ew1 = R[:, 0, :, :].rearrange("p s (w n) -> p s w n", w=2)

        S = {}
        for name in (
            "x_in", "w_mamba", "w_ctx", "w_lru", "w_att", "w_gate", "w_e0a", "w_e0b", "w_e1a", "w_e1b", "out_sent",
            "const", "const_step", "dve_step", "act_step", "pool_step",
            "ln_stats", "ln_rstd", "ln_xn", "ln_tr", "ln_xnT",
            "in_mm", "in_silu", "dl_mm", "dl_abs", "dl_relu", "dl_ln", "dl_done", "bc_mm", "bc_split",
            "diag_ready", "b_bcast", "c_bcast", "decay", "b_copied", "drive", "scanned", "hc", "y_acc", "y_gated", "a_out", "a_res",
            "q_mm", "q_ev", "k_mm", "k_ev", "v_mm", "v_ev", "sc_mm", "sc_max", "sc_exp", "pt_mm", "pt_ev", "pv_mm", "pv_res",
            "rt_mm", "rt_sub", "rt_exp", "rt_cw", "up_mm", "silu0", "hid0", "down0", "res0",
            "xz_mm", "xz_ev", "lv_mm", "lv_ev", "lam_done", "sq_done", "vv_mm", "w_done", "r_prod", "r_dot", "r_h",
            "g1_ready", "d_out", "d_res",
            "hq_mm", "hq_ev", "hk_mm", "hk_ev", "hv_mm", "hv_ev", "hs_mm", "hs_sub", "hs_exp", "ht_mm", "ht_ev", "ho_mm",
            "ho_norm", "hoT_mm", "hoT_ev", "hw_mm", "hw_res",
            "gu_mm", "g_act", "g_hid", "gl_mm", "gl_cw", "wt_mm", "wt_ev", "eb_mm", "eb_res",
            "up1_mm", "act1", "hid1", "down1", "res1", "coef_done", "coef_sp", "omega_ln",
        ):
            S[name] = sem(name)

        class Chain:

            def __init__(self, eng, s):
                self.eng, self.s, self.n = eng, s, 0

            def __call__(self, ins):
                self.n += 1
                ins.then_inc(self.s, 1)
                self.eng.wait_ge(self.s, self.n)

        block = ctx.enter_context(nc.Block())

        gcols = lambda g: slice(g * GT, (g + 1) * GT)
        gb = lambda g: slice(g * GB, (g + 1) * GB)
        GBUF = lambda i: G[:, i, :, :]

        uT, zT, dT, duT = (GBUF(i) for i in range(4))
        yT = GBUF(4)
        tmpT = GBUF(5)
        dBu = R[:, 0, :, :]
        hst = R[:, 1, :, :]
        hC = R[:, 2, :, :]
        Bsb = R[:, 3, :, 0:GT]
        qT = G[:, 0, 0, :]
        kT = G[:, 0, 1, 0:B * LK].rearrange("p (b k) -> p b k", b=B)
        vS = G[:, 1, 0, :].rearrange("p (b d) -> p b d", b=B)
        pr = G[:, 1, 1, 0:B * LK].rearrange("p (b k) -> p b k", b=B)
        prT = G[:, 2, 0, :].rearrange("p (b q) -> p b q", b=B)
        sh = G[:, 3, :, :].rearrange("p h (s n) -> p (h s) n", n=2 * GT)
        hidr = G[:, 4, :, :].rearrange("p h (s n) -> p (h s) n", n=2 * GT)
        pair = G[:, 5, 0, :].rearrange("p (k b e f) -> p k b e f", k=2, b=B, e=E)
        gl = G[:, 3, 0, :].rearrange("p (b d) -> p b d", b=B)
        top = G[:, 3, 1, 0:B * 8].rearrange("p (b k) -> p b k", b=B)
        cwT = G[0:E, 5, 1, :].rearrange("p (b t) -> p b t", b=B)
        xi, z1, lam, vv, bb, ww = (GBUF(i) for i in range(6))
        sq = LN
        q1T = G[:, 0, 0, :]
        kb = G[:, 1:3, :, :].rearrange("p g h n -> p (g h n)")[:, 0:B * HQ * LK].rearrange(
            "p (b j k) -> p b j k", b=B, j=HQ)
        k1T = G[:, 0, 1, 0:B * LK].rearrange("p (b k) -> p b k", b=B)
        va = G[:, 3, :, :].rearrange("p h n -> p (h n)")[:, 0:B * NH * (DK + 1)].rearrange(
            "p (b h d) -> p b h d", b=B, h=NH)
        p1 = G[:, 4, 0, 0:NH * LK].rearrange("p (h k) -> p h k", h=NH)
        e1 = G[:, 4, 1, 0:NH * LK].rearrange("p (h k) -> p h k", h=NH)
        p1T = G[:, 5, 0, :].rearrange("p (h q) -> p h q", h=NH)
        o1 = G[:, 5, 1, 0:P]
        o1T = G[:, 5, 1, P:2 * P]
        o1r = G[:, 5, 1, 2 * P:2 * P + NH]

        def bank(i, n=1):
            return ps[:, i:i + n, :]

        @block.sync
        def _(sp):
            for g in range(NG):
                sp.dma_start(X[:, gb(g), :], a["x"].rearrange("b t d -> t b d")[:, gb(g), :]).then_inc(S["x_in"], 16)
            half = lambda ap: ap.rearrange("(k p) n -> p k n", p=P)
            row = lambda ap: ap.rearrange("(o n) -> o n", o=1)
            tiles = lambda ap: ap.rearrange("p (m n) -> p m n", n=P)

            def load(s, pairs):
                for name, src in pairs:
                    sp.dma_start(w[name][:], src).then_inc(S[s], 16)

            load("w_mamba", (("W_in", tiles(a["W_in"])), ("W_delta", half(a["W_delta"])), ("b_delta", a["b_delta"]),
                             ("W_BC", half(a["W_BC"])), ("A_log", half(a["A_log"])), ("D_param", a["D_param"]),
                             ("W_out", half(a["W_out"])), ("omega", a["omega"])))
            load("w_ctx", (("ctxT", a["ctxT"]), ("Wq0", a["Wq0"]), ("bq0", a["bq0"]), ("Wk0", a["Wk0"]),
                           ("Wv0", a["Wv0"]), ("router0", a["router0"])))
            load("w_lru", (("Win1", tiles(a["Win1"])), ("Wl", half(a["Wl"])), ("bl", a["bl"]),
                           ("Wv", half(a["Wv"])), ("bv", a["bv"]), ("Wout1", half(a["Wout1"]))))
            load("w_att", (("Wq1", a["Wq1"]), ("bq1", a["bq1"]), ("Wk1", a["Wk1"]), ("Wv1", a["Wv1"]),
                           ("Wo1", a["Wo1"]), ("bo1", row(a["bo1"]))))
            load("w_gate", (("gate_wi", tiles(a["gate_wi"])), ("gate_bi", a["gate_bi"]),
                            ("gate_wo", half(a["gate_wo"])), ("gate_bo", row(a["gate_bo"])),
                            ("exp_bi", a["exp_bi"]), ("exp_bo", a["exp_bo"])))

            def expert0(slot, s, w1, w3, w2):
                sp.dma_start(ew0[:, slot, 0, :], w1).then_inc(S[s], 16)
                sp.dma_start(ew0[:, slot, 1, :], w3).then_inc(S[s], 16)
                sp.dma_start(ew0[:, slot, 2, :].rearrange("p (m n) -> p m n", m=M0), half(w2)).then_inc(S[s], 16)

            expert0(0, "w_e0a", a["w1"][0], a["w3"][0], a["w2"][0])
            expert0(1, "w_e0b", a["w1"][1], a["w3"][1], a["w2"][1])
            for e in range(2, E + 1):
                sp.wait_ge(S["down0"], NG * (e - 1))
                if e < E:
                    expert0(e % 2, "w_e0b" if e % 2 else "w_e0a", a["w1"][e], a["w3"][e], a["w2"][e])
                else:
                    expert0(0, "w_e0a", a["sw1"], a["sw3"], a["sw2"])

            def expert1(slot, s, e):
                sp.dma_start(ew1[:, slot, 0, :], a["exp_wi"][e]).then_inc(S[s], 16)
                sp.dma_start(ew1[:, slot, 1, :].rearrange("p (m n) -> p m n", m=M1), half(a["exp_wo"][e])).then_inc(S[s], 16)

            sp.wait_ge(S["y_gated"], NG)
            for e in range(E):
                if e >= 2:
                    sp.wait_ge(S["down1"], NG * (e - 1))
                expert1(e % 2, "w_e1b" if e % 2 else "w_e1a", e)
            for g in range(NG):
                sp.wait_ge(S["res1"], NG * (E - 1) + g + 1)
                sp.dma_start(out.rearrange("b t d -> t b d")[:, gb(g), :], X[:, gb(g), :]).then_inc(S["out_sent"], 16)
            sp.wait_ge(S["out_sent"], 16 * NG)

        @block.gpsimd
        def _(pool):
            step = Chain(pool, S["pool_step"])
            gp = nc.gpsimd

            def rstd_of_ln(i):
                pool.wait_ge(S["ln_stats"], i + 1)
                gp.tensor_tensor(rstd[:], small[:, 0, :], mhalf[:], ALU.pow).then_inc(S["ln_rstd"], 1)

            gp.memset(mhalf[:], -0.5)
            step(gp.memset(ident[:], 0.0))
            step(gp.affine_select(out=ident[:], in_=ident[:], compare_op=ALU.not_equal, fill=1.0, base=0,
                                  pattern=[[-1, P]], channel_multiplier=1))
            gp.memset(ones[:], 1.0)
            step(gp.memset(sel[:], 0.0))
            for k in range(3):
                part = sel[32 * k:32 * k + 32, :, :]
                step(gp.affine_select(out=part, in_=part, compare_op=ALU.not_equal, fill=1.0, base=0,
                                      pattern=[[-1, 32], [0, P]], channel_multiplier=1))
            gp.memset(tri[:], 1.0)
            gp.memset(cw0[:], 1.0)
            step(gp.memset(hmask[:], 1.0))
            step(gp.affine_select(out=tri[:], in_=tri[:], compare_op=ALU.is_gt, fill=0.0, base=0,
                                  pattern=[[1, E], [-1, E]], channel_multiplier=0))
            for r in range(P // 32):
                part = hmask[32 * r:32 * r + 32, :]
                step(gp.affine_select(out=part, in_=part, compare_op=ALU.is_ge, fill=0.0, base=0,
                                      pattern=[[-DK, HQ]], channel_multiplier=1))
                step(gp.affine_select(out=part, in_=part, compare_op=ALU.is_ge, fill=0.0, base=DK - 1,
                                      pattern=[[DK, HQ]], channel_multiplier=-1))
            gp.memset(rstd[:], 0.0).then_inc(S["const"], 1)
            rstd_of_ln(0)
            for g in range(NG):
                pool.wait_ge(S["dl_done"], 2 * g + 2)
                for n in range(NS):
                    i, j = g * NS + n, n % 2
                    pool.wait_ge(S["b_copied"], i + 1)
                    if i >= 2:
                        pool.wait_ge(S["scanned"], i - 1)
                    gp.tensor_tensor(
                        dBu[:, j, :].rearrange("p (h n) -> p h n", h=HI), duT[:, :, gcols(g)],
                        Bsb[:, j:j + 1, :].broadcast_to([P, HI, GT]), ALU.mult).then_inc(S["drive"], 1)
            for i in range(1, NLN):
                rstd_of_ln(i)

        @block.scalar
        def _(act):
            sc = nc.scalar
            step = Chain(act, S["act_step"])

            def xnT_copy(i):
                for g in range(NG):
                    act.wait_ge(S["ln_tr"], i * NG + g + 1)
                    sc.copy(xnT[:, gcols(g)], bank(g)[:, 0, :]).then_inc(S["ln_xnT"], 1)

            act.wait_ge(S["w_mamba"], 16 * 8)
            step(sc.activation(negA[:].rearrange("p h n -> p (h n)"), w["A_log"][:].rearrange("p h n -> p (h n)"), ACT.Exp))
            step(sc.mul(negA[:].rearrange("p h n -> p (h n)"), negA[:].rearrange("p h n -> p (h n)"), -1.0))
            xnT_copy(0)
            for g in range(NG):
                for m in range(4):
                    act.wait_ge(S["in_mm"], 4 * g + m + 1)
                    dst = uT if m < HI else zT
                    sc.activation(dst[:, m % HI, gcols(g)], bank(4 + m)[:, 0, :], ACT.Silu).then_inc(S["in_silu"], 1)
            for g in range(NG):
                for m in range(HI):
                    act.wait_ge(S["dl_mm"], HI * g + m + 1)
                    sc.activation(tmpT[:, m, gcols(g)], bank(2 * (g % 2) + m)[:, 0, :], ACT.Abs,
                                  bias=w["b_delta"][:, m:m + 1]).then_inc(S["dl_abs"], 1)
            act.wait_ge(S["dl_abs"], HI * NG)
            step(sc.activation(tmpT[:], tmpT[:], ACT.Exp, scale=-1.0))
            sc.activation(tmpT[:], tmpT[:], ACT.Ln, bias=1.0).then_inc(S["dl_ln"], 1)
            for g in range(NG):
                act.wait_ge(S["dl_done"], 2 * g + 1)
                for n in range(NS):
                    i, j = g * NS + n, n % 2
                    if i >= 2:
                        act.wait_ge(S["scanned"], i - 1)
                    for m in range(HI):
                        sc.activation(
                            bank(2 * j + m)[:, 0, :].rearrange("p (b t) -> p b t", b=GB)[:, :, 1:T],
                            dT[:, m, gcols(g)].rearrange("p (b t) -> p b t", b=GB)[:, :, 1:T], ACT.Exp,
                            scale=negA[:, m, n:n + 1]).then_inc(S["decay"], 1)
                    act.wait_ge(S["b_bcast"], i + 1)
                    if i >= 2:
                        act.wait_ge(S["drive"], i - 1)
                    sc.copy(Bsb[:, j, :], bank(4)[:, 0, :]).then_inc(S["b_copied"], 1)
            xnT_copy(1)
            for g in range(NG):
                act.wait_ge(S["q_mm"], g + 1)
                sc.activation(qT[:, gcols(g)], bank(4 + g)[:, 0, :], ACT.Identity, bias=w["bq0"][:, 0:1]).then_inc(S["q_ev"], 1)
            for g in range(NG):
                act.wait_ge(S["v_mm"], g + 1)
                sc.copy(vS[0:LK, gb(g), :], bank(4 + g)[0:LK, 0, :].rearrange("p (b d) -> p b d", b=GB)).then_inc(S["v_ev"], 1)
            for g in range(NG):
                act.wait_ge(S["sc_max"], g + 1)
                for b in range(GB):
                    sc.activation(pr[:, g * GB + b, :], bank(g)[:, 0, b * LK:(b + 1) * LK], ACT.Exp,
                                  bias=small[:, 1, g * GB + b:g * GB + b + 1],
                                  accum_out=small[:, 2, g * GB + b:g * GB + b + 1]).then_inc(S["sc_exp"], 1)
            xnT_copy(2)
            act.wait_ge(S["rt_sub"], 1)
            sc.activation(router[:, 1, :, :], router[:, 0, :, :], ACT.Exp).then_inc(S["rt_exp"], 1)
            for i in range((E + 1) * NG):
                for m in range(M0):
                    k = M0 * i + m
                    act.wait_ge(S["up_mm"], k + 1)
                    if i >= 2:
                        act.wait_ge(S["hid0"], k + 1 - 2 * M0)
                    sc.activation(sh[:, i % 2, m * GT:(m + 1) * GT], bank(m)[:, 0, :], ACT.Silu).then_inc(S["silu0"], 1)
            xnT_copy(3)
            for g in range(NG):
                for m in range(4):
                    act.wait_ge(S["xz_mm"], 4 * g + m + 1)
                    dst = xi if m < HI else z1
                    sc.activation(dst[:, m % HI, gcols(g)], bank(4 + m)[:, 0, :], ACT.Copy if m < HI else ACT.Silu)\
                        .then_inc(S["xz_ev"], 1)
            for g in range(NG):
                for m in range(4):
                    act.wait_ge(S["lv_mm"], 4 * g + m + 1)
                    if m < HI:
                        sc.activation(lam[:, m, gcols(g)], bank(m)[:, 0, :], ACT.Sigmoid,
                                      bias=w["bl"][:, m:m + 1]).then_inc(S["lv_ev"], 1)
                    else:
                        sc.activation(vv[:, m - HI, gcols(g)], bank(m)[:, 0, :], ACT.Identity,
                                      bias=w["bv"][:, m - HI:m - HI + 1]).then_inc(S["lv_ev"], 1)
            step(sc.activation(coef[:, 1, :], w["omega"][:], ACT.Abs))
            step(sc.activation(coef[:, 1, :], coef[:, 1, :], ACT.Exp, scale=-1.0))
            sc.activation(coef[:, 1, :], coef[:, 1, :], ACT.Ln, bias=1.0).then_inc(S["omega_ln"], 1)
            act.wait_ge(S["coef_done"], 1)
            act.wait_ge(S["lv_ev"], 4 * NG)
            for m in range(HI):
                sc.activation(lam[:, m, :], lam[:, m, :], ACT.Exp, scale=coef[:, 2, m:m + 1]).then_inc(S["lam_done"], 1)
            xnT_copy(4)
            for g in range(NG):
                act.wait_ge(S["hq_mm"], g + 1)
                sc.activation(q1T[:, gcols(g)], bank(4 + g)[:, 0, :], ACT.Identity, bias=w["bq1"][:, 0:1]).then_inc(S["hq_ev"], 1)
            for g in range(NG):
                act.wait_ge(S["hv_mm"], g + 1)
                sc.copy(va[0:LK, gb(g), :, 0:DK],
                        bank(4 + g)[0:LK, 0, :].rearrange("p (b h d) -> p b h d", b=GB, h=NH)).then_inc(S["hv_ev"], 1)

            def head_out_copy(b):
                act.wait_ge(S["hoT_mm"], b + 1)
                if b >= 1:
                    act.wait_ge(S["hw_mm"], b)
                sc.copy(o1T, bank(7)[:, 0, 0:P]).then_inc(S["hoT_ev"], 1)

            for b in range(B):
                for q in range(2):
                    act.wait_ge(S["hs_sub"], 2 * b + q + 1)
                    if b >= 1:
                        act.wait_ge(S["ht_mm"], 2 * b - 1 + q)
                    sc.activation(e1[:, 8 * q:8 * q + 8, :], p1[:, 8 * q:8 * q + 8, :], ACT.Exp,
                                  scale=float(DK) ** -0.5).then_inc(S["hs_exp"], 1)
                for q in range(2):
                    act.wait_ge(S["ht_mm"], 2 * b + q + 1)
                    if b >= 1:
                        act.wait_ge(S["ho_mm"], b)
                    sc.copy(p1T[0:LK, 8 * q:8 * q + 8, :].rearrange("p (c h) q -> p c (h q)", c=2),
                            bank(4, 2)[0:LK, :, :]).then_inc(S["ht_ev"], 1)
                if b >= 1:
                    head_out_copy(b - 1)
            head_out_copy(B - 1)
            xnT_copy(5)

            def selu(i, slot, banks, lin_bias, exp_bias, mm_s, act_s):
                for m in range(M1):
                    act.wait_ge(S[mm_s], M1 * i + m + 1)
                    sc.activation(G[:, 0, slot, m * GT:(m + 1) * GT], banks[:, m, :], ACT.Exp, bias=exp_bias[m])
                    sc.activation(G[:, 1, slot, m * GT:(m + 1) * GT], banks[:, m, :], ACT.Relu, bias=lin_bias[m],
                                  scale=SELU_L).then_inc(S[act_s], 1)

            act.wait_ge(S["coef_sp"], 1)
            for g in range(NG):
                if g >= 2:
                    act.wait_ge(S["g_hid"], g - 1)
                selu(g, g % 2, bank(0, M1), [ebs[:, 0, m:m + 1] for m in range(M1)],
                     [w["gate_bi"][:, m:m + 1] for m in range(M1)], "gu_mm", "g_act")
            for i in range(E * NG):
                e = i // NG
                act.wait_ge(S["g_hid"], NG)
                if i >= 2:
                    act.wait_ge(S["hid1"], i - 1)
                selu(i, i % 2, bank(0, M1), [ebs[:, 1 + e, m:m + 1] for m in range(M1)],
                     [w["exp_bi"][:, e, m:m + 1] for m in range(M1)], "up1_mm", "act1")

        @block.vector
        def _(dve):
            v = nc.vector
            step = Chain(dve, S["dve_step"])

            def layer_norm(i):
                for b in range(B):
                    v.bn_stats(stats[:, b, :], X[:, b, :]) if b < B - 1 else step(v.bn_stats(stats[:, b, :], X[:, b, :]))
                for b in range(B):
                    v.bn_aggr(mv[:, b, :], stats[:, b, :]) if b < B - 1 else step(v.bn_aggr(mv[:, b, :], stats[:, b, :]))
                v.tensor_scalar(small[:, 0, :], mv[:, :, 1], EPS, None, ALU.add).then_inc(S["ln_stats"], 1)
                dve.wait_ge(S["ln_rstd"], i + 1)
                for b in range(B):
                    ins = v.tensor_scalar(xn[:, b, :], X[:, b, :], mv[:, b, 0:1], rstd[:, b:b + 1], ALU.subtract, ALU.mult)
                    if b % GB == GB - 1:
                        ins.then_inc(S["ln_xn"], 1)

            def choose(val, cw):
                vb = val.unsqueeze(3).broadcast_to([P, B, E, E])
                vo = val.unsqueeze(2).broadcast_to([P, B, E, E])
                step(v.tensor_tensor(pair[:, 0], vo, vb, ALU.is_equal))
                step(v.tensor_tensor(pair[:, 1], vo, vb, ALU.is_gt))
                tb = tri[:].unsqueeze(1).broadcast_to([P, B, E, E])
                step(v.tensor_tensor(pair[:, 0], pair[:, 0], tb, ALU.mult))
                step(v.tensor_tensor(pair[:, 0], pair[:, 0], pair[:, 1], ALU.add))
                step(v.tensor_reduce(router[:, 2], pair[:, 0], AX.X, ALU.add))
                step(v.tensor_scalar(router[:, 3], router[:, 2], 1.5, None, ALU.is_lt))
                step(v.tensor_tensor(router[:, 4], router[:, 3], val, ALU.mult))
                step(v.tensor_reduce(small[:, 3, :], router[:, 4], AX.X, ALU.add))
                step(v.reciprocal(small[:, 1, :], small[:, 3, :]))
                return v.tensor_tensor(cw, router[:, 4], small[:, 1, :].unsqueeze(2).broadcast_to([P, B, E]), ALU.mult)

            dve.wait_ge(S["x_in"], 16 * NG)
            dve.wait_ge(S["const"], 1)
            layer_norm(0)
            dve.wait_ge(S["w_mamba"], 16 * 8)
            for m in range(HI):
                v.tensor_scalar(diagD[:, m, :], ident[:], w["D_param"][:, m:m + 1], None, ALU.mult).then_inc(S["diag_ready"], 1)
            for g in range(NG):
                for m in range(HI):
                    dve.wait_ge(S["dl_abs"], HI * g + m + 1)
                    v.tensor_scalar(dT[:, m, gcols(g)], bank(2 * (g % 2) + m)[:, 0, :], w["b_delta"][:, m:m + 1], 0.0,
                                    ALU.add, ALU.max).then_inc(S["dl_relu"], 1)
            dve.wait_ge(S["bc_mm"], NG)
            psBC = bank(4, 4)[0:2 * NS].rearrange("p g n -> p (g n)")
            rem = yT[0:2 * NS, 0, :]
            mid = yT[0:2 * NS, 1, :].bitcast(BF16)[:, 0:N]
            step(v.tensor_copy(bc3[0:32, :], psBC))
            step(v.tensor_tensor(rem, psBC, bc3[0:32, :], ALU.subtract))
            step(v.tensor_copy(mid, rem))
            v.tensor_copy(bc3[32:64, :], mid)
            step(v.tensor_tensor(bc3[64:96, :], rem, mid, ALU.subtract))
            for j in range(4):
                ins = v.memset(bank(j)[:, 0, :].rearrange("p (b t) -> p b t", b=GB)[:, :, 0:1], 0.0)
            ins.then_inc(S["bc_split"], 1)
            dve.wait_ge(S["dl_ln"], 1)
            dve.wait_ge(S["dl_relu"], HI * NG)
            for g in range(NG):
                v.tensor_tensor(dT[:, :, gcols(g)], dT[:, :, gcols(g)], tmpT[:, :, gcols(g)], ALU.add).then_inc(S["dl_done"], 1)
                dve.wait_ge(S["dl_done"], 2 * g + 1)
                v.tensor_tensor(duT[:, :, gcols(g)], dT[:, :, gcols(g)], uT[:, :, gcols(g)], ALU.mult).then_inc(S["dl_done"], 1)
            for g in range(NG):
                for n in range(NS):
                    i, j = g * NS + n, n % 2
                    dve.wait_ge(S["decay"], HI * i + HI)
                    dve.wait_ge(S["drive"], i + 1)
                    v.tensor_tensor_scan(hst[:, j, :], bank(2 * j, 2).rearrange("p h n -> p (h n)"), dBu[:, j, :], 0.0,
                                         ALU.mult, ALU.add).then_inc(S["scanned"], 1)
                    dve.wait_ge(S["scanned"], i + 1)
                    dve.wait_ge(S["c_bcast"], i + 1)
                    if i >= 2:
                        dve.wait_ge(S["y_acc"], i - 1)
                    v.tensor_tensor(hC[:, j, :].rearrange("p (h n) -> p h n", h=HI),
                                    hst[:, j, :].rearrange("p (h n) -> p h n", h=HI),
                                    bank(5).broadcast_to([P, HI, GT]), ALU.mult).then_inc(S["hc"], 1)
                dve.wait_ge(S["y_acc"], (g + 1) * NS)
                v.tensor_tensor(yT[:, :, gcols(g)], bank(6, 2), zT[:, :, gcols(g)], ALU.mult).then_inc(S["y_gated"], 1)
            for g in range(NG):
                dve.wait_ge(S["a_out"], g + 1)
                v.tensor_tensor(X[:, gb(g), :], X[:, gb(g), :], bank(g)[:, 0, :].rearrange("p (b d) -> p b d", b=GB),
                                ALU.add).then_inc(S["a_res"], 1)
            dve.wait_ge(S["a_res"], NG)
            layer_norm(1)
            for g in range(NG):
                dve.wait_ge(S["k_mm"], g + 1)
                v.tensor_copy(kT[:, gb(g), :], bank(g)[:, 0, 0:GB * LK].rearrange("p (b k) -> p b k", b=GB)).then_inc(S["k_ev"], 1)
            for g in range(NG):
                dve.wait_ge(S["sc_mm"], g + 1)
                v.tensor_reduce(small[:, 1, gb(g)], bank(g)[:, 0, 0:GB * LK].rearrange("p (b k) -> p b k", b=GB), AX.X,
                                ALU.max, negate=True).then_inc(S["sc_max"], 1)
            for g in range(NG):
                dve.wait_ge(S["pt_mm"], g + 1)
                v.tensor_copy(prT[0:LK, gb(g), :], bank(4 + g)[0:LK, 0, :].rearrange("p (b q) -> p b q", b=GB)).then_inc(S["pt_ev"], 1)
            dve.wait_ge(S["sc_exp"], B)
            step(v.reciprocal(small[:, 3, :], small[:, 2, :]))
            for g in range(NG):
                dve.wait_ge(S["pv_mm"], g + 1)
                for b in range(GB):
                    bi = g * GB + b
                    v.scalar_tensor_tensor(X[:, bi, :], bank(g)[:, 0, b * D:(b + 1) * D], small[:, 3, bi:bi + 1], X[:, bi, :],
                                           ALU.mult, ALU.add).then_inc(S["pv_res"], 1)
            dve.wait_ge(S["pv_res"], B)
            layer_norm(2)
            dve.wait_ge(S["rt_mm"], 1)
            lg = bank(7)[:, 0, 0:B * E].rearrange("p (b e) -> p b e", b=B)
            step(v.tensor_reduce(small[:, 1, :], lg, AX.X, ALU.max))
            v.tensor_tensor(router[:, 0], lg, small[:, 1, :].unsqueeze(2).broadcast_to([P, B, E]), ALU.subtract).then_inc(S["rt_sub"], 1)
            dve.wait_ge(S["rt_exp"], 1)
            choose(router[:, 1], cw0[:, :, 0:E]).then_inc(S["rt_cw"], 1)
            dve.wait_ge(S["rt_cw"], 1)

            def add_expert(i, cw, e, dn, rs):
                g = i % NG
                dve.wait_ge(S[dn], i + 1)
                for b in range(GB):
                    bi = g * GB + b
                    ins = v.scalar_tensor_tensor(X[:, bi, :], bank(4 + i % 2)[:, 0, b * D:(b + 1) * D], cw[:, bi, e:e + 1],
                                                 X[:, bi, :], ALU.mult, ALU.add)
                ins.then_inc(S[rs], 1)

            for i in range((E + 1) * NG + 1):
                if i < (E + 1) * NG:
                    if i >= 2:
                        dve.wait_ge(S["down0"], i - 1)
                    for m in range(M0):
                        dve.wait_ge(S["silu0"], M0 * i + m + 1)
                        v.tensor_tensor(hidr[:, i % 2, m * GT:(m + 1) * GT], sh[:, i % 2, m * GT:(m + 1) * GT],
                                        bank(2 + m)[:, 0, :], ALU.mult).then_inc(S["hid0"], 1)
                if i >= 1:
                    if i > NG:
                        dve.wait_ge(S["res0"], i - NG)
                    add_expert(i - 1, cw0, (i - 1) // NG, "down0", "res0")
            dve.wait_ge(S["res0"], (E + 1) * NG)
            layer_norm(3)
            step(v.tensor_scalar(coef[:, 0, :], w["omega"][:], 0.0, None, ALU.max))
            dve.wait_ge(S["omega_ln"], 1)
            step(v.tensor_tensor(coef[:, 3, :], coef[:, 0, :], coef[:, 1, :], ALU.add))
            v.tensor_scalar(coef[:, 2, :], coef[:, 3, :], -8.0, None, ALU.mult).then_inc(S["coef_done"], 1)
            dve.wait_ge(S["lv_ev"], 4 * NG)
            for m in range(HI):
                v.tensor_tensor(sq[:, m, :], vv[:, m, :], vv[:, m, :], ALU.mult).then_inc(S["sq_done"], 1)
            for m in range(HI):
                dve.wait_ge(S["lam_done"], m + 1)
                step(v.tensor_scalar(bb[:, m, :], lam[:, m, :], -1.0, 1.0, ALU.mult, ALU.add))
                step(v.tensor_tensor(bb[:, m, :], bb[:, m, :], xi[:, m, :], ALU.mult))
            for g in range(NG):
                dve.wait_ge(S["vv_mm"], g + 1)
                dve.wait_ge(S["vv_mm"], NG)
                step(v.reciprocal(LN[:, 0, gcols(g)], bank(g)[:, 0, :]))
                step(v.scalar_tensor_tensor(ww[:, :, gcols(g)], vv[:, :, gcols(g)], -2.0,
                                            LN[:, 0:1, gcols(g)].broadcast_to([P, HI, GT]), ALU.mult, ALU.mult))
                step(v.tensor_tensor(ww[:, :, gcols(g)], ww[:, :, gcols(g)], lam[:, :, gcols(g)], ALU.mult))
            at = lambda buf, t: buf.rearrange("p h (b t) -> p h b t", b=B)[:, :, :, bass.ds(t, 1)].rearrange("p h b o -> p h (b o)")
            pdot = bank(4)[:, :, 0:B].broadcast_to([P, HI, B])
            n0 = step.n
            with dve.Fori(1, T) as t:
                k = t * 5
                v.tensor_tensor(mrec[:], at(vv, t), at(xi, t - 1), ALU.mult).then_inc(S["r_prod"], 1)
                v.tensor_tensor(prec[:], at(lam, t), at(xi, t - 1), ALU.mult).then_inc(S["r_h"], 1)
                dve.wait_ge(S["r_h"], t * 4 - 3)
                v.tensor_tensor(prec[:], prec[:], at(bb, t), ALU.add).then_inc(S["r_h"], 1)
                dve.wait_ge(S["r_dot"], t)
                v.tensor_tensor(rrec[:], at(ww, t), pdot, ALU.mult).then_inc(S["r_h"], 1)
                dve.wait_ge(S["r_h"], t * 4 - 1)
                v.tensor_tensor(at(xi, t), rrec[:], prec[:], ALU.add).then_inc(S["r_h"], 1)
                dve.wait_ge(S["r_h"], t * 4)
            for g in range(NG):
                v.tensor_tensor(bb[:, :, gcols(g)], xi[:, :, gcols(g)], z1[:, :, gcols(g)], ALU.mult).then_inc(S["g1_ready"], 1)
            for g in range(NG):
                dve.wait_ge(S["d_out"], g + 1)
                v.tensor_tensor(X[:, gb(g), :], X[:, gb(g), :], bank(g)[:, 0, :].rearrange("p (b d) -> p b d", b=GB),
                                ALU.add).then_inc(S["d_res"], 1)
            dve.wait_ge(S["d_res"], NG)
            layer_norm(4)
            for g in range(NG):
                dve.wait_ge(S["hk_mm"], g + 1)
                v.tensor_copy(k1T[:, gb(g), :], bank(g)[:, 0, 0:GB * LK].rearrange("p (b k) -> p b k", b=GB)).then_inc(S["hk_ev"], 1)
            dve.wait_ge(S["hk_ev"], NG)
            v.memset(va[0:LK, :, :, DK:DK + 1], 1.0).then_inc(S["hk_ev"], 1)
            for j in range(HQ):
                v.tensor_scalar(kb[:, :, j, :], k1T[:], hmask[:, j:j + 1], None, ALU.mult).then_inc(S["hk_ev"], 1)
            for b in range(B + 2):
                if b < B:
                    for q in range(2):
                        hh = slice(8 * q, 8 * q + 8)
                        dve.wait_ge(S["hs_mm"], 2 * b + q + 1)
                        sc2 = bank(2 * q, 2)[:, :, 0:HQ * LK].rearrange("p g (j k) -> p g j k", j=HQ)
                        step(v.tensor_reduce(small[:, 1, hh].rearrange("p (g j) -> p g j", j=HQ), sc2, AX.X, ALU.max))
                        if b >= 1:
                            dve.wait_ge(S["hs_exp"], 2 * b - 1 + q)
                        for r in range(2):
                            h4 = slice(8 * q + HQ * r, 8 * q + HQ * r + HQ)
                            ins = v.tensor_tensor(p1[:, h4, :], sc2[:, r],
                                                  small[:, 1, h4].unsqueeze(2).broadcast_to([P, HQ, LK]), ALU.subtract)
                        ins.then_inc(S["hs_sub"], 1)
                if 1 <= b <= B:
                    dve.wait_ge(S["ho_mm"], b)
                    po = bank(6)[:, 0, 0:NH * (DK + 1)].rearrange("p (h d) -> p h d", h=NH)
                    step(v.reciprocal(o1r, po[:, :, DK]))
                    if b >= 2:
                        dve.wait_ge(S["hoT_mm"], b - 1)
                    v.tensor_tensor(o1.rearrange("p (h d) -> p h d", h=NH), po[:, :, 0:DK],
                                    o1r.unsqueeze(2).broadcast_to([P, NH, DK]), ALU.mult).then_inc(S["ho_norm"], 1)
                if b >= 2:
                    c = b - 2
                    dve.wait_ge(S["hw_mm"], c + 1)
                    v.tensor_tensor(X[:, c, :], X[:, c, :], bank(7)[:, 0, P:2 * P], ALU.add).then_inc(S["hw_res"], 1)
            dve.wait_ge(S["hw_res"], B)
            layer_norm(5)
            dve.wait_ge(S["w_gate"], 16 * 6)
            v.tensor_scalar(ebs[:, 0, :], w["gate_bi"][:], SELU_L, None, ALU.mult)
            v.tensor_scalar(ebs[:, 1:, :], w["exp_bi"][:], SELU_L, None, ALU.mult).then_inc(S["coef_sp"], 1)

            def selu_sum(i, slot, a_s, h_s):
                dve.wait_ge(S[a_s], M1 * (i + 1))
                step(v.tensor_scalar(G[:, 0, slot, :], G[:, 0, slot, :], 1.0, 1.0, ALU.min, ALU.subtract))
                v.scalar_tensor_tensor(G[:, 2, slot, :], G[:, 0, slot, :], SELU_LA, G[:, 1, slot, :], ALU.mult,
                                       ALU.add).then_inc(S[h_s], 1)

            for g in range(NG):
                if g >= 2:
                    dve.wait_ge(S["gl_mm"], g - 1)
                selu_sum(g, g % 2, "g_act", "g_hid")
            for g in range(NG):
                dve.wait_ge(S["gl_mm"], g + 1)
                step(v.tensor_copy(gl[:, gb(g), :], bank(4 + g)[:, 0, :].rearrange("p (b d) -> p b d", b=GB)))
            for b in range(B):
                ins = v.max(top[:, b, :], gl[:, b, :])
            step(ins)
            le = gl[:, :, 0:E]
            step(v.tensor_tensor(pair[:, 0], le.unsqueeze(2).broadcast_to([P, B, E, E]),
                                 le.unsqueeze(3).broadcast_to([P, B, E, E]), ALU.is_equal))
            step(v.tensor_tensor(pair[:, 0], pair[:, 0], tri[:].unsqueeze(1).broadcast_to([P, B, E, E]), ALU.mult))
            step(v.tensor_reduce(router[:, 2], pair[:, 0], AX.X, ALU.add))
            for k in range(2):
                step(v.tensor_tensor(router[:, 3], top[:, :, k:k + 1].broadcast_to([P, B, E]), le, ALU.is_gt))
                step(v.tensor_tensor(router[:, 2], router[:, 2], router[:, 3], ALU.add))
            step(v.tensor_scalar(router[:, 3], router[:, 2], 1.5, None, ALU.is_lt))
            step(v.tensor_tensor(router[:, 4], router[:, 3], le, ALU.mult))
            step(v.tensor_tensor(small[:, 3, :], top[:, :, 0], top[:, :, 1], ALU.add))
            step(v.reciprocal(small[:, 1, :], small[:, 3, :]))
            v.tensor_tensor(cw1[:], router[:, 4], small[:, 1, :].unsqueeze(2).broadcast_to([P, B, E]), ALU.mult).then_inc(S["gl_cw"], 1)
            dve.wait_ge(S["gl_cw"], 1)
            for g in range(NG):
                dve.wait_ge(S["wt_mm"], g + 1)
                v.tensor_copy(cwT[:, gb(g), :], bank(4 + g % 2)[0:E, 0, :].rearrange("p (b t) -> p b t", b=GB)).then_inc(S["wt_ev"], 1)
                dve.wait_ge(S["eb_mm"], g + 1)
                v.tensor_tensor(X[:, gb(g), :], X[:, gb(g), :], bank(6 + g % 2)[:, 0, :].rearrange("p (b d) -> p b d", b=GB),
                                ALU.add).then_inc(S["eb_res"], 1)
            dve.wait_ge(S["eb_res"], NG)
            for i in range(E * NG + 1):
                if i < E * NG:
                    if i >= 2:
                        dve.wait_ge(S["down1"], i - 1)
                    selu_sum(i, i % 2, "act1", "hid1")
                if i >= 1:
                    if i > NG:
                        dve.wait_ge(S["res1"], i - NG)
                    add_expert(i - 1, cw1, (i - 1) // NG, "down1", "res1")

        @block.tensor
        def _(pe):
            mm = nc.tensor.matmul

            def transpose_xn(i):
                for g in range(NG):
                    pe.wait_ge(S["ln_xn"], i * NG + g + 1)
                    for b in range(GB):
                        ins = nc.tensor.transpose(bank(g)[:, 0, b * T:(b + 1) * T], xn[:, g * GB + b, :], ident[:])
                    ins.then_inc(S["ln_tr"], 1)

            def down(i, ks, lhs, rhs, o, width=D):
                for b in range(GB):
                    for k in range(ks):
                        ins = mm(bank(o)[:, 0, b * width:(b + 1) * width], lhs(k, b), rhs(k), start=k == 0, stop=k == ks - 1)
                return ins

            pe.wait_ge(S["const"], 1)
            transpose_xn(0)
            pe.wait_ge(S["w_mamba"], 16 * 8)
            for g in range(NG):
                pe.wait_ge(S["ln_xnT"], g + 1)
                for m in range(4):
                    if g:
                        pe.wait_ge(S["in_silu"], 4 * g - 3 + m)
                    mm(bank(4 + m)[:, 0, :], w["W_in"][:, m, :], xnT[:, gcols(g)], start=True, stop=True).then_inc(S["in_mm"], 1)
            pe.wait_ge(S["ln_xnT"], NG)
            for g in range(NG):
                pe.wait_ge(S["in_silu"], 4 * g + 4)
                for m in range(HI):
                    if g >= 2:
                        pe.wait_ge(S["dl_abs"], HI * (g - 2) + m + 1)
                        pe.wait_ge(S["dl_relu"], HI * (g - 2) + m + 1)
                    for k in range(HI):
                        ins = mm(bank(2 * (g % 2) + m)[:, 0, :], w["W_delta"][:, k, m * P:(m + 1) * P], uT[:, k, gcols(g)],
                                 start=k == 0, stop=k == HI - 1)
                    ins.then_inc(S["dl_mm"], 1)
            for g in range(NG):
                for k in range(HI):
                    ins = mm(bank(4 + g)[0:2 * NS, 0, :], w["W_BC"][:, k, :], uT[:, k, gcols(g)], start=k == 0, stop=k == HI - 1)
                ins.then_inc(S["bc_mm"], 1)
            pe.wait_ge(S["bc_split"], 1)
            pe.wait_ge(S["diag_ready"], HI)
            def broadcast(bank_i, r, g, s):
                mm(bank(bank_i)[:, 0, :], sel[:, r, :], bc3[:, gcols(g)],
                   start=True, stop=True).then_inc(S[s], 1)

            def b_ahead(n, g, i):
                pe.wait_ge(S["b_copied"], i + 2)
                broadcast(4, n, g, "b_bcast")

            def c_row(n, g, i):
                pe.wait_ge(S["hc"], i)
                broadcast(5, n + NS, g, "c_bcast")

            def y_sum(i, j, last=False):
                pe.wait_ge(S["hc"], i + 1)
                for m in range(HI):
                    ins = mm(bank(6 + m)[:, 0, :], ident[:], hC[:, j, m * GT:(m + 1) * GT], start=False, stop=last,
                             skip_group_check=True)
                ins.then_inc(S["y_acc"], 1)

            broadcast(4, 0, 0, "b_bcast")
            pe.wait_ge(S["b_copied"], 1)
            broadcast(4, 1, 0, "b_bcast")
            for g in range(NG):
                i0 = g * NS
                c_row(0, g, i0) if g else broadcast(5, NS, 0, "c_bcast")
                b_ahead(2, g, i0)
                if g:
                    pe.wait_ge(S["y_gated"], g)
                for m in range(HI):
                    mm(bank(6 + m)[:, 0, :], diagD[:, m, :], uT[:, m, gcols(g)], start=True, stop=False, skip_group_check=True)
                for n in range(1, NS):
                    c_row(n, g, i0 + n)
                    if n + 2 < NS:
                        b_ahead(n + 2, g, i0 + n)
                    elif g < NG - 1:
                        b_ahead(n + 2 - NS, g + 1, i0 + n)
                    y_sum(i0 + n - 1, (n - 1) % 2)
                y_sum(i0 + NS - 1, 1, last=True)
            for g in range(NG):
                pe.wait_ge(S["y_gated"], NG)
                down(g, HI, lambda k, b: yT[:, k, (g * GB + b) * T:(g * GB + b + 1) * T], lambda k: w["W_out"][:, k, :], g)\
                    .then_inc(S["a_out"], 1)
            transpose_xn(1)
            pe.wait_ge(S["w_ctx"], 16 * 6)
            for g in range(NG):
                pe.wait_ge(S["ln_xnT"], NG + g + 1)
                mm(bank(4 + g)[:, 0, :], w["Wq0"][:], xnT[:, gcols(g)], start=True, stop=True).then_inc(S["q_mm"], 1)
            for g in range(NG):
                mm(bank(g)[:, 0, 0:GB * LK], w["Wk0"][:], w["ctxT"][:, gb(g), :].rearrange("p b k -> p (b k)"),
                   start=True, stop=True).then_inc(S["k_mm"], 1)
            for g in range(NG):
                pe.wait_ge(S["q_ev"], g + 1)
                for b in range(GB):
                    ins = mm(bank(4 + g)[0:LK, 0, b * D:(b + 1) * D], w["ctxT"][:, g * GB + b, :], w["Wv0"][:], start=True, stop=True)
                ins.then_inc(S["v_mm"], 1)
            for g in range(NG):
                pe.wait_ge(S["k_ev"], g + 1)
                for b in range(GB):
                    bi = g * GB + b
                    ins = mm(bank(g)[:, 0, b * LK:(b + 1) * LK], qT[:, bi * T:(bi + 1) * T], kT[:, bi, :], start=True, stop=True)
                ins.then_inc(S["sc_mm"], 1)
            for g in range(NG):
                pe.wait_ge(S["sc_exp"], GB * (g + 1))
                pe.wait_ge(S["v_ev"], g + 1)
                for b in range(GB):
                    ins = nc.tensor.transpose(bank(4 + g)[0:LK, 0, b * T:(b + 1) * T], pr[:, g * GB + b, :], ident[:])
                ins.then_inc(S["pt_mm"], 1)
            for g in range(NG):
                pe.wait_ge(S["pt_ev"], g + 1)
                for b in range(GB):
                    ins = mm(bank(g)[:, 0, b * D:(b + 1) * D], prT[0:LK, g * GB + b, :], vS[0:LK, g * GB + b, :], start=True, stop=True)
                ins.then_inc(S["pv_mm"], 1)
            transpose_xn(2)
            for g in range(NG):
                pe.wait_ge(S["ln_xnT"], 2 * NG + g + 1)
                for b in range(g * GB, (g + 1) * GB):
                    ins = mm(bank(7)[:, 0, b * E:(b + 1) * E], xnT[:, b * T:(b + 1) * T], w["router0"][:], start=True, stop=True)
            ins.then_inc(S["rt_mm"], 1)
            for i in range((E + 1) * NG + 1):
                e, g = divmod(i, NG)
                if i < (E + 1) * NG:
                    if g == 0:
                        pe.wait_ge(S["w_e0b" if e % 2 else "w_e0a"], 48 * (e // 2 + 1))
                    for m in range(M0):
                        if i:
                            pe.wait_ge(S["silu0"], M0 * (i - 1) + m + 1)
                        mm(bank(m)[:, 0, :], ew0[:, e % 2, 0, m * P:(m + 1) * P], xnT[:, gcols(g)], start=True, stop=True)
                        if i:
                            pe.wait_ge(S["hid0"], M0 * (i - 1) + m + 1)
                        mm(bank(2 + m)[:, 0, :], ew0[:, e % 2, 1, m * P:(m + 1) * P], xnT[:, gcols(g)], start=True, stop=True)\
                            .then_inc(S["up_mm"], 1)
                if i >= 1:
                    c = i - 1
                    pe.wait_ge(S["hid0"], M0 * (c + 1))
                    if c >= 2:
                        pe.wait_ge(S["res0"], c - 1)
                    sl = (c // NG) % 2
                    down(c, M0, lambda k, b: hidr[:, c % 2, k * GT + b * T:k * GT + (b + 1) * T],
                         lambda k: ew0[:, sl, 2, k * D:(k + 1) * D], 4 + c % 2).then_inc(S["down0"], 1)
            transpose_xn(3)
            pe.wait_ge(S["w_lru"], 16 * 6)
            for g in range(NG):
                pe.wait_ge(S["ln_xnT"], 3 * NG + g + 1)
                for m in range(4):
                    if g:
                        pe.wait_ge(S["xz_ev"], 4 * g - 3 + m)
                    mm(bank(4 + m)[:, 0, :], w["Win1"][:, m, :], xnT[:, gcols(g)], start=True, stop=True).then_inc(S["xz_mm"], 1)
            for g in range(NG):
                pe.wait_ge(S["xz_ev"], 4 * g + 4)
                for m in range(4):
                    if g:
                        pe.wait_ge(S["lv_ev"], 4 * g - 3 + m)
                    wt = w["Wl"] if m < HI else w["Wv"]
                    for k in range(HI):
                        ins = mm(bank(m)[:, 0, :], wt[:, k, (m % HI) * P:(m % HI + 1) * P], xi[:, k, gcols(g)],
                                 start=k == 0, stop=k == HI - 1)
                    ins.then_inc(S["lv_mm"], 1)
            pe.wait_ge(S["sq_done"], HI)
            for g in range(NG):
                for k in range(HI):
                    ins = mm(bank(g)[:, 0, :], ones[:], sq[:, k, gcols(g)], start=k == 0, stop=k == HI - 1)
                ins.then_inc(S["vv_mm"], 1)
            with pe.Fori(1, T) as t:
                pe.wait_ge(S["r_prod"], t)
                mm(bank(4)[:, 0, 0:B], ones[:], mrec[:, 0, :], start=True, stop=False)
                mm(bank(4)[:, 0, 0:B], ones[:], mrec[:, 1, :], start=False, stop=True).then_inc(S["r_dot"], 1)
            for g in range(NG):
                pe.wait_ge(S["g1_ready"], g + 1)
                down(g, HI, lambda k, b: bb[:, k, (g * GB + b) * T:(g * GB + b + 1) * T], lambda k: w["Wout1"][:, k, :], g)\
                    .then_inc(S["d_out"], 1)
            transpose_xn(4)
            pe.wait_ge(S["w_att"], 16 * 6)
            for g in range(NG):
                pe.wait_ge(S["ln_xnT"], 4 * NG + g + 1)
                mm(bank(4 + g)[:, 0, :], w["Wq1"][:], xnT[:, gcols(g)], start=True, stop=True).then_inc(S["hq_mm"], 1)
            for g in range(NG):
                mm(bank(g)[:, 0, 0:GB * LK], w["Wk1"][:], w["ctxT"][:, gb(g), :].rearrange("p b k -> p (b k)"),
                   start=True, stop=True).then_inc(S["hk_mm"], 1)
            for g in range(NG):
                pe.wait_ge(S["hq_ev"], g + 1)
                for b in range(GB):
                    ins = mm(bank(4 + g)[0:LK, 0, b * D:(b + 1) * D], w["ctxT"][:, g * GB + b, :], w["Wv1"][:], start=True, stop=True)
                ins.then_inc(S["hv_mm"], 1)

            def head_scores(b, q):
                for r in range(2 * q, 2 * q + 2):
                    rows = slice(32 * r, 32 * r + 32)
                    ins = mm(bank(r)[:, 0, 0:HQ * LK], q1T[rows, b * T:(b + 1) * T],
                             kb[rows, b, :, :].rearrange("p j k -> p (j k)"), start=True, stop=True)
                ins.then_inc(S["hs_mm"], 1)

            def head_out_transpose(b):
                pe.wait_ge(S["ho_norm"], b + 1)
                if b:
                    pe.wait_ge(S["hw_res"], b)
                nc.tensor.transpose(bank(7)[:, 0, 0:P], o1, ident[:]).then_inc(S["hoT_mm"], 1)

            def head_out(b):
                pe.wait_ge(S["hoT_ev"], b + 1)
                mm(bank(7)[:, 0, P:2 * P], o1T, w["Wo1"][:], start=True, stop=False)
                mm(bank(7)[:, 0, P:2 * P], ones[0:1, :], w["bo1"][:], start=False, stop=True).then_inc(S["hw_mm"], 1)

            pe.wait_ge(S["hk_ev"], NG + 1 + HQ)
            head_scores(0, 0)
            head_scores(0, 1)
            for b in range(B):
                if b == 0:
                    pe.wait_ge(S["hv_ev"], NG)
                for q in range(2):
                    if b < B - 1:
                        pe.wait_ge(S["hs_sub"], 2 * b + q + 1)
                        head_scores(b + 1, q)
                    pe.wait_ge(S["hs_exp"], 2 * b + q + 1)
                    if 2 * b + q:
                        pe.wait_ge(S["ht_ev"], 2 * b + q)
                    for h in range(8):
                        ins = nc.tensor.transpose(bank(4 + h // 4)[0:LK, 0, (h % 4) * T:(h % 4 + 1) * T], e1[:, 8 * q + h, :], ident[:])
                    ins.then_inc(S["ht_mm"], 1)
                if b:
                    head_out_transpose(b - 1)
                pe.wait_ge(S["ht_ev"], 2 * b + 2)
                for h in range(NH):
                    ins = mm(bank(6)[:, 0, h * (DK + 1):(h + 1) * (DK + 1)], p1T[0:LK, h, :], va[0:LK, b, h, :], start=True, stop=True)
                ins.then_inc(S["ho_mm"], 1)
                if b:
                    head_out(b - 1)
            head_out_transpose(B - 1)
            head_out(B - 1)
            transpose_xn(5)
            pe.wait_ge(S["w_gate"], 16 * 6)

            def logits(g):
                pe.wait_ge(S["g_hid"], g + 1)
                for b in range(GB):
                    o = bank(4 + g)[:, 0, b * D:(b + 1) * D]
                    for m in range(M1):
                        mm(o, G[:, 2, g % 2, m * GT + b * T:m * GT + (b + 1) * T], w["gate_wo"][:, m, :], start=m == 0, stop=False)
                    ins = mm(o, ones[0:1, :], w["gate_bo"][:], start=False, stop=True)
                ins.then_inc(S["gl_mm"], 1)

            for g in range(NG):
                pe.wait_ge(S["ln_xnT"], 5 * NG + (g + 1 if g else NG))
                for m in range(M1):
                    if g:
                        pe.wait_ge(S["g_act"], M1 * (g - 1) + m + 1)
                    mm(bank(m)[:, 0, :], w["gate_wi"][:, m, :], xnT[:, gcols(g)], start=True, stop=True).then_inc(S["gu_mm"], 1)
                if g:
                    logits(g - 1)
            logits(NG - 1)
            pe.wait_ge(S["gl_cw"], 1)
            for g in range(NG):
                if g >= 2:
                    pe.wait_ge(S["wt_ev"], g - 1)
                for b in range(GB):
                    ins = nc.tensor.transpose(bank(4 + g % 2)[0:E, 0, b * T:(b + 1) * T], cw1[:, g * GB + b, :], ident[:])
                ins.then_inc(S["wt_mm"], 1)
                pe.wait_ge(S["wt_ev"], g + 1)
                if g >= 2:
                    pe.wait_ge(S["eb_res"], g - 1)
                for b in range(GB):
                    ins = mm(bank(6 + g % 2)[:, 0, b * D:(b + 1) * D], cwT[:, g * GB + b, :], w["exp_bo"][:], start=True, stop=True)
                ins.then_inc(S["eb_mm"], 1)
            for i in range(E * NG + 1):
                e, g = divmod(i, NG)
                if i < E * NG:
                    if g == 0:
                        pe.wait_ge(S["w_e1b" if e % 2 else "w_e1a"], 32 * (e // 2 + 1))
                    for m in range(M1):
                        if i:
                            pe.wait_ge(S["act1"], M1 * (i - 1) + m + 1)
                        else:
                            pe.wait_ge(S["g_act"], M1 * NG)
                        mm(bank(m)[:, 0, :], ew1[:, e % 2, 0, m * P:(m + 1) * P], xnT[:, gcols(g)], start=True, stop=True)\
                            .then_inc(S["up1_mm"], 1)
                if i >= 1:
                    c = i - 1
                    pe.wait_ge(S["hid1"], c + 1)
                    if c >= 2:
                        pe.wait_ge(S["res1"], c - 1)
                    sl = (c // NG) % 2
                    down(c, M1, lambda k, b: G[:, 2, c % 2, k * GT + b * T:k * GT + (b + 1) * T],
                         lambda k: ew1[:, sl, 1, k * D:(k + 1) * D], 4 + c % 2).then_inc(S["down1"], 1)


def kernel(**inputs):
    import numpy as _np
    import concourse.bacc as _bacc
    from concourse import mybir as _mybir
    from concourse.bass_utils import run_bass_kernel_spmd as _run

    I = {k: _np.asarray(v) for k, v in inputs.items()}
    ctx = _np.ones((DC + 1, B, LK), _np.float32)
    ctx[0:DC] = I["ctx_512"].transpose(2, 0, 1)
    lay = {"x": I["x"], "ctxT": ctx}
    for name in ("W_in", "W_delta", "b_delta", "A_log", "D_param", "W_out"):
        lay[name] = I["L0_attn_" + name]
    lay["W_BC"] = _np.concatenate([I["L0_attn_W_B"], I["L0_attn_W_C"]], 1)
    for l, x in ((0, "L0_xattn_"), (1, "L1_xattn_")):
        lay[f"Wq{l}"], lay[f"bq{l}"] = I[x + "Wq"], I[x + "bq"]
        lay[f"Wk{l}"] = _np.concatenate([I[x + "Wk"], I[x + "bk"][None]], 0)
        lay[f"Wv{l}"] = _np.concatenate([I[x + "Wv"], I[x + "bv"][None]], 0)
    lay["Wo1"], lay["bo1"] = I["L1_xattn_Wo"], I["L1_xattn_bo"]
    lay["router0"] = I["L0_ffn_w_router"]
    for name in ("w1", "w3", "w2", "sw1", "sw3", "sw2"):
        lay[name] = I["L0_ffn_" + name]
    lay["omega"] = I["L1_attn_omega"].reshape(DI)
    lay["bl"], lay["bv"] = I["L1_attn_bl"], I["L1_attn_bv"]
    for name, src in (("Win1", "Win"), ("Wl", "Wl"), ("Wv", "Wv"), ("Wout1", "Wout")):
        lay[name] = I["L1_attn_" + src].T
    for name in ("gate_wi", "gate_bi", "gate_wo", "gate_bo", "exp_wi", "exp_wo", "exp_bo"):
        lay[name] = I["L1_ffn_" + name]
    lay["exp_bi"] = I["L1_ffn_exp_bi"].reshape(E, M1, P).transpose(2, 0, 1)

    for name in ("b_delta", "D_param", "omega", "bl", "bv", "bq0", "bq1", "gate_bi"):
        lay[name] = lay[name].reshape(-1, P).T

    nc = _bacc.Bacc("TRN2", target_bir_lowering=False, num_devices=1)
    arrays, args = {}, {}
    for name, v in lay.items():
        v = _np.ascontiguousarray(v)
        arrays[f"in_{name}_dram"] = v
        args[name] = nc.dram_tensor(f"in_{name}_dram", v.shape, _mybir.dt.from_np(v.dtype), kind="ExternalInput").ap()
    res = nc.dram_tensor("out_0_dram", (B, T, D), F32, kind="ExternalOutput").ap()
    decoder_program(nc, args, res)
    r = _run(nc, [arrays], core_ids=[0])
    return r.results[0]["out_0_dram"]
```

```python
import numpy as np
import concourse.bass as bass
from concourse import mybir
from contextlib import ExitStack

F32 = mybir.dt.float32
BF16 = mybir.dt.bfloat16
F32R = mybir.dt.float32r
ALU = mybir.AluOpType
ACT = mybir.ActivationFunctionType
AX = mybir.AxisListType

P = 128
B, T, D = 16, 128, 128
N = B * T
GB = 4
NG = B // GB
GT = GB * T
DI = 256
HI = DI // P
NS = 16
LK, DC = 120, 64
E = 8
H0 = 256
M0 = H0 // P
H1 = 512
M1 = H1 // P
NH, DK = 16, 8
HQ = 4
EPS = 1e-5
SELU_L = 1.0507009873554805
SELU_A = 1.6732632423543772
SELU_LA = SELU_L * SELU_A
NLN = 6
UR = 8


def decoder_program(nc, a, out):
    with ExitStack() as ctx:
        def sb(name, shape, dt=F32):
            return ctx.enter_context(nc.sbuf_tensor(name, shape, dt))

        def sem(name):
            return ctx.enter_context(nc.semaphore(name))

        ps = ctx.enter_context(nc.psum_tensor("ps", [P, 8, GT], F32))
        X = sb("X", [P, B, D])
        LN = sb("LN", [P, 2, N])
        xn = LN[:, 0, :].rearrange("p (b d) -> p b d", b=B)
        xnT = LN[:, 1, :]
        stats = sb("stats", [P, B, 6])
        mv = sb("mv", [P, B, 2])
        rstd = sb("rstd", [P, B])
        mhalf = sb("mhalf", [P, B])
        ident = sb("ident", [P, P])
        ones = sb("ones", [P, P])
        sel = sb("sel", [3 * 32, 32, P], BF16)
        bc3 = sb("bc3", [3 * 32, N], BF16)
        hmask = sb("hmask", [P, HQ])
        tri = sb("tri", [P, E, E])
        negA = sb("negA", [P, HI, NS])
        diagD = sb("diagD", [P, HI, P])
        router = sb("router", [P, 6, B, E])
        cw0 = sb("cw0", [P, B, E + 1])
        cw1 = sb("cw1", [P, B, E])
        small = sb("small", [P, 4, B])
        coef = sb("coef", [P, 4, HI])
        ebs = sb("ebs", [P, E + 1, M1])
        nones = diagD[:, 0, :]
        lm = sb("lm", [P, 2, 2, HI, B])
        grec = sb("grec", [P, 2, HI, B])
        rrec = sb("rrec", [P, HI, B])
        sdot = sb("sdot", [P, B])
        acc = sb("acc", [P, B])

        w = {}
        for name, shape in (
            ("W_in", [P, 4, P]), ("W_delta", [P, HI, DI]), ("b_delta", [P, HI]), ("W_BC", [P, HI, 2 * NS]),
            ("A_log", [P, HI, NS]), ("D_param", [P, HI]), ("W_out", [P, HI, D]),
            ("Wq0", [P, P]), ("bq0", [P, 1]), ("Wk0", [DC + 1, P]), ("Wv0", [DC + 1, P]), ("ctxT", [DC + 1, B, LK]),
            ("router0", [P, E]),
            ("omega", [P, HI]), ("Win1", [P, 4, P]), ("Wl", [P, HI, DI]), ("bl", [P, HI]), ("Wv", [P, HI, DI]),
            ("bv", [P, HI]), ("Wout1", [P, HI, D]),
            ("Wq1", [P, P]), ("bq1", [P, 1]), ("Wk1", [DC + 1, P]), ("Wv1", [DC + 1, P]), ("Wo1", [P, P]),
            ("bo1", [1, P]),
            ("gate_wi", [P, M1, P]), ("gate_bi", [P, M1]), ("gate_wo", [P, M1, D]), ("gate_bo", [1, D]),
            ("exp_bi", [P, E, M1]), ("exp_bo", [E, P]),
        ):
            w[name] = sb("w_" + name, shape)
        ew0 = sb("ew0", [P, 2, 3, M0 * P])
        with nc.sbuf_tensor("R", [P, 4, 2, 2 * GT], F32) as R:
            pass
        sb("over_R0", [P, 2, 2 * GT])
        xhl = sb("xhl", [P, 2, N], F32R)
        whl = sb("whl", [P, 2, 2, GT], F32R)
        with nc.sbuf_tensor("G", [P, 6, HI, N], F32) as G:
            pass
        qhl = sb("qhl", [P, HI, N], F32R)
        sb("over_G1_to_G4", [P, 4, HI, N])
        kz = sb("kz", [P, 2, 2, HQ * LK], F32R)
        ew1 = R[:, 0, :, :].rearrange("p s (w n) -> p s w n", w=2)

        S = {}
        for name in (
            "x_in", "w_mamba", "w_ctx", "w_lru", "w_att", "w_gate", "w_e0a", "w_e0b", "w_e1a", "w_e1b", "out_sent",
            "const", "const_step", "dve_step", "act_step", "pool_step",
            "ln_stats", "ln_rstd", "ln_xn", "ln_tr", "ln_xnT", "ln_lo", "w_split",
            "in_mm", "in_silu", "dl_mm", "dl_abs", "dl_relu", "dl_ln", "dl_done", "bc_mm", "bc_split",
            "diag_ready", "b_bcast", "c_bcast", "decay", "b_copied", "drive", "scanned", "hc", "y_acc", "y_gated", "a_out", "a_res",
            "q_mm", "q_ev", "k_mm", "k_ev", "v_mm", "v_ev", "sc_mm", "sc_max", "sc_exp", "pt_mm", "pt_ev", "pv_mm", "pv_res",
            "rt_mm", "rt_sub", "rt_exp", "rt_cw", "up_mm", "silu0", "hid0", "down0", "res0",
            "xz_mm", "xz_ev", "l_mm", "l_ev", "v2_mm", "v2_ev", "lam_done", "z_silu", "sq_done", "vv_mm", "vv_read", "nb_done",
            "w_done", "dots_in", "vl_done", "r_dot", "r_s", "r_r", "r_acc", "r_g", "r_h", "r_lm", "g1_ready", "d_out", "d_res",
            "hq_mm", "hq_ev", "hq_lo", "hk_mm", "hk_ev", "hk_split", "hv_mm", "hv_ev", "bo_mm", "bo_ev", "bo_add", "kz_ready", "vz_ready",
            "hs_mm", "hs_sub", "hs_exp", "hs_inv", "hs_norm", "ht_mm", "ht_ev", "ho_mm", "ho_ev", "hw_mm", "hw_res",
            "gu_mm", "g_act", "g_hid", "gl_mm", "gl_cw", "wt_mm", "wt_ev", "eb_mm", "eb_res",
            "up1_mm", "act1", "hid1", "down1", "res1", "coef_done", "coef_sp", "omega_ln",
        ):
            S[name] = sem(name)

        class Chain:

            def __init__(self, eng, s):
                self.eng, self.s, self.n = eng, s, 0

            def __call__(self, ins):
                self.n += 1
                ins.then_inc(self.s, 1)
                self.eng.wait_ge(self.s, self.n)

        block = ctx.enter_context(nc.Block())

        SPLIT = (0, 2, 3, 5)
        PARTS = ((0, 0), (0, 1), (1, 0))
        wslot = lambda n: (n + 1) % 2
        N_E0, N_WIN1, N_GATE, N_E1 = 1, E + 2, E + 3, E + 4

        gcols = lambda g: slice(g * GT, (g + 1) * GT)
        gb = lambda g: slice(g * GB, (g + 1) * GB)
        GBUF = lambda i: G[:, i, :, :]

        uT, zT, dT, duT = (GBUF(i) for i in range(4))
        yT = GBUF(4)
        tmpT = GBUF(5)
        dBu = R[:, 0, :, :]
        hst = R[:, 1, :, :]
        hC = R[:, 2, :, :]
        Bsb = R[:, 3, :, 0:GT]
        qT = G[:, 0, 0, :]
        kT = G[:, 0, 1, 0:B * LK].rearrange("p (b k) -> p b k", b=B)
        vS = G[:, 1, 0, :].rearrange("p (b d) -> p b d", b=B)
        pr = G[:, 1, 1, 0:B * LK].rearrange("p (b k) -> p b k", b=B)
        prT = G[:, 2, 0, :].rearrange("p (b q) -> p b q", b=B)
        sh = G[:, 3, :, :].rearrange("p h (s n) -> p (h s) n", n=2 * GT)
        hidr = G[:, 4, :, :].rearrange("p h (s n) -> p (h s) n", n=2 * GT)
        pair = G[:, 5, 0, :].rearrange("p (k b e f) -> p k b e f", k=2, b=B, e=E)
        gl = G[:, 3, 0, :].rearrange("p (b d) -> p b d", b=B)
        top = G[:, 3, 1, 0:B * 8].rearrange("p (b k) -> p b k", b=B)
        cwT = G[0:E, 5, 1, :].rearrange("p (b t) -> p b t", b=B)
        xi, z1, lam, vv, nb, ww = (GBUF(i) for i in range(6))
        vb = LN[:]
        vw = R[:, 1:3, :, :].rearrange("p h s n -> p h (s n)")
        rvv = R[:, 3, :, :].rearrange("p s n -> p (s n)")
        col = lambda t, k: (t - k % 4) * (B // 4)
        sq = LN
        k1T = R[:, 1, :, :].rearrange("p s n -> p (s n)")[:, 0:B * LK].rearrange("p (b k) -> p b k", b=B)
        khl = R[:, 2:4, :, :].rearrange("p i s n -> p i (s n)")[:, :, 0:B * LK].rearrange("p i (b k) -> p i b k", b=B)
        v1S = G[:, 1, 0, :].rearrange("p (b d) -> p b d", b=B)
        p1 = G[:, 2, 0, 0:NH * LK].rearrange("p (h k) -> p h k", h=NH)
        e1 = G[:, 2, 1, 0:NH * LK].rearrange("p (h k) -> p h k", h=NH)
        n1 = G[:, 3, 0, 0:NH * LK].rearrange("p (h k) -> p h k", h=NH)
        n1T = G[:, 3, 1, :].rearrange("p (h q) -> p h q", h=NH)
        vz = G[:, 4, 0, 0:2 * HQ * P].rearrange("p (s j c) -> p s j c", s=2, j=HQ)
        oT = G[:, 4, 1, 0:P]
        bo_b = G[:, 4, 1, P:2 * P]

        def bank(i, n=1):
            return ps[:, i:i + n, :]

        @block.sync
        def _(sp):
            for g in range(NG):
                sp.dma_start(X[:, gb(g), :], a["x"].rearrange("b t d -> t b d")[:, gb(g), :]).then_inc(S["x_in"], 16)
            half = lambda ap: ap.rearrange("(k p) n -> p k n", p=P)
            row = lambda ap: ap.rearrange("(o n) -> o n", o=1)
            tiles = lambda ap: ap.rearrange("p (m n) -> p m n", n=P)

            def load(s, pairs):
                for name, src in pairs:
                    sp.dma_start(w[name][:], src).then_inc(S[s], 16)

            load("w_mamba", (("W_in", tiles(a["W_in"])), ("W_delta", half(a["W_delta"])), ("b_delta", a["b_delta"]),
                             ("W_BC", half(a["W_BC"])), ("A_log", half(a["A_log"])), ("D_param", a["D_param"]),
                             ("W_out", half(a["W_out"])), ("omega", a["omega"])))
            load("w_ctx", (("ctxT", a["ctxT"]), ("Wq0", a["Wq0"]), ("bq0", a["bq0"]), ("Wk0", a["Wk0"]),
                           ("Wv0", a["Wv0"]), ("router0", a["router0"])))
            load("w_lru", (("Win1", tiles(a["Win1"])), ("Wl", half(a["Wl"])), ("bl", a["bl"]),
                           ("Wv", half(a["Wv"])), ("bv", a["bv"]), ("Wout1", half(a["Wout1"]))))
            load("w_att", (("Wq1", a["Wq1"]), ("bq1", a["bq1"]), ("Wk1", a["Wk1"]), ("Wv1", a["Wv1"]),
                           ("Wo1", a["Wo1"]), ("bo1", row(a["bo1"]))))
            load("w_gate", (("gate_wi", tiles(a["gate_wi"])), ("gate_bi", a["gate_bi"]),
                            ("gate_wo", half(a["gate_wo"])), ("gate_bo", row(a["gate_bo"])),
                            ("exp_bi", a["exp_bi"]), ("exp_bo", a["exp_bo"])))

            def expert0(slot, s, w1, w3, w2):
                sp.dma_start(ew0[:, slot, 0, :], w1).then_inc(S[s], 16)
                sp.dma_start(ew0[:, slot, 1, :], w3).then_inc(S[s], 16)
                sp.dma_start(ew0[:, slot, 2, :].rearrange("p (m n) -> p m n", m=M0), half(w2)).then_inc(S[s], 16)

            expert0(0, "w_e0a", a["w1"][0], a["w3"][0], a["w2"][0])
            expert0(1, "w_e0b", a["w1"][1], a["w3"][1], a["w2"][1])
            for e in range(2, E + 1):
                sp.wait_ge(S["down0"], NG * (e - 1))
                if e < E:
                    expert0(e % 2, "w_e0b" if e % 2 else "w_e0a", a["w1"][e], a["w3"][e], a["w2"][e])
                else:
                    expert0(0, "w_e0a", a["sw1"], a["sw3"], a["sw2"])

            def expert1(slot, s, e):
                sp.dma_start(ew1[:, slot, 0, :], a["exp_wi"][e]).then_inc(S[s], 16)
                sp.dma_start(ew1[:, slot, 1, :].rearrange("p (m n) -> p m n", m=M1), half(a["exp_wo"][e])).then_inc(S[s], 16)

            sp.wait_ge(S["y_gated"], NG)
            for e in range(E):
                if e >= 2:
                    sp.wait_ge(S["down1"], NG * (e - 1))
                expert1(e % 2, "w_e1b" if e % 2 else "w_e1a", e)
            for g in range(NG):
                sp.wait_ge(S["res1"], NG * (E - 1) + g + 1)
                sp.dma_start(out.rearrange("b t d -> t b d")[:, gb(g), :], X[:, gb(g), :]).then_inc(S["out_sent"], 16)
            sp.wait_ge(S["out_sent"], 16 * NG)

        @block.gpsimd
        def _(pool):
            step = Chain(pool, S["pool_step"])
            gp = nc.gpsimd

            def rstd_of_ln(i):
                pool.wait_ge(S["ln_stats"], i + 1)
                gp.tensor_tensor(rstd[:], small[:, 0, :], mhalf[:], ALU.pow).then_inc(S["ln_rstd"], 1)

            gp.memset(mhalf[:], -0.5)
            step(gp.memset(ident[:], 0.0))
            step(gp.affine_select(out=ident[:], in_=ident[:], compare_op=ALU.not_equal, fill=1.0, base=0,
                                  pattern=[[-1, P]], channel_multiplier=1))
            gp.memset(ones[:], 1.0)
            step(gp.memset(sel[:], 0.0))
            for k in range(3):
                part = sel[32 * k:32 * k + 32, :, :]
                step(gp.affine_select(out=part, in_=part, compare_op=ALU.not_equal, fill=1.0, base=0,
                                      pattern=[[-1, 32], [0, P]], channel_multiplier=1))
            gp.memset(tri[:], 1.0)
            gp.memset(cw0[:], 1.0)
            step(gp.memset(hmask[:], 1.0))
            step(gp.affine_select(out=tri[:], in_=tri[:], compare_op=ALU.is_gt, fill=0.0, base=0,
                                  pattern=[[1, E], [-1, E]], channel_multiplier=0))
            for r in range(P // 32):
                part = hmask[32 * r:32 * r + 32, :]
                step(gp.affine_select(out=part, in_=part, compare_op=ALU.is_ge, fill=0.0, base=0,
                                      pattern=[[-DK, HQ]], channel_multiplier=1))
                step(gp.affine_select(out=part, in_=part, compare_op=ALU.is_ge, fill=0.0, base=DK - 1,
                                      pattern=[[DK, HQ]], channel_multiplier=-1))
            gp.memset(rstd[:], 0.0).then_inc(S["const"], 1)

            def split(n, src):
                step(gp.tensor_copy(whl[:, wslot(n), 0], src))
                gp.tensor_tensor(whl[:, wslot(n), 1], src, whl[:, wslot(n), 0].bitcast(F32), ALU.subtract).then_inc(S["w_split"], 1)

            pool.wait_ge(S["w_mamba"], 16 * 8)
            split(0, w["W_in"][:].rearrange("p m n -> p (m n)"))
            rstd_of_ln(0)
            for g in range(NG):
                pool.wait_ge(S["dl_done"], 2 * g + 2)
                for n in range(NS):
                    i, j = g * NS + n, n % 2
                    pool.wait_ge(S["b_copied"], i + 1)
                    if i >= 2:
                        pool.wait_ge(S["scanned"], i - 1)
                    gp.tensor_tensor(
                        dBu[:, j, :].rearrange("p (h n) -> p h n", h=HI), duT[:, :, gcols(g)],
                        Bsb[:, j:j + 1, :].broadcast_to([P, HI, GT]), ALU.mult).then_inc(S["drive"], 1)
            step(gp.memset(nones[:], -1.0))
            rstd_of_ln(1)

            def split_e0(e):
                pool.wait_ge(S["w_e0b" if e % 2 else "w_e0a"], 48 * (e // 2 + 1))
                if e >= 2:
                    pool.wait_ge(S["up_mm"], M0 * NG * (e - 1))
                split(N_E0 + e, ew0[:, e % 2, 0:2].rearrange("p w n -> p (w n)"))

            split_e0(0)
            split_e0(1)
            rstd_of_ln(2)
            for e in range(2, E + 1):
                split_e0(e)
            pool.wait_ge(S["w_lru"], 16 * 6)
            pool.wait_ge(S["up_mm"], M0 * NG * E)
            split(N_WIN1, w["Win1"][:].rearrange("p m n -> p (m n)"))
            rstd_of_ln(3)
            tok = lambda buf, g: buf[:, :, gcols(g)].rearrange("p h (b t) -> p h b t", b=GB)
            for g in range(NG):
                for buf, src, ready in ((vb, nb, "vv_read"), (vw, ww, "w_done")):
                    pool.wait_ge(S[ready], g + 1)
                    if buf is vb:
                        pool.wait_ge(S["nb_done"], g + 1)
                    gp.memset(tok(buf, g)[:, :, :, 0:1], 0.0)
                    gp.tensor_tensor(tok(buf, g)[:, :, :, 1:T], tok(vv, g)[:, :, :, 1:T], tok(src, g)[:, :, :, 0:T - 1],
                                     ALU.mult).then_inc(S["dots_in"], 1)
            at = lambda buf, t: buf.rearrange("p h (b t) -> p h b t", b=B)[:, :, :, bass.ds(t, 1)].rearrange("p h b o -> p h (b o)")

            def add_drive(t, k):
                pool.wait_ge(S["r_lm"], t)
                gp.tensor_tensor(grec[:, k % 2], lm[:, (k - 1) % 2, 0], at(nb, t), ALU.subtract).then_inc(S["r_g"], 1)

            with pool.Fori(0, T - 2 * UR + 1, UR) as t0:
                for k in range(1, UR + 1):
                    add_drive(t0 + k, k)
            for t in range(T - UR + 1, T):
                add_drive(t, t % UR)
            pool.wait_ge(S["hk_ev"], NG)
            step(gp.tensor_copy(khl[:, 0].bitcast(F32R), k1T))
            gp.tensor_tensor(khl[:, 1].bitcast(F32R), k1T, khl[:, 0], ALU.subtract).then_inc(S["hk_split"], 1)
            pool.wait_ge(S["d_out"], NG)
            step(gp.memset(vz, 0.0))
            rstd_of_ln(4)

            def keys(b):
                if b >= 2:
                    pool.wait_ge(S["hs_mm"], 2 * (b - 1))
                for i in range(2):
                    ins = gp.tensor_tensor(kz[:, b % 2, i, :].rearrange("p (j k) -> p j k", j=HQ),
                                           khl[:, i, b, :].unsqueeze(1).broadcast_to([P, HQ, LK]),
                                           hmask[:].unsqueeze(2).broadcast_to([P, HQ, LK]), ALU.mult)
                ins.then_inc(S["kz_ready"], 1)

            pool.wait_ge(S["hk_split"], 1)
            keys(0)
            pool.wait_ge(S["bo_ev"], 1)
            pool.wait_ge(S["ln_xn"], 5 * NG)
            gp.tensor_tensor(X[:], X[:], bo_b.unsqueeze(1).broadcast_to([P, B, D]), ALU.add).then_inc(S["bo_add"], 1)
            for b in range(B):
                if b + 1 < B:
                    keys(b + 1)
                if b >= 2:
                    pool.wait_ge(S["ho_mm"], b - 1)
                for j in range(HQ):
                    ins = gp.tensor_copy(vz[0:LK, b % 2, j].rearrange("p (r i d) -> p r i d", r=4, i=HQ)[:, :, j, :],
                                         v1S[0:LK, b, :].rearrange("p (r i d) -> p r i d", r=4, i=HQ)[:, :, j, :])
                ins.then_inc(S["vz_ready"], 1)
                for q in range(2):
                    hh = slice(8 * q, 8 * q + 8)
                    pool.wait_ge(S["hs_inv"], 2 * b + q + 1)
                    if b:
                        pool.wait_ge(S["ht_mm"], 2 * b - 1 + q)
                    gp.tensor_tensor(n1[:, hh, :], e1[:, hh, :], small[:, 3, hh].unsqueeze(2).broadcast_to([P, 8, LK]), ALU.mult)\
                        .then_inc(S["hs_norm"], 1)
            pool.wait_ge(S["w_gate"], 16 * 6)
            split(N_GATE, w["gate_wi"][:].rearrange("p m n -> p (m n)"))

            def split_e1(e):
                pool.wait_ge(S["w_e1b" if e % 2 else "w_e1a"], 32 * (e // 2 + 1))
                if e >= 2:
                    pool.wait_ge(S["up1_mm"], M1 * NG * (e - 1))
                elif e == 1:
                    pool.wait_ge(S["gu_mm"], M1 * NG)
                split(N_E1 + e, ew1[:, e % 2, 0])

            rstd_of_ln(5)
            for e in range(E):
                split_e1(e)

        @block.scalar
        def _(act):
            sc = nc.scalar
            step = Chain(act, S["act_step"])

            def xnT_copy(i):
                for g in range(NG):
                    act.wait_ge(S["ln_tr"], i * NG + g + 1)
                    if i == 2:
                        sc.copy(xnT[:, gcols(g)], bank(g)[:, 0, :])
                    sc.copy((xhl[:, 0] if i in SPLIT else xnT)[:, gcols(g)], bank(g)[:, 0, :]).then_inc(S["ln_xnT"], 1)

            act.wait_ge(S["w_mamba"], 16 * 8)
            step(sc.activation(negA[:].rearrange("p h n -> p (h n)"), w["A_log"][:].rearrange("p h n -> p (h n)"), ACT.Exp))
            step(sc.mul(negA[:].rearrange("p h n -> p (h n)"), negA[:].rearrange("p h n -> p (h n)"), -1.0))
            xnT_copy(0)
            for g in range(NG):
                for m in range(4):
                    act.wait_ge(S["in_mm"], 4 * g + m + 1)
                    dst = uT if m < HI else zT
                    sc.activation(dst[:, m % HI, gcols(g)], bank(4 + m)[:, 0, :], ACT.Silu).then_inc(S["in_silu"], 1)
            for g in range(NG):
                for m in range(HI):
                    act.wait_ge(S["dl_mm"], HI * g + m + 1)
                    sc.activation(tmpT[:, m, gcols(g)], bank(2 * (g % 2) + m)[:, 0, :], ACT.Abs,
                                  bias=w["b_delta"][:, m:m + 1]).then_inc(S["dl_abs"], 1)
            act.wait_ge(S["dl_abs"], HI * NG)
            step(sc.activation(tmpT[:], tmpT[:], ACT.Exp, scale=-1.0))
            sc.activation(tmpT[:], tmpT[:], ACT.Ln, bias=1.0).then_inc(S["dl_ln"], 1)
            def b_copy(i):
                act.wait_ge(S["b_bcast"], i + 1)
                if i >= 2:
                    act.wait_ge(S["drive"], i - 1)
                sc.copy(Bsb[:, i % 2, :], bank(4)[:, 0, :]).then_inc(S["b_copied"], 1)

            b_copy(0)
            for g in range(NG):
                act.wait_ge(S["dl_done"], 2 * g + 1)
                for n in range(NS):
                    i, j = g * NS + n, n % 2
                    if i + 1 < NG * NS:
                        b_copy(i + 1)
                    if i >= 2:
                        act.wait_ge(S["scanned"], i - 1)
                    for m in range(HI):
                        sc.activation(
                            bank(2 * j + m)[:, 0, :].rearrange("p (b t) -> p b t", b=GB)[:, :, 1:T],
                            dT[:, m, gcols(g)].rearrange("p (b t) -> p b t", b=GB)[:, :, 1:T], ACT.Exp,
                            scale=negA[:, m, n:n + 1]).then_inc(S["decay"], 1)
            xnT_copy(1)
            for g in range(NG):
                act.wait_ge(S["q_mm"], g + 1)
                sc.activation(qT[:, gcols(g)], bank(4 + g)[:, 0, :], ACT.Identity, bias=w["bq0"][:, 0:1]).then_inc(S["q_ev"], 1)
            for g in range(NG):
                act.wait_ge(S["v_mm"], g + 1)
                sc.copy(vS[0:LK, gb(g), :], bank(4 + g)[0:LK, 0, :].rearrange("p (b d) -> p b d", b=GB)).then_inc(S["v_ev"], 1)
            for g in range(NG):
                act.wait_ge(S["sc_max"], g + 1)
                for b in range(GB):
                    sc.activation(pr[:, g * GB + b, :], bank(g)[:, 0, b * LK:(b + 1) * LK], ACT.Exp,
                                  bias=small[:, 1, g * GB + b:g * GB + b + 1],
                                  accum_out=small[:, 2, g * GB + b:g * GB + b + 1]).then_inc(S["sc_exp"], 1)
            xnT_copy(2)
            act.wait_ge(S["rt_sub"], 1)
            sc.activation(router[:, 1, :, :], router[:, 0, :, :], ACT.Exp).then_inc(S["rt_exp"], 1)
            for i in range((E + 1) * NG):
                for m in range(M0):
                    k = M0 * i + m
                    act.wait_ge(S["up_mm"], k + 1)
                    if i >= 2:
                        act.wait_ge(S["hid0"], k + 1 - 2 * M0)
                    sc.activation(sh[:, i % 2, m * GT:(m + 1) * GT], bank(m)[:, 0, :], ACT.Silu).then_inc(S["silu0"], 1)
            step(sc.activation(coef[:, 1, :], w["omega"][:], ACT.Abs))
            step(sc.activation(coef[:, 1, :], coef[:, 1, :], ACT.Exp, scale=-1.0))
            sc.activation(coef[:, 1, :], coef[:, 1, :], ACT.Ln, bias=1.0).then_inc(S["omega_ln"], 1)
            xnT_copy(3)
            act.wait_ge(S["coef_done"], 1)

            def xz_copy(g):
                for m in range(4):
                    act.wait_ge(S["xz_mm"], 4 * g + m + 1)
                    sc.copy((xi if m < HI else z1)[:, m % HI, gcols(g)], bank(4 + m)[:, 0, :]).then_inc(S["xz_ev"], 1)

            xz_copy(0)
            for g in range(NG):
                if g + 1 < NG:
                    xz_copy(g + 1)
                for m in range(HI):
                    act.wait_ge(S["l_mm"], HI * g + m + 1)
                    sc.activation(lam[:, m, gcols(g)], bank(m)[:, 0, :], ACT.Sigmoid, bias=w["bl"][:, m:m + 1])\
                        .then_inc(S["l_ev"], 1)
                for m in range(HI):
                    act.wait_ge(S["l_ev"], HI * g + m + 1)
                    sc.activation(lam[:, m, gcols(g)], lam[:, m, gcols(g)], ACT.Exp, scale=coef[:, 2, m:m + 1])\
                        .then_inc(S["lam_done"], 1)
            for m in range(HI):
                sc.activation(z1[:, m, :], z1[:, m, :], ACT.Silu).then_inc(S["z_silu"], 1)
            for g in range(NG):
                act.wait_ge(S["hk_mm"], g + 1)
                sc.copy(k1T[:, gb(g), :], bank(4 + g)[:, 0, 0:GB * LK].rearrange("p (b k) -> p b k", b=GB)).then_inc(S["hk_ev"], 1)
            for g in range(NG):
                act.wait_ge(S["hv_mm"], g + 1)
                act.wait_ge(S["g1_ready"], NG)
                sc.copy(v1S[0:LK, gb(g), :], bank(4 + g)[0:LK, 0, :].rearrange("p (b d) -> p b d", b=GB)).then_inc(S["hv_ev"], 1)
            act.wait_ge(S["bo_mm"], 1)
            sc.copy(bo_b, bank(4)[:, 0, 0:P]).then_inc(S["bo_ev"], 1)
            xnT_copy(4)
            for g in range(NG):
                act.wait_ge(S["hq_mm"], g + 1)
                sc.activation(qhl[:, 0, gcols(g)], bank(4 + g)[:, 0, :], ACT.Identity, bias=w["bq1"][:, 0:1]).then_inc(S["hq_ev"], 1)

            def head_out_copy(b):
                act.wait_ge(S["ho_mm"], b + 1)
                if b:
                    act.wait_ge(S["hw_mm"], b)
                for r in range(4):
                    rows = slice(32 * r, 32 * r + 32)
                    ins = sc.copy(oT[rows, :], bank(6)[rows, 0, r * T:(r + 1) * T])
                ins.then_inc(S["ho_ev"], 1)

            for b in range(-1, B):
                if b >= 1:
                    head_out_copy(b - 1)
                for q in range(2):
                    if b >= 0:
                        act.wait_ge(S["ht_mm"], 2 * b + q + 1)
                        if b:
                            act.wait_ge(S["ho_mm"], b)
                        sc.copy(n1T[0:LK, 8 * q:8 * q + 8, :].rearrange("p (c h) q -> p c (h q)", c=2),
                                bank(4, 2)[0:LK, :, :]).then_inc(S["ht_ev"], 1)
                    if b + 1 < B:
                        c = b + 1
                        act.wait_ge(S["hs_sub"], 2 * c + q + 1)
                        if c:
                            act.wait_ge(S["hs_norm"], 2 * c - 1 + q)
                        sc.activation(e1[:, 8 * q:8 * q + 8, :], p1[:, 8 * q:8 * q + 8, :], ACT.Exp,
                                      scale=float(DK) ** -0.5).then_inc(S["hs_exp"], 1)
            head_out_copy(B - 1)
            xnT_copy(5)

            def selu(i, slot, banks, lin_bias, exp_bias, mm_s, act_s):
                for m in range(M1):
                    act.wait_ge(S[mm_s], M1 * i + m + 1)
                    sc.activation(G[:, 0, slot, m * GT:(m + 1) * GT], banks[:, m, :], ACT.Exp, bias=exp_bias[m])
                    sc.activation(G[:, 1, slot, m * GT:(m + 1) * GT], banks[:, m, :], ACT.Relu, bias=lin_bias[m],
                                  scale=SELU_L).then_inc(S[act_s], 1)

            act.wait_ge(S["coef_sp"], 1)
            for g in range(NG):
                if g >= 2:
                    act.wait_ge(S["g_hid"], g - 1)
                selu(g, g % 2, bank(0, M1), [ebs[:, 0, m:m + 1] for m in range(M1)],
                     [w["gate_bi"][:, m:m + 1] for m in range(M1)], "gu_mm", "g_act")
            for i in range(E * NG):
                e = i // NG
                act.wait_ge(S["g_hid"], NG)
                if i >= 2:
                    act.wait_ge(S["hid1"], i - 1)
                selu(i, i % 2, bank(0, M1), [ebs[:, 1 + e, m:m + 1] for m in range(M1)],
                     [w["exp_bi"][:, e, m:m + 1] for m in range(M1)], "up1_mm", "act1")

        @block.vector
        def _(dve):
            v = nc.vector
            step = Chain(dve, S["dve_step"])

            def layer_norm(i):
                for b in range(B):
                    v.bn_stats(stats[:, b, :], X[:, b, :]) if b < B - 1 else step(v.bn_stats(stats[:, b, :], X[:, b, :]))
                for b in range(B):
                    v.bn_aggr(mv[:, b, :], stats[:, b, :]) if b < B - 1 else step(v.bn_aggr(mv[:, b, :], stats[:, b, :]))
                v.tensor_scalar(small[:, 0, :], mv[:, :, 1], EPS, None, ALU.add).then_inc(S["ln_stats"], 1)
                dve.wait_ge(S["ln_rstd"], i + 1)
                for b in range(B):
                    ins = v.tensor_scalar(xn[:, b, :], X[:, b, :], mv[:, b, 0:1], rstd[:, b:b + 1], ALU.subtract, ALU.mult)
                    if b % GB == GB - 1:
                        ins.then_inc(S["ln_xn"], 1)
                if i in SPLIT:
                    for g in range(NG):
                        dve.wait_ge(S["ln_xnT"], i * NG + g + 1)
                        v.tensor_tensor(xhl[:, 1, gcols(g)], bank(g)[:, 0, :], xhl[:, 0, gcols(g)].bitcast(F32), ALU.subtract)\
                            .then_inc(S["ln_lo"], 1)

            def choose(val, cw):
                vb = val.unsqueeze(3).broadcast_to([P, B, E, E])
                vo = val.unsqueeze(2).broadcast_to([P, B, E, E])
                step(v.tensor_tensor(pair[:, 0], vo, vb, ALU.is_equal))
                step(v.tensor_tensor(pair[:, 1], vo, vb, ALU.is_gt))
                tb = tri[:].unsqueeze(1).broadcast_to([P, B, E, E])
                step(v.tensor_tensor(pair[:, 0], pair[:, 0], tb, ALU.mult))
                step(v.tensor_tensor(pair[:, 0], pair[:, 0], pair[:, 1], ALU.add))
                step(v.tensor_reduce(router[:, 2], pair[:, 0], AX.X, ALU.add))
                step(v.tensor_scalar(router[:, 3], router[:, 2], 1.5, None, ALU.is_lt))
                step(v.tensor_tensor(router[:, 4], router[:, 3], val, ALU.mult))
                step(v.tensor_reduce(small[:, 3, :], router[:, 4], AX.X, ALU.add))
                step(v.reciprocal(small[:, 1, :], small[:, 3, :]))
                return v.tensor_tensor(cw, router[:, 4], small[:, 1, :].unsqueeze(2).broadcast_to([P, B, E]), ALU.mult)

            dve.wait_ge(S["x_in"], 16 * NG)
            dve.wait_ge(S["const"], 1)
            layer_norm(0)
            dve.wait_ge(S["w_mamba"], 16 * 8)
            for m in range(HI):
                v.tensor_scalar(diagD[:, m, :], ident[:], w["D_param"][:, m:m + 1], None, ALU.mult).then_inc(S["diag_ready"], 1)
            for g in range(NG):
                for m in range(HI):
                    dve.wait_ge(S["dl_abs"], HI * g + m + 1)
                    v.tensor_scalar(dT[:, m, gcols(g)], bank(2 * (g % 2) + m)[:, 0, :], w["b_delta"][:, m:m + 1], 0.0,
                                    ALU.add, ALU.max).then_inc(S["dl_relu"], 1)
            dve.wait_ge(S["bc_mm"], NG)
            psBC = bank(4, 4)[0:2 * NS].rearrange("p g n -> p (g n)")
            rem = yT[0:2 * NS, 0, :]
            mid = yT[0:2 * NS, 1, :].bitcast(BF16)[:, 0:N]
            step(v.tensor_copy(bc3[0:32, :], psBC))
            step(v.tensor_tensor(rem, psBC, bc3[0:32, :], ALU.subtract))
            step(v.tensor_copy(mid, rem))
            v.tensor_copy(bc3[32:64, :], mid)
            step(v.tensor_tensor(bc3[64:96, :], rem, mid, ALU.subtract))
            for j in range(4):
                ins = v.memset(bank(j)[:, 0, :].rearrange("p (b t) -> p b t", b=GB)[:, :, 0:1], 0.0)
            ins.then_inc(S["bc_split"], 1)
            dve.wait_ge(S["dl_ln"], 1)
            dve.wait_ge(S["dl_relu"], HI * NG)
            for g in range(NG):
                v.tensor_tensor(dT[:, :, gcols(g)], dT[:, :, gcols(g)], tmpT[:, :, gcols(g)], ALU.add).then_inc(S["dl_done"], 1)
                dve.wait_ge(S["dl_done"], 2 * g + 1)
                v.tensor_tensor(duT[:, :, gcols(g)], dT[:, :, gcols(g)], uT[:, :, gcols(g)], ALU.mult).then_inc(S["dl_done"], 1)
            for g in range(NG):
                for n in range(NS):
                    i, j = g * NS + n, n % 2
                    dve.wait_ge(S["decay"], HI * i + HI)
                    dve.wait_ge(S["drive"], i + 1)
                    v.tensor_tensor_scan(hst[:, j, :], bank(2 * j, 2).rearrange("p h n -> p (h n)"), dBu[:, j, :], 0.0,
                                         ALU.mult, ALU.add).then_inc(S["scanned"], 1)
                    dve.wait_ge(S["scanned"], i + 1)
                    dve.wait_ge(S["c_bcast"], i + 1)
                    if i >= 2:
                        dve.wait_ge(S["y_acc"], i - 1)
                    v.tensor_tensor(hC[:, j, :].rearrange("p (h n) -> p h n", h=HI),
                                    hst[:, j, :].rearrange("p (h n) -> p h n", h=HI),
                                    bank(5).broadcast_to([P, HI, GT]), ALU.mult).then_inc(S["hc"], 1)
                dve.wait_ge(S["y_acc"], (g + 1) * NS)
                v.tensor_tensor(yT[:, :, gcols(g)], bank(6, 2), zT[:, :, gcols(g)], ALU.mult).then_inc(S["y_gated"], 1)
            for g in range(NG):
                dve.wait_ge(S["a_out"], g + 1)
                v.tensor_tensor(X[:, gb(g), :], X[:, gb(g), :], bank(g)[:, 0, :].rearrange("p (b d) -> p b d", b=GB),
                                ALU.add).then_inc(S["a_res"], 1)
            dve.wait_ge(S["a_res"], NG)
            layer_norm(1)
            for g in range(NG):
                dve.wait_ge(S["k_mm"], g + 1)
                v.tensor_copy(kT[:, gb(g), :], bank(g)[:, 0, 0:GB * LK].rearrange("p (b k) -> p b k", b=GB)).then_inc(S["k_ev"], 1)
            for g in range(NG):
                dve.wait_ge(S["sc_mm"], g + 1)
                v.tensor_reduce(small[:, 1, gb(g)], bank(g)[:, 0, 0:GB * LK].rearrange("p (b k) -> p b k", b=GB), AX.X,
                                ALU.max, negate=True).then_inc(S["sc_max"], 1)
            for g in range(NG):
                dve.wait_ge(S["pt_mm"], g + 1)
                v.tensor_copy(prT[0:LK, gb(g), :], bank(4 + g)[0:LK, 0, :].rearrange("p (b q) -> p b q", b=GB)).then_inc(S["pt_ev"], 1)
            dve.wait_ge(S["sc_exp"], B)
            step(v.reciprocal(small[:, 3, :], small[:, 2, :]))
            for g in range(NG):
                dve.wait_ge(S["pv_mm"], g + 1)
                for b in range(GB):
                    bi = g * GB + b
                    v.scalar_tensor_tensor(X[:, bi, :], bank(g)[:, 0, b * D:(b + 1) * D], small[:, 3, bi:bi + 1], X[:, bi, :],
                                           ALU.mult, ALU.add).then_inc(S["pv_res"], 1)
            dve.wait_ge(S["pv_res"], B)
            layer_norm(2)
            dve.wait_ge(S["rt_mm"], 1)
            lg = bank(7)[:, 0, 0:B * E].rearrange("p (b e) -> p b e", b=B)
            step(v.tensor_reduce(small[:, 1, :], lg, AX.X, ALU.max))
            v.tensor_tensor(router[:, 0], lg, small[:, 1, :].unsqueeze(2).broadcast_to([P, B, E]), ALU.subtract).then_inc(S["rt_sub"], 1)
            dve.wait_ge(S["rt_exp"], 1)
            choose(router[:, 1], cw0[:, :, 0:E]).then_inc(S["rt_cw"], 1)
            dve.wait_ge(S["rt_cw"], 1)

            def add_expert(i, cw, e, dn, rs):
                g = i % NG
                dve.wait_ge(S[dn], i + 1)
                for b in range(GB):
                    bi = g * GB + b
                    ins = v.scalar_tensor_tensor(X[:, bi, :], bank(4 + i % 2)[:, 0, b * D:(b + 1) * D], cw[:, bi, e:e + 1],
                                                 X[:, bi, :], ALU.mult, ALU.add)
                ins.then_inc(S[rs], 1)

            for i in range((E + 1) * NG + 1):
                if i < (E + 1) * NG:
                    if i >= 2:
                        dve.wait_ge(S["down0"], i - 1)
                    for m in range(M0):
                        dve.wait_ge(S["silu0"], M0 * i + m + 1)
                        v.tensor_tensor(hidr[:, i % 2, m * GT:(m + 1) * GT], sh[:, i % 2, m * GT:(m + 1) * GT],
                                        bank(2 + m)[:, 0, :], ALU.mult).then_inc(S["hid0"], 1)
                if i >= 1:
                    if i > NG:
                        dve.wait_ge(S["res0"], i - NG)
                    add_expert(i - 1, cw0, (i - 1) // NG, "down0", "res0")
            dve.wait_ge(S["res0"], (E + 1) * NG)
            layer_norm(3)
            step(v.tensor_scalar(coef[:, 0, :], w["omega"][:], 0.0, None, ALU.max))
            dve.wait_ge(S["omega_ln"], 1)
            step(v.tensor_tensor(coef[:, 3, :], coef[:, 0, :], coef[:, 1, :], ALU.add))
            v.tensor_scalar(coef[:, 2, :], coef[:, 3, :], -8.0, None, ALU.mult).then_inc(S["coef_done"], 1)
            tok = lambda buf, g: buf[:, :, gcols(g)].rearrange("p h (b t) -> p h b t", b=GB)

            def v_and_square(g):
                for m in range(HI):
                    dve.wait_ge(S["v2_mm"], HI * g + m + 1)
                    v.tensor_scalar(vv[:, m, gcols(g)], bank(2 - 2 * m)[:, 0, :], w["bv"][:, m:m + 1], None, ALU.add)\
                        .then_inc(S["v2_ev"], 1)
                dve.wait_ge(S["v2_ev"], HI * (g + 1))
                v.tensor_tensor(sq[:, :, gcols(g)], vv[:, :, gcols(g)], vv[:, :, gcols(g)], ALU.mult).then_inc(S["sq_done"], 1)

            v_and_square(0)
            for g in range(NG):
                dve.wait_ge(S["lam_done"], HI * (g + 1))
                step(v.memset(tok(lam, g)[:, :, :, 0:1], 0.0))
                v.scalar_tensor_tensor(nb[:, :, gcols(g)], lam[:, :, gcols(g)], 1.0, xi[:, :, gcols(g)], ALU.subtract,
                                       ALU.mult).then_inc(S["nb_done"], 1)
                if g + 1 < NG:
                    v_and_square(g + 1)
                dve.wait_ge(S["vv_mm"], g + 1)
                ins = v.reciprocal(rvv[:, gcols(g)], bank(3)[:, 0, :])
                ins.then_inc(S["vv_read"], 1)
                dve.wait_ge(S["vv_read"], g + 1)
                step(v.scalar_tensor_tensor(ww[:, :, gcols(g)], vv[:, :, gcols(g)], -2.0,
                                            rvv[:, gcols(g)].unsqueeze(1).broadcast_to([P, HI, GT]), ALU.mult, ALU.mult))
                v.tensor_tensor(ww[:, :, gcols(g)], ww[:, :, gcols(g)], lam[:, :, gcols(g)], ALU.mult).then_inc(S["w_done"], 1)
            for g in range(NG):
                dve.wait_ge(S["dots_in"], 2 * (g + 1))
                v.tensor_tensor(tok(vv, g)[:, :, :, 0:T - 1], tok(vv, g)[:, :, :, 1:T], tok(lam, g)[:, :, :, 0:T - 1],
                                ALU.mult).then_inc(S["vl_done"], 1)
            at = lambda buf, t: buf.rearrange("p h (b t) -> p h b t", b=B)[:, :, :, bass.ds(t, 1)].rearrange("p h b o -> p h (b o)")
            lamvl = G[:, 2:4, :, :]

            def to_next(t, k):
                src = lamvl.rearrange("p i h (b t) -> p i h b t", b=B)[:, :, :, :, bass.ds(t + 1, 1)]
                h = at(xi, t).unsqueeze(1).broadcast_to([P, 2, HI, B])
                return v.tensor_tensor(lm[:, k % 2], src.rearrange("p i h b o -> p i h (b o)"), h, ALU.mult)

            def advance(t, k, last=False):
                slot = lambda first: ps[:, first + k % 4, bass.ds(col(t, k), B)]
                dve.wait_ge(S["r_dot"], t)
                v.tensor_tensor(sdot[:], slot(0), acc[:], ALU.add).then_inc(S["r_s"], 1)
                dve.wait_ge(S["r_s"], t)
                v.tensor_tensor(rrec[:], at(ww, t), sdot[:].unsqueeze(1).broadcast_to([P, HI, B]), ALU.mult)\
                    .then_inc(S["r_r"], 1)
                dve.wait_ge(S["r_r"], t)
                dve.wait_ge(S["r_g"], t)
                v.tensor_tensor(at(xi, t), rrec[:], grec[:, k % 2], ALU.add).then_inc(S["r_h"], 1)
                if not last:
                    nxt = ps[:, 4 + (k + 1) % 4, bass.ds(col(t + 1, k + 1), B)]
                    v.tensor_tensor(acc[:], nxt, sdot[:], ALU.mult).then_inc(S["r_acc"], 1)
                    dve.wait_ge(S["r_h"], t)
                    to_next(t, k).then_inc(S["r_lm"], 1)
                    dve.wait_ge(S["r_acc"], t)

            dve.wait_ge(S["vl_done"], NG)
            step(v.memset(acc[:], 0.0))
            to_next(0, 0).then_inc(S["r_lm"], 1)
            with dve.Fori(0, T - 2 * UR + 1, UR) as t0:
                for k in range(1, UR + 1):
                    advance(t0 + k, k)
            for t in range(T - UR + 1, T):
                advance(t, t % UR, last=t == T - 1)
            dve.wait_ge(S["r_h"], T - 1)
            dve.wait_ge(S["z_silu"], HI)
            for g in range(NG):
                v.tensor_tensor(nb[:, :, gcols(g)], xi[:, :, gcols(g)], z1[:, :, gcols(g)], ALU.mult).then_inc(S["g1_ready"], 1)
            for g in range(NG):
                dve.wait_ge(S["d_out"], g + 1)
                v.tensor_tensor(X[:, gb(g), :], X[:, gb(g), :], bank(g)[:, 0, :].rearrange("p (b d) -> p b d", b=GB),
                                ALU.add).then_inc(S["d_res"], 1)
            dve.wait_ge(S["d_res"], NG)
            layer_norm(4)
            for g in range(NG):
                dve.wait_ge(S["hq_ev"], g + 1)
                v.scalar_tensor_tensor(qhl[:, 1, gcols(g)], bank(4 + g)[:, 0, :], w["bq1"][:, 0:1], qhl[:, 0, gcols(g)].bitcast(F32),
                                       ALU.add, ALU.subtract).then_inc(S["hq_lo"], 1)

            def head_sums(b, q):
                hh = slice(8 * q, 8 * q + 8)
                dve.wait_ge(S["hs_exp"], 2 * b + q + 1)
                step(v.tensor_reduce(small[:, 2, hh], e1[:, hh, :], AX.X, ALU.add))
                if b:
                    dve.wait_ge(S["hs_norm"], 2 * b - 1 + q)
                v.reciprocal(small[:, 3, hh], small[:, 2, hh]).then_inc(S["hs_inv"], 1)

            for b in range(B + 2):
                for q in range(2):
                    if q == 0 and 1 <= b <= B:
                        head_sums(b - 1, 1)
                    if b < B:
                        hh = slice(8 * q, 8 * q + 8)
                        dve.wait_ge(S["hs_mm"], 2 * b + q + 1)
                        sc2 = bank(2 * q, 2)[:, :, 0:HQ * LK].rearrange("p g (j k) -> p g j k", j=HQ)
                        step(v.tensor_reduce(small[:, 1, hh].rearrange("p (g j) -> p g j", j=HQ), sc2, AX.X, ALU.max))
                        if b:
                            dve.wait_ge(S["hs_exp"], 2 * b - 1 + q)
                        for r in range(2):
                            h4 = slice(8 * q + HQ * r, 8 * q + HQ * r + HQ)
                            ins = v.tensor_tensor(p1[:, h4, :], sc2[:, r],
                                                  small[:, 1, h4].unsqueeze(2).broadcast_to([P, HQ, LK]), ALU.subtract)
                        ins.then_inc(S["hs_sub"], 1)
                    if q and b < B:
                        head_sums(b, 0)
                if b >= 2:
                    c = b - 2
                    dve.wait_ge(S["hw_mm"], c + 1)
                    if c == 0:
                        dve.wait_ge(S["bo_add"], 1)
                    v.tensor_tensor(X[:, c, :], X[:, c, :], bank(7)[:, 0, 0:P], ALU.add).then_inc(S["hw_res"], 1)
            dve.wait_ge(S["hw_res"], B)
            layer_norm(5)
            dve.wait_ge(S["w_gate"], 16 * 6)
            v.tensor_scalar(ebs[:, 0, :], w["gate_bi"][:], SELU_L, None, ALU.mult)
            v.tensor_scalar(ebs[:, 1:, :], w["exp_bi"][:], SELU_L, None, ALU.mult).then_inc(S["coef_sp"], 1)

            def selu_sum(i, slot, a_s, h_s):
                dve.wait_ge(S[a_s], M1 * (i + 1))
                step(v.tensor_scalar(G[:, 0, slot, :], G[:, 0, slot, :], 1.0, 1.0, ALU.min, ALU.subtract))
                v.scalar_tensor_tensor(G[:, 2, slot, :], G[:, 0, slot, :], SELU_LA, G[:, 1, slot, :], ALU.mult,
                                       ALU.add).then_inc(S[h_s], 1)

            for g in range(NG):
                if g >= 2:
                    dve.wait_ge(S["gl_mm"], g - 1)
                selu_sum(g, g % 2, "g_act", "g_hid")
            for g in range(NG):
                dve.wait_ge(S["gl_mm"], g + 1)
                step(v.tensor_copy(gl[:, gb(g), :], bank(4 + g)[:, 0, :].rearrange("p (b d) -> p b d", b=GB)))
            for b in range(B):
                ins = v.max(top[:, b, :], gl[:, b, :])
            step(ins)
            le = gl[:, :, 0:E]
            step(v.tensor_tensor(pair[:, 0], le.unsqueeze(2).broadcast_to([P, B, E, E]),
                                 le.unsqueeze(3).broadcast_to([P, B, E, E]), ALU.is_equal))
            step(v.tensor_tensor(pair[:, 0], pair[:, 0], tri[:].unsqueeze(1).broadcast_to([P, B, E, E]), ALU.mult))
            step(v.tensor_reduce(router[:, 2], pair[:, 0], AX.X, ALU.add))
            for k in range(2):
                step(v.tensor_tensor(router[:, 3], top[:, :, k:k + 1].broadcast_to([P, B, E]), le, ALU.is_gt))
                step(v.tensor_tensor(router[:, 2], router[:, 2], router[:, 3], ALU.add))
            step(v.tensor_scalar(router[:, 3], router[:, 2], 1.5, None, ALU.is_lt))
            step(v.tensor_tensor(router[:, 4], router[:, 3], le, ALU.mult))
            step(v.tensor_tensor(small[:, 3, :], top[:, :, 0], top[:, :, 1], ALU.add))
            step(v.reciprocal(small[:, 1, :], small[:, 3, :]))
            v.tensor_tensor(cw1[:], router[:, 4], small[:, 1, :].unsqueeze(2).broadcast_to([P, B, E]), ALU.mult).then_inc(S["gl_cw"], 1)
            dve.wait_ge(S["gl_cw"], 1)
            for g in range(NG):
                dve.wait_ge(S["wt_mm"], g + 1)
                v.tensor_copy(cwT[:, gb(g), :], bank(4 + g % 2)[0:E, 0, :].rearrange("p (b t) -> p b t", b=GB)).then_inc(S["wt_ev"], 1)
                dve.wait_ge(S["eb_mm"], g + 1)
                v.tensor_tensor(X[:, gb(g), :], X[:, gb(g), :], bank(6 + g % 2)[:, 0, :].rearrange("p (b d) -> p b d", b=GB),
                                ALU.add).then_inc(S["eb_res"], 1)
            dve.wait_ge(S["eb_res"], NG)
            for i in range(E * NG + 1):
                if i < E * NG:
                    if i >= 2:
                        dve.wait_ge(S["down1"], i - 1)
                    selu_sum(i, i % 2, "act1", "hid1")
                if i >= 1:
                    if i > NG:
                        dve.wait_ge(S["res1"], i - NG)
                    add_expert(i - 1, cw1, (i - 1) // NG, "down1", "res1")

        @block.tensor
        def _(pe):
            mm = nc.tensor.matmul

            def transpose_xn(i):
                for g in range(NG):
                    pe.wait_ge(S["ln_xn"], i * NG + g + 1)
                    for b in range(GB):
                        ins = nc.tensor.transpose(bank(g)[:, 0, b * T:(b + 1) * T], xn[:, g * GB + b, :], ident[:])
                    ins.then_inc(S["ln_tr"], 1)

            def down(i, ks, lhs, rhs, o, width=D):
                for b in range(GB):
                    for k in range(ks):
                        ins = mm(bank(o)[:, 0, b * width:(b + 1) * width], lhs(k, b), rhs(k), start=k == 0, stop=k == ks - 1)
                return ins

            def up(out, n, m, g):
                for k, (i, j) in enumerate(PARTS):
                    ins = mm(out, whl[:, wslot(n), i, m * P:(m + 1) * P], xhl[:, j, gcols(g)], start=k == 0, stop=k == 2)
                return ins

            pe.wait_ge(S["const"], 1)
            transpose_xn(0)
            pe.wait_ge(S["w_mamba"], 16 * 8)
            pe.wait_ge(S["w_split"], 1)
            for g in range(NG):
                pe.wait_ge(S["ln_lo"], g + 1)
                for m in range(4):
                    if g:
                        pe.wait_ge(S["in_silu"], 4 * g - 3 + m)
                    up(bank(4 + m)[:, 0, :], 0, m, g).then_inc(S["in_mm"], 1)
            for g in range(NG):
                pe.wait_ge(S["in_silu"], 4 * g + 4)
                for m in range(HI):
                    if g >= 2:
                        pe.wait_ge(S["dl_abs"], HI * (g - 2) + m + 1)
                        pe.wait_ge(S["dl_relu"], HI * (g - 2) + m + 1)
                    for k in range(HI):
                        ins = mm(bank(2 * (g % 2) + m)[:, 0, :], w["W_delta"][:, k, m * P:(m + 1) * P], uT[:, k, gcols(g)],
                                 start=k == 0, stop=k == HI - 1)
                    ins.then_inc(S["dl_mm"], 1)
            for g in range(NG):
                for k in range(HI):
                    ins = mm(bank(4 + g)[0:2 * NS, 0, :], w["W_BC"][:, k, :], uT[:, k, gcols(g)], start=k == 0, stop=k == HI - 1)
                ins.then_inc(S["bc_mm"], 1)
            pe.wait_ge(S["bc_split"], 1)
            pe.wait_ge(S["diag_ready"], HI)
            def broadcast(bank_i, r, g, s):
                mm(bank(bank_i)[:, 0, :], sel[:, r, :], bc3[:, gcols(g)],
                   start=True, stop=True).then_inc(S[s], 1)

            def b_ahead(n, g, i):
                pe.wait_ge(S["b_copied"], i + 2)
                broadcast(4, n, g, "b_bcast")

            def c_row(n, g, i):
                pe.wait_ge(S["hc"], i)
                broadcast(5, n + NS, g, "c_bcast")

            def y_sum(i, j, last=False):
                pe.wait_ge(S["hc"], i + 1)
                for m in range(HI):
                    ins = mm(bank(6 + m)[:, 0, :], ident[:], hC[:, j, m * GT:(m + 1) * GT], start=False, stop=last,
                             skip_group_check=True)
                ins.then_inc(S["y_acc"], 1)

            broadcast(4, 0, 0, "b_bcast")
            pe.wait_ge(S["b_copied"], 1)
            broadcast(4, 1, 0, "b_bcast")
            for g in range(NG):
                i0 = g * NS
                c_row(0, g, i0) if g else broadcast(5, NS, 0, "c_bcast")
                b_ahead(2, g, i0)
                if g:
                    pe.wait_ge(S["y_gated"], g)
                for m in range(HI):
                    mm(bank(6 + m)[:, 0, :], diagD[:, m, :], uT[:, m, gcols(g)], start=True, stop=False, skip_group_check=True)
                for n in range(1, NS):
                    c_row(n, g, i0 + n)
                    if n + 2 < NS:
                        b_ahead(n + 2, g, i0 + n)
                    elif g < NG - 1:
                        b_ahead(n + 2 - NS, g + 1, i0 + n)
                    y_sum(i0 + n - 1, (n - 1) % 2)
                y_sum(i0 + NS - 1, 1, last=True)
            for g in range(NG):
                pe.wait_ge(S["y_gated"], NG)
                down(g, HI, lambda k, b: yT[:, k, (g * GB + b) * T:(g * GB + b + 1) * T], lambda k: w["W_out"][:, k, :], g)\
                    .then_inc(S["a_out"], 1)
            transpose_xn(1)
            pe.wait_ge(S["w_ctx"], 16 * 6)
            for g in range(NG):
                pe.wait_ge(S["ln_xnT"], NG + g + 1)
                mm(bank(4 + g)[:, 0, :], w["Wq0"][:], xnT[:, gcols(g)], start=True, stop=True).then_inc(S["q_mm"], 1)
            for g in range(NG):
                mm(bank(g)[:, 0, 0:GB * LK], w["Wk0"][:], w["ctxT"][:, gb(g), :].rearrange("p b k -> p (b k)"),
                   start=True, stop=True).then_inc(S["k_mm"], 1)
            for g in range(NG):
                pe.wait_ge(S["q_ev"], g + 1)
                for b in range(GB):
                    ins = mm(bank(4 + g)[0:LK, 0, b * D:(b + 1) * D], w["ctxT"][:, g * GB + b, :], w["Wv0"][:], start=True, stop=True)
                ins.then_inc(S["v_mm"], 1)
            for g in range(NG):
                pe.wait_ge(S["k_ev"], g + 1)
                for b in range(GB):
                    bi = g * GB + b
                    ins = mm(bank(g)[:, 0, b * LK:(b + 1) * LK], qT[:, bi * T:(bi + 1) * T], kT[:, bi, :], start=True, stop=True)
                ins.then_inc(S["sc_mm"], 1)
            for g in range(NG):
                pe.wait_ge(S["sc_exp"], GB * (g + 1))
                pe.wait_ge(S["v_ev"], g + 1)
                for b in range(GB):
                    ins = nc.tensor.transpose(bank(4 + g)[0:LK, 0, b * T:(b + 1) * T], pr[:, g * GB + b, :], ident[:])
                ins.then_inc(S["pt_mm"], 1)
            for g in range(NG):
                pe.wait_ge(S["pt_ev"], g + 1)
                for b in range(GB):
                    ins = mm(bank(g)[:, 0, b * D:(b + 1) * D], prT[0:LK, g * GB + b, :], vS[0:LK, g * GB + b, :], start=True, stop=True)
                ins.then_inc(S["pv_mm"], 1)
            transpose_xn(2)
            for g in range(NG):
                pe.wait_ge(S["ln_xnT"], 2 * NG + g + 1)
                for b in range(g * GB, (g + 1) * GB):
                    ins = mm(bank(7)[:, 0, b * E:(b + 1) * E], xnT[:, b * T:(b + 1) * T], w["router0"][:], start=True, stop=True)
            ins.then_inc(S["rt_mm"], 1)
            for i in range((E + 1) * NG + 1):
                e, g = divmod(i, NG)
                if i < (E + 1) * NG:
                    if g == 0:
                        pe.wait_ge(S["w_split"], N_E0 + e + 1)
                    if i == 0:
                        pe.wait_ge(S["ln_lo"], 2 * NG)
                    for m in range(M0):
                        if i:
                            pe.wait_ge(S["silu0"], M0 * (i - 1) + m + 1)
                        up(bank(m)[:, 0, :], N_E0 + e, m, g)
                        if i:
                            pe.wait_ge(S["hid0"], M0 * (i - 1) + m + 1)
                        up(bank(2 + m)[:, 0, :], N_E0 + e, M0 + m, g).then_inc(S["up_mm"], 1)
                if i >= 1:
                    c = i - 1
                    pe.wait_ge(S["hid0"], M0 * (c + 1))
                    if c >= 2:
                        pe.wait_ge(S["res0"], c - 1)
                    sl = (c // NG) % 2
                    down(c, M0, lambda k, b: hidr[:, c % 2, k * GT + b * T:k * GT + (b + 1) * T],
                         lambda k: ew0[:, sl, 2, k * D:(k + 1) * D], 4 + c % 2).then_inc(S["down0"], 1)
            transpose_xn(3)
            pe.wait_ge(S["w_lru"], 16 * 6)
            pe.wait_ge(S["w_split"], N_WIN1 + 1)

            def xz(g):
                pe.wait_ge(S["ln_lo"], 2 * NG + g + 1)
                for m in range(4):
                    if g:
                        pe.wait_ge(S["xz_ev"], 4 * g - 3 + m)
                    up(bank(4 + m)[:, 0, :], N_WIN1, m, g).then_inc(S["xz_mm"], 1)

            def lam_or_v(g, wt, banks, done, freed):
                for m in range(HI):
                    if freed[m][1] > 0:
                        pe.wait_ge(S[freed[m][0]], freed[m][1])
                    for k in range(HI):
                        ins = mm(bank(banks[m])[:, 0, :], wt[:, k, m * P:(m + 1) * P], xi[:, k, gcols(g)],
                                 start=k == 0, stop=k == HI - 1)
                    ins.then_inc(S[done], 1)

            def v_dot_v(g):
                pe.wait_ge(S["sq_done"], g + 1)
                if g:
                    pe.wait_ge(S["vv_read"], g)
                for k in range(HI):
                    ins = mm(bank(3)[:, 0, :], ones[:], sq[:, k, gcols(g)], start=k == 0, stop=k == HI - 1)
                ins.then_inc(S["vv_mm"], 1)

            xz(0)
            for g in range(NG):
                if g + 1 < NG:
                    xz(g + 1)
                pe.wait_ge(S["xz_ev"], 4 * g + HI)
                if g == 0:
                    pe.wait_ge(S["ln_lo"], 3 * NG)
                lam_or_v(g, w["Wl"], (0, 1), "l_mm", (("v2_ev", HI * g), ("l_ev", HI * g)))
                lam_or_v(g, w["Wv"], (2, 0), "v2_mm", (("v2_ev", HI * g - 1), ("l_ev", HI * g + 1)))
                v_dot_v(g)
            pe.wait_ge(S["dots_in"], 2 * NG)
            for first, lhs, buf in ((0, nones, vb), (4, ones, vw)):
                for r in range(4):
                    for k in range(HI):
                        rhs = buf[:, k, :].rearrange("p (b c r) -> p r c b", b=B, r=4)[:, r]
                        ins = mm(bank(first + r)[:, 0, :].rearrange("p (c b) -> p c b", b=B), lhs[:], rhs, start=k == 0, stop=k == HI - 1)
            ins.then_inc(S["r_dot"], 1)

            def dot(t, k):
                pe.wait_ge(S["r_lm"], t - 1)
                for h in range(HI):
                    ins = mm(ps[:, k % 4, bass.ds(col(t, k), B)], ones[:], lm[:, k % 2, 1, h, :], start=False, stop=h == HI - 1,
                             skip_group_check=True)
                ins.then_inc(S["r_dot"], 1)

            with pe.Fori(0, T - 2 * UR + 1, UR) as t0:
                for k in range(2, UR + 2):
                    dot(t0 + k, k)
            for t in range(T - UR + 2, T):
                dot(t, t % UR)
            for g in range(NG):
                pe.wait_ge(S["g1_ready"], g + 1)
                down(g, HI, lambda k, b: nb[:, k, (g * GB + b) * T:(g * GB + b + 1) * T], lambda k: w["Wout1"][:, k, :], g)\
                    .then_inc(S["d_out"], 1)
            pe.wait_ge(S["w_att"], 16 * 6)
            for g in range(NG):
                mm(bank(4 + g)[:, 0, 0:GB * LK], w["Wk1"][:], w["ctxT"][:, gb(g), :].rearrange("p b k -> p (b k)"),
                   start=True, stop=True).then_inc(S["hk_mm"], 1)
            for g in range(NG):
                pe.wait_ge(S["hk_ev"], g + 1)
                for b in range(GB):
                    ins = mm(bank(4 + g)[0:LK, 0, b * D:(b + 1) * D], w["ctxT"][:, g * GB + b, :], w["Wv1"][:], start=True, stop=True)
                ins.then_inc(S["hv_mm"], 1)
            pe.wait_ge(S["hv_ev"], 1)
            mm(bank(4)[:, 0, 0:P], ones[0:1, :], w["bo1"][:], start=True, stop=True).then_inc(S["bo_mm"], 1)
            pe.wait_ge(S["hv_ev"], NG)
            pe.wait_ge(S["bo_ev"], 1)
            transpose_xn(4)
            for g in range(NG):
                pe.wait_ge(S["ln_xnT"], 4 * NG + g + 1)
                mm(bank(4 + g)[:, 0, :], w["Wq1"][:], xnT[:, gcols(g)], start=True, stop=True).then_inc(S["hq_mm"], 1)

            def head_scores(b, q):
                pe.wait_ge(S["kz_ready"], b + 1)
                for r in range(2 * q, 2 * q + 2):
                    rows = slice(32 * r, 32 * r + 32)
                    for n, (i, j) in enumerate(((0, 0), (0, 1), (1, 0))):
                        ins = mm(bank(r)[:, 0, 0:HQ * LK], qhl[rows, i, b * T:(b + 1) * T], kz[rows, b % 2, j, :],
                                 start=n == 0, stop=n == 2)
                ins.then_inc(S["hs_mm"], 1)

            def head_values(b):
                pe.wait_ge(S["ht_ev"], 2 * b + 2)
                pe.wait_ge(S["vz_ready"], b + 1)
                if b:
                    pe.wait_ge(S["ho_ev"], b)
                for j in range(HQ):
                    ins = mm(bank(6)[:, 0, :].rearrange("p (r q) -> p r q", r=4), vz[0:LK, b % 2, j, :],
                             n1T[0:LK].rearrange("p (r j) q -> p j r q", j=HQ)[:, j], start=j == 0, stop=j == HQ - 1)
                ins.then_inc(S["ho_mm"], 1)

            def head_out(b):
                pe.wait_ge(S["ho_ev"], b + 1)
                if b:
                    pe.wait_ge(S["hw_res"], b)
                mm(bank(7)[:, 0, 0:P], oT, w["Wo1"][:], start=True, stop=True).then_inc(S["hw_mm"], 1)

            pe.wait_ge(S["hq_lo"], NG)
            head_scores(0, 0)
            head_scores(0, 1)
            for b in range(B):
                for q in range(2):
                    if b < B - 1:
                        pe.wait_ge(S["hs_sub"], 2 * b + q + 1)
                        head_scores(b + 1, q)
                    if b:
                        head_out(b - 1) if q else head_values(b - 1)
                    pe.wait_ge(S["hs_norm"], 2 * b + q + 1)
                    if 2 * b + q:
                        pe.wait_ge(S["ht_ev"], 2 * b + q)
                    for h in range(8):
                        ins = nc.tensor.transpose(bank(4 + h // 4)[0:LK, 0, (h % 4) * T:(h % 4 + 1) * T], n1[:, 8 * q + h, :], ident[:])
                    ins.then_inc(S["ht_mm"], 1)
            head_values(B - 1)
            head_out(B - 1)
            transpose_xn(5)
            pe.wait_ge(S["w_gate"], 16 * 6)

            def logits(g):
                pe.wait_ge(S["g_hid"], g + 1)
                for b in range(GB):
                    o = bank(4 + g)[:, 0, b * D:(b + 1) * D]
                    for m in range(M1):
                        mm(o, G[:, 2, g % 2, m * GT + b * T:m * GT + (b + 1) * T], w["gate_wo"][:, m, :], start=m == 0, stop=False)
                    ins = mm(o, ones[0:1, :], w["gate_bo"][:], start=False, stop=True)
                ins.then_inc(S["gl_mm"], 1)

            pe.wait_ge(S["w_split"], N_GATE + 1)
            for g in range(NG):
                if g == 0:
                    pe.wait_ge(S["ln_lo"], 4 * NG)
                for m in range(M1):
                    if g:
                        pe.wait_ge(S["g_act"], M1 * (g - 1) + m + 1)
                    up(bank(m)[:, 0, :], N_GATE, m, g).then_inc(S["gu_mm"], 1)
                if g:
                    logits(g - 1)
            logits(NG - 1)
            pe.wait_ge(S["gl_cw"], 1)
            for g in range(NG):
                if g >= 2:
                    pe.wait_ge(S["wt_ev"], g - 1)
                for b in range(GB):
                    ins = nc.tensor.transpose(bank(4 + g % 2)[0:E, 0, b * T:(b + 1) * T], cw1[:, g * GB + b, :], ident[:])
                ins.then_inc(S["wt_mm"], 1)
                pe.wait_ge(S["wt_ev"], g + 1)
                if g >= 2:
                    pe.wait_ge(S["eb_res"], g - 1)
                for b in range(GB):
                    ins = mm(bank(6 + g % 2)[:, 0, b * D:(b + 1) * D], cwT[:, g * GB + b, :], w["exp_bo"][:], start=True, stop=True)
                ins.then_inc(S["eb_mm"], 1)
            for i in range(E * NG + 1):
                e, g = divmod(i, NG)
                if i < E * NG:
                    if g == 0:
                        pe.wait_ge(S["w_split"], N_E1 + e + 1)
                    for m in range(M1):
                        if i:
                            pe.wait_ge(S["act1"], M1 * (i - 1) + m + 1)
                        else:
                            pe.wait_ge(S["g_act"], M1 * NG)
                        up(bank(m)[:, 0, :], N_E1 + e, m, g).then_inc(S["up1_mm"], 1)
                if i >= 1:
                    c = i - 1
                    pe.wait_ge(S["hid1"], c + 1)
                    if c >= 2:
                        pe.wait_ge(S["res1"], c - 1)
                    sl = (c // NG) % 2
                    down(c, M1, lambda k, b: G[:, 2, c % 2, k * GT + b * T:k * GT + (b + 1) * T],
                         lambda k: ew1[:, sl, 1, k * D:(k + 1) * D], 4 + c % 2).then_inc(S["down1"], 1)


def kernel(**inputs):
    import numpy as _np
    import concourse.bacc as _bacc
    from concourse import mybir as _mybir
    from concourse.bass_utils import run_bass_kernel_spmd as _run

    I = {k: _np.asarray(v) for k, v in inputs.items()}
    ctx = _np.ones((DC + 1, B, LK), _np.float32)
    ctx[0:DC] = I["ctx_512"].transpose(2, 0, 1)
    lay = {"x": I["x"], "ctxT": ctx}
    for name in ("W_in", "W_delta", "b_delta", "A_log", "D_param", "W_out"):
        lay[name] = I["L0_attn_" + name]
    lay["W_BC"] = _np.concatenate([I["L0_attn_W_B"], I["L0_attn_W_C"]], 1)
    for l, x in ((0, "L0_xattn_"), (1, "L1_xattn_")):
        lay[f"Wq{l}"], lay[f"bq{l}"] = I[x + "Wq"], I[x + "bq"]
        lay[f"Wk{l}"] = _np.concatenate([I[x + "Wk"], I[x + "bk"][None]], 0)
        lay[f"Wv{l}"] = _np.concatenate([I[x + "Wv"], I[x + "bv"][None]], 0)
    lay["Wo1"], lay["bo1"] = I["L1_xattn_Wo"], I["L1_xattn_bo"]
    lay["router0"] = I["L0_ffn_w_router"]
    for name in ("w1", "w3", "w2", "sw1", "sw3", "sw2"):
        lay[name] = I["L0_ffn_" + name]
    lay["omega"] = I["L1_attn_omega"].reshape(DI)
    lay["bl"], lay["bv"] = I["L1_attn_bl"], I["L1_attn_bv"]
    for name, src in (("Win1", "Win"), ("Wl", "Wl"), ("Wv", "Wv"), ("Wout1", "Wout")):
        lay[name] = I["L1_attn_" + src].T
    for name in ("gate_wi", "gate_bi", "gate_wo", "gate_bo", "exp_wi", "exp_wo", "exp_bo"):
        lay[name] = I["L1_ffn_" + name]
    lay["exp_bi"] = I["L1_ffn_exp_bi"].reshape(E, M1, P).transpose(2, 0, 1)

    for name in ("b_delta", "D_param", "omega", "bl", "bv", "bq0", "bq1", "gate_bi"):
        lay[name] = lay[name].reshape(-1, P).T

    nc = _bacc.Bacc("TRN2", target_bir_lowering=False, num_devices=1)
    arrays, args = {}, {}
    for name, v in lay.items():
        v = _np.ascontiguousarray(v)
        arrays[f"in_{name}_dram"] = v
        args[name] = nc.dram_tensor(f"in_{name}_dram", v.shape, _mybir.dt.from_np(v.dtype), kind="ExternalInput").ap()
    res = nc.dram_tensor("out_0_dram", (B, T, D), F32, kind="ExternalOutput").ap()
    decoder_program(nc, args, res)
    r = _run(nc, [arrays], core_ids=[0])
    return r.results[0]["out_0_dram"]
```

```python
from concourse import mybir
from contextlib import ExitStack

F32 = mybir.dt.float32
BF16 = mybir.dt.bfloat16
F32R = mybir.dt.float32r
ALU = mybir.AluOpType
ACT = mybir.ActivationFunctionType
AX = mybir.AxisListType

P = 128
B, T, D = 16, 128, 128
N = B * T
GB = 4
NG = B // GB
GT = GB * T
DI = 256
HI = DI // P
NS = 16
LK, DC = 120, 64
E = 8
M0 = 256 // P
M1 = 512 // P
NH, DK = 16, 8
HQ = 4
EPS = 1e-5
SELU_L = 1.0507009873554805
SELU_A = 1.6732632423543772
SELU_LA = SELU_L * SELU_A
EB = 8


def decoder_program(nc, a, out):
    with ExitStack() as ctx:
        def sb(name, shape, dt=F32):
            return ctx.enter_context(nc.sbuf_tensor(name, shape, dt))

        def sem(name):
            return ctx.enter_context(nc.semaphore(name))

        ps = ctx.enter_context(nc.psum_tensor("ps", [P, 8, GT], F32))
        X = sb("X", [P, B, D])
        LN = sb("LN", [P, 2, N])
        xn = LN[:, 0, :].rearrange("p (b d) -> p b d", b=B)
        xnT = LN[:, 1, :]
        stats = sb("stats", [P, B, 6])
        mv = sb("mv", [P, B, 2])
        rstd = sb("rstd", [P, B])
        nmean, shift = stats[:, :, 0], stats[:, :, 1]
        mhalf = sb("mhalf", [P, B])
        ident = sb("ident", [P, P])
        ones = sb("ones", [P, P])
        sel = sb("sel", [3 * 32, 32, P], BF16)
        bc3 = sb("bc3", [3 * 32, N], BF16)
        hmask = sb("hmask", [P, HQ])
        negA = sb("negA", [P, HI, NS])
        diagD = sb("diagD", [P, HI, P])
        router = sb("router", [P, 6, B, E])
        cw0 = sb("cw0", [P, B, E + 1])
        cw1 = sb("cw1", [P, B, E])
        small = sb("small", [P, 4, B])
        coef = sb("coef", [P, 4, HI])
        ebs = sb("ebs", [P, E + 1, M1])
        nones = diagD[:, 0, :]
        lm = sb("lm", [P, 2, 2, HI, B])
        grec = sb("grec", [P, 2, HI, B])
        rrec = sb("rrec", [P, HI, B])
        sdot = sb("sdot", [P, B])
        acc = sb("acc", [P, B])

        w = {}
        for name, shape in (
            ("W_in", [P, 4, P]), ("W_delta", [P, HI, DI]), ("b_delta", [P, HI]), ("W_BC", [P, HI, 2 * NS]),
            ("A_log", [P, HI, NS]), ("D_param", [P, HI]), ("W_out", [P, HI, D]),
            ("Wq0", [P, P]), ("bq0", [P, 1]), ("Wk0", [DC + 1, P]), ("Wv0", [DC + 1, P]), ("ctxT", [DC + 1, B, LK]),
            ("router0", [P, E]),
            ("omega", [P, HI]), ("Win1", [P, 4, P]), ("Wl", [P, HI, DI]), ("bl", [P, HI]), ("Wv", [P, HI, DI]),
            ("bv", [P, HI]), ("Wout1", [P, HI, D]),
            ("Wq1", [P, P]), ("bq1", [P, 1]), ("Wk1", [DC + 1, P]), ("Wv1", [DC + 1, P]), ("Wo1", [P, P]),
            ("bo1", [1, P]),
            ("gate_wi", [P, M1, P]), ("gate_bi", [P, M1]), ("gate_wo", [P, M1, D]), ("gate_bo", [1, D]),
            ("exp_bi", [P, E, M1]), ("exp_bo", [E, P]),
        ):
            w[name] = sb("w_" + name, shape)
        ew0 = sb("ew0", [P, 2, 3, M0 * P])
        with nc.sbuf_tensor("R", [P, 4, 2, 2 * GT], F32) as R:
            pass
        sb("over_R0", [P, 2, 2 * GT])
        xhl = sb("xhl", [P, 2, N], F32R)
        whl = sb("whl", [P, 2, 2, GT], F32R)
        with nc.sbuf_tensor("G", [P, 6, HI, N], F32) as G:
            pass
        qhl = sb("qhl", [P, HI, N], F32R)
        sb("over_G1_to_G4", [P, 4, HI, N])
        kz = sb("kz", [P, 2, 2, HQ * LK], F32R)
        ew1 = R[:, 0, :, :].rearrange("p s (w n) -> p s w n", w=2)

        S = {}
        for name in (
            "x_in0", "x_in1", "x_in2", "x_in3", "w_mamba", "w_ctx", "w_lru", "w_att", "w_gate",
            "w_e0a", "w_e0b", "w_e1a", "w_e1b", "out_sent",
            "const", "const_rest", "dve_step", "act_step", "pool_step",
            "ln_stats", "ln_scale", "ln_xn_a", "ln_xn_b", "ln_tr", "ln_xnT", "ln_lo", "w_upper", "w_split",
            "in_mm", "in_silu", "dl_mm", "dl_abs", "dl_exp", "dl_relu", "dl_ln", "dl_done", "bc_mm", "bc_split",
            "diag_ready", "b_bcast", "c_bcast", "decay", "b_copied", "drive", "scanned", "hc", "y_acc", "y_gated", "a_out", "a_res",
            "q_mm", "q_ev", "k_mm", "k_ev", "v_mm", "v_ev", "sc_mm", "sc_max", "sc_exp", "pt_mm", "pt_ev", "pv_mm", "pv_res",
            "rt_mm", "rt_sub", "rt_exp", "rt_cw", "up_mm", "silu0", "hid0", "down0", "res0",
            "xz_mm", "xz_ev", "l_mm", "l_ev", "v2_mm", "v2_ev", "lam_done", "z_silu", "sq_done", "vv_mm", "vv_read", "nb_done",
            "w_done", "dots_in", "dots_sum", "vl_done", "r_dot", "r_s", "r_r", "r_acc", "r_g", "r_h", "r_lm", "g1_ready", "d_out", "d_res",
            "hq_mm", "hq_ev", "hq_lo", "hk_mm", "hk_ev", "hk_lo", "hv_mm", "hv_ev", "bo_mm", "bo_ev", "bo_add", "kz_ready", "vz_ready",
            "hs_mm", "hs_sub", "hs_exp", "hs_inv", "hs_norm", "ht_mm", "ht_ev", "ho_mm", "ho_ev", "hw_mm", "hw_res",
            "gu_mm", "g_act", "g_hid", "gl_mm", "gl_read", "gl_cw", "wt_mm", "wt_ev", "eb_mm", "eb_res",
            "up1_mm", "act1", "hid1", "down1", "res1", "coef_done", "coef_sp", "omega_ln",
        ):
            S[name] = sem(name)

        class Chain:

            def __init__(self, eng, s):
                self.eng, self.s, self.n = eng, s, 0

            def __call__(self, ins):
                self.n += 1
                ins.then_inc(self.s, 1)
                self.eng.wait_ge(self.s, self.n)

        block = ctx.enter_context(nc.Block())

        SPLIT = (0, 2, 3, 5)
        PARTS = ((0, 0), (0, 1), (1, 0))
        ln_bank = lambda i, g: g + 4 * (i == 5)
        wslot = lambda n: (n + 1) % 2
        N_E0, N_WIN1, N_GATE, N_E1 = 1, E + 2, E + 3, E + 4

        gcols = lambda g: slice(g * GT, (g + 1) * GT)
        gb = lambda g: slice(g * GB, (g + 1) * GB)
        GBUF = lambda i: G[:, i, :, :]

        uT, zT, dT, duT = (GBUF(i) for i in range(4))
        yT = GBUF(4)
        tmpT = GBUF(5)
        dBu = R[:, 0, :, :]
        hst = R[:, 1, :, :]
        hC = R[:, 2, :, :]
        Bsb = R[:, 3, :, :].rearrange("p s (i n) -> p (s i) n", n=GT)
        qT = G[:, 0, 0, :]
        kT = G[:, 0, 1, 0:B * LK].rearrange("p (b k) -> p b k", b=B)
        vS = G[:, 1, 0, :].rearrange("p (b d) -> p b d", b=B)
        pr = G[:, 1, 1, 0:B * LK].rearrange("p (b k) -> p b k", b=B)
        prT = G[:, 2, 0, :].rearrange("p (b q) -> p b q", b=B)
        sh = G[:, 3, :, :].rearrange("p h (s n) -> p (h s) n", n=2 * GT)
        hidr = G[:, 4, :, :].rearrange("p h (s n) -> p (h s) n", n=2 * GT)
        pair = G[:, 5, 0, 0:B * E * E].rearrange("p (b e f) -> p b e f", b=B, e=E)
        top = G[:, 3, 1, 0:B * 8].rearrange("p (b k) -> p b k", b=B)
        cwT = G[0:E, 5, 1, :].rearrange("p (b t) -> p b t", b=B)
        xi, z1, lam, vv, nb, ww = (GBUF(i) for i in range(6))
        vb = LN[:]
        vw = R[:, 1:3, :, :].rearrange("p h s n -> p h (s n)")
        rvv = R[:, 3, :, :].rearrange("p s n -> p (s n)")
        at = lambda buf, t: buf.rearrange("p h (b t) -> p h b t", b=B)[:, :, :, t]
        slot = lambda first, t: ps[:, first + t % 4, t // 4 * B:(t // 4 + 1) * B]
        sq = LN
        khl = R[:, 2:4, :, :].rearrange("p i s n -> p i (s n)")[:, :, 0:B * LK].rearrange("p i (b k) -> p i b k", b=B)
        v1S = G[:, 1, 0, :].rearrange("p (b d) -> p b d", b=B)
        p1 = G[:, 2, 0, 0:NH * LK].rearrange("p (h k) -> p h k", h=NH)
        e1 = G[:, 2, 1, 0:NH * LK].rearrange("p (h k) -> p h k", h=NH)
        n1 = G[:, 3, 0, 0:NH * LK].rearrange("p (h k) -> p h k", h=NH)
        n1T = G[:, 3, 1, :].rearrange("p (h q) -> p h q", h=NH)
        vz = G[:, 4, 0, 0:2 * HQ * P].rearrange("p (s j c) -> p s j c", s=2, j=HQ)
        oT = G[:, 4, 1, 0:P]
        bo_b = G[:, 4, 1, P:2 * P]

        def bank(i, n=1):
            return ps[:, i:i + n, :]

        @block.sync
        def _(sp):
            for g in range(NG):
                sp.dma_start(X[:, gb(g), :], a["x"].rearrange("b t d -> t b d")[:, gb(g), :]).then_inc(S[f"x_in{g}"], 16)
            half = lambda ap: ap.rearrange("(k p) n -> p k n", p=P)
            row = lambda ap: ap.rearrange("(o n) -> o n", o=1)
            tiles = lambda ap: ap.rearrange("p (m n) -> p m n", n=P)

            def load(s, pairs):
                for name, src in pairs:
                    sp.dma_start(w[name][:], src).then_inc(S[s], 16)

            load("w_mamba", (("W_in", tiles(a["W_in"])), ("W_delta", half(a["W_delta"])), ("b_delta", a["b_delta"]),
                             ("W_BC", half(a["W_BC"])), ("A_log", half(a["A_log"])), ("D_param", a["D_param"]),
                             ("W_out", half(a["W_out"])), ("omega", a["omega"])))
            load("w_ctx", (("ctxT", a["ctxT"]), ("Wq0", a["Wq0"]), ("bq0", a["bq0"]), ("Wk0", a["Wk0"]),
                           ("Wv0", a["Wv0"]), ("router0", a["router0"])))
            load("w_lru", (("Win1", tiles(a["Win1"])), ("Wl", half(a["Wl"])), ("bl", a["bl"]),
                           ("Wv", half(a["Wv"])), ("bv", a["bv"]), ("Wout1", half(a["Wout1"]))))
            load("w_att", (("Wq1", a["Wq1"]), ("bq1", a["bq1"]), ("Wk1", a["Wk1"]), ("Wv1", a["Wv1"]),
                           ("Wo1", a["Wo1"]), ("bo1", row(a["bo1"]))))
            load("w_gate", (("gate_wi", tiles(a["gate_wi"])), ("gate_bi", a["gate_bi"]),
                            ("gate_wo", half(a["gate_wo"])), ("gate_bo", row(a["gate_bo"])),
                            ("exp_bi", a["exp_bi"]), ("exp_bo", a["exp_bo"])))

            def expert0(slot, s, w1, w3, w2):
                sp.dma_start(ew0[:, slot, 0, :], w1).then_inc(S[s], 16)
                sp.dma_start(ew0[:, slot, 1, :], w3).then_inc(S[s], 16)
                sp.dma_start(ew0[:, slot, 2, :].rearrange("p (m n) -> p m n", m=M0), half(w2)).then_inc(S[s], 16)

            expert0(0, "w_e0a", a["w1"][0], a["w3"][0], a["w2"][0])
            expert0(1, "w_e0b", a["w1"][1], a["w3"][1], a["w2"][1])
            for e in range(2, E + 1):
                sp.wait_ge(S["down0"], NG * (e - 1))
                if e < E:
                    expert0(e % 2, "w_e0b" if e % 2 else "w_e0a", a["w1"][e], a["w3"][e], a["w2"][e])
                else:
                    expert0(0, "w_e0a", a["sw1"], a["sw3"], a["sw2"])

            def expert1(slot, s, e):
                sp.dma_start(ew1[:, slot, 0, :], a["exp_wi"][e]).then_inc(S[s], 16)
                sp.dma_start(ew1[:, slot, 1, :].rearrange("p (m n) -> p m n", m=M1), half(a["exp_wo"][e])).then_inc(S[s], 16)

            sp.wait_ge(S["y_gated"], NG)
            for e in range(E):
                if e >= 2:
                    sp.wait_ge(S["down1"], NG * (e - 1))
                expert1(e % 2, "w_e1b" if e % 2 else "w_e1a", e)
            for g in range(NG):
                sp.wait_ge(S["res1"], NG * (E - 1) + g + 1)
                sp.dma_start(out.rearrange("b t d -> t b d")[:, gb(g), :], X[:, gb(g), :]).then_inc(S["out_sent"], 16)
            sp.wait_ge(S["out_sent"], 16 * NG)

        @block.gpsimd
        def _(pool):
            step = Chain(pool, S["pool_step"])
            gp = nc.gpsimd

            def ln_scale(i, groups=range(NG)):
                for g in groups:
                    pool.wait_ge(S["ln_stats"], i * NG + g + 1)
                    step(gp.tensor_tensor(rstd[:, gb(g)], small[:, 0, gb(g)], mhalf[:, gb(g)], ALU.pow))
                    gp.tensor_tensor(shift[:, gb(g)], nmean[:, gb(g)], rstd[:, gb(g)], ALU.mult).then_inc(S["ln_scale"], 1)

            def split(n, src):
                step(gp.tensor_copy(whl[:, wslot(n), 0], src))
                gp.tensor_tensor(whl[:, wslot(n), 1], src, whl[:, wslot(n), 0].bitcast(F32), ALU.subtract).then_inc(S["w_split"], 1)

            step(gp.memset(mhalf[:], -0.5))
            step(gp.memset(ident[:], 0.0))
            gp.affine_select(out=ident[:], in_=ident[:], compare_op=ALU.not_equal, fill=1.0, base=0,
                             pattern=[[-1, P]], channel_multiplier=1).then_inc(S["const"], 1)
            ln_scale(0)
            gp.memset(ones[:], 1.0)
            step(gp.memset(sel[:], 0.0))
            for k in range(3):
                part = sel[32 * k:32 * k + 32, :, :]
                step(gp.affine_select(out=part, in_=part, compare_op=ALU.not_equal, fill=1.0, base=0,
                                      pattern=[[-1, 32], [0, P]], channel_multiplier=1))
            gp.memset(cw0[:], 1.0)
            step(gp.memset(hmask[:], 1.0))
            for r in range(P // 32):
                part = hmask[32 * r:32 * r + 32, :]
                step(gp.affine_select(out=part, in_=part, compare_op=ALU.is_ge, fill=0.0, base=0,
                                      pattern=[[-DK, HQ]], channel_multiplier=1))
                step(gp.affine_select(out=part, in_=part, compare_op=ALU.is_ge, fill=0.0, base=DK - 1,
                                      pattern=[[DK, HQ]], channel_multiplier=-1))
            gp.memset(cw1[:], 0.0).then_inc(S["const_rest"], 1)
            for g in range(NG):
                pool.wait_ge(S["dl_done"], 2 * g + 2)
                for n in range(NS):
                    i, j = g * NS + n, n % 2
                    pool.wait_ge(S["b_copied"], i + 1)
                    if i >= 2:
                        pool.wait_ge(S["scanned"], i - 1)
                    gp.tensor_tensor(
                        dBu[:, j, :].rearrange("p (h n) -> p h n", h=HI), duT[:, :, gcols(g)],
                        Bsb[:, i % 4:i % 4 + 1, :].broadcast_to([P, HI, GT]), ALU.mult).then_inc(S["drive"], 1)
            step(gp.memset(nones[:], -1.0))
            ln_scale(1)

            def split_e0(e):
                pool.wait_ge(S["w_e0b" if e % 2 else "w_e0a"], 48 * (e // 2 + 1))
                if e >= 2:
                    pool.wait_ge(S["up_mm"], M0 * NG * (e - 1))
                split(N_E0 + e, ew0[:, e % 2, 0:2].rearrange("p w n -> p (w n)"))

            split_e0(0)
            split_e0(1)
            ln_scale(2)
            for e in range(2, E + 1):
                split_e0(e)
            pool.wait_ge(S["w_lru"], 16 * 6)
            pool.wait_ge(S["up_mm"], M0 * NG * E)
            split(N_WIN1, w["Win1"][:].rearrange("p m n -> p (m n)"))
            ln_scale(3)
            tok = lambda buf, g: buf[:, :, gcols(g)].rearrange("p h (b t) -> p h b t", b=GB)
            for g in range(NG):
                for buf, src, ready in ((vb, nb, "vv_mm"), (vw, ww, "w_done")):
                    pool.wait_ge(S[ready], g + 1)
                    if buf is vb:
                        pool.wait_ge(S["nb_done"], g + 1)
                    gp.memset(tok(buf, g)[:, 0, :, 0:1], 0.0)
                    gp.tensor_tensor(tok(buf, g)[:, :, :, 1:T], tok(vv, g)[:, :, :, 1:T], tok(src, g)[:, :, :, 0:T - 1],
                                     ALU.mult).then_inc(S["dots_in"], 1)
                    pool.wait_ge(S["dots_in"], 2 * g + (1 if buf is vb else 2))
                    gp.tensor_tensor(tok(buf, g)[:, 0, :, 1:T], tok(buf, g)[:, 0, :, 1:T], tok(buf, g)[:, 1, :, 1:T], ALU.add)\
                        .then_inc(S["dots_sum"], 1)

            def add_drive(t):
                pool.wait_ge(S["r_lm"], t)
                gp.tensor_tensor(grec[:, t % 2], lm[:, (t - 1) % 2, 0], at(nb, t), ALU.subtract).then_inc(S["r_g"], 1)

            for t in range(1, T):
                add_drive(t)
            ln_scale(4)
            pool.wait_ge(S["d_out"], NG)
            step(gp.memset(vz, 0.0))

            def keys(b):
                if b >= 2:
                    pool.wait_ge(S["hs_mm"], 2 * (b - 1))
                for i in range(2):
                    ins = gp.tensor_tensor(kz[:, b % 2, i, :].rearrange("p (j k) -> p j k", j=HQ),
                                           khl[:, i, b, :].unsqueeze(1).broadcast_to([P, HQ, LK]),
                                           hmask[:].unsqueeze(2).broadcast_to([P, HQ, LK]), ALU.mult)
                ins.then_inc(S["kz_ready"], 1)

            pool.wait_ge(S["hk_lo"], NG)
            keys(0)
            pool.wait_ge(S["bo_ev"], 1)
            pool.wait_ge(S["ln_xn_a"], 5 * NG)
            pool.wait_ge(S["ln_xn_b"], 5 * NG)
            gp.tensor_tensor(X[:], X[:], bo_b.unsqueeze(1).broadcast_to([P, B, D]), ALU.add).then_inc(S["bo_add"], 1)
            for b in range(B):
                if b + 1 < B:
                    keys(b + 1)
                if b >= 2:
                    pool.wait_ge(S["ho_mm"], b - 1)
                for j in range(HQ):
                    ins = gp.tensor_copy(vz[0:LK, b % 2, j].rearrange("p (r i d) -> p r i d", r=4, i=HQ)[:, :, j, :],
                                         v1S[0:LK, b, :].rearrange("p (r i d) -> p r i d", r=4, i=HQ)[:, :, j, :])
                ins.then_inc(S["vz_ready"], 1)
                for q in range(2):
                    hh = slice(8 * q, 8 * q + 8)
                    pool.wait_ge(S["hs_inv"], 2 * b + q + 1)
                    if b:
                        pool.wait_ge(S["ht_mm"], 2 * b - 1 + q)
                    if q == 0 and b % GB == GB - 2 and b > GB:
                        ln_scale(5, (b // GB - 1,))
                    gp.tensor_tensor(n1[:, hh, :], e1[:, hh, :], small[:, 3, hh].unsqueeze(2).broadcast_to([P, 8, LK]), ALU.mult)\
                        .then_inc(S["hs_norm"], 1)
            pool.wait_ge(S["w_gate"], 16 * 6)
            split(N_GATE, w["gate_wi"][:].rearrange("p m n -> p (m n)"))

            def split_e1(e):
                pool.wait_ge(S["w_e1b" if e % 2 else "w_e1a"], 32 * (e // 2 + 1))
                if e >= 2:
                    pool.wait_ge(S["up1_mm"], M1 * NG * (e - 1))
                elif e == 1:
                    pool.wait_ge(S["gu_mm"], M1 * NG)
                split(N_E1 + e, ew1[:, e % 2, 0])

            ln_scale(5, (NG - 1,))
            for e in range(E):
                split_e1(e)

        @block.scalar
        def _(act):
            sc = nc.scalar
            step = Chain(act, S["act_step"])

            def normalize(i, g):
                act.wait_ge(S["ln_scale"], i * NG + g + 1)
                for b in range(g * GB, g * GB + GB // 2):
                    ins = sc.activation(xn[:, b, :], X[:, b, :], ACT.Identity, scale=rstd[:, b:b + 1], bias=shift[:, b:b + 1])
                ins.then_inc(S["ln_xn_a"], 1)

            def copy_xnT(i, g):
                act.wait_ge(S["ln_tr"], i * NG + g + 1)
                src = bank(ln_bank(i, g))[:, 0, :]
                if i == 2:
                    sc.copy(xnT[:, gcols(g)], src)
                sc.copy((xhl[:, 0] if i in SPLIT else xnT)[:, gcols(g)], src).then_inc(S["ln_xnT"], 1)

            def layer_norm(i):
                for g in range(NG + 1):
                    if g < NG:
                        normalize(i, g)
                    if g:
                        copy_xnT(i, g - 1)

            for g in range(NG):
                normalize(0, g)
                if 1 <= g < NG - 1:
                    copy_xnT(0, g - 1)
                if g == 1:
                    act.wait_ge(S["w_mamba"], 16 * 8)
                    sc.copy(whl[:, wslot(0), 0], w["W_in"][:].rearrange("p m n -> p (m n)")).then_inc(S["w_upper"], 1)
            for g in range(NG):
                if g >= 1 and g + 1 < NG:
                    copy_xnT(0, g + 1)
                for m in range(4):
                    act.wait_ge(S["in_mm"], 4 * g + m + 1)
                    dst = uT if m < HI else zT
                    sc.activation(dst[:, m % HI, gcols(g)], bank(4 + m)[:, 0, :], ACT.Silu).then_inc(S["in_silu"], 1)
            for g in range(NG):
                for m in range(HI):
                    act.wait_ge(S["dl_mm"], HI * g + m + 1)
                    sc.activation(tmpT[:, m, gcols(g)], bank(2 * (g % 2) + m)[:, 0, :], ACT.Abs,
                                  bias=w["b_delta"][:, m:m + 1]).then_inc(S["dl_abs"], 1)
                act.wait_ge(S["dl_abs"], HI * (g + 1))
                sc.activation(tmpT[:, :, gcols(g)], tmpT[:, :, gcols(g)], ACT.Exp, scale=-1.0).then_inc(S["dl_exp"], 1)
            step(sc.activation(negA[:].rearrange("p h n -> p (h n)"), w["A_log"][:].rearrange("p h n -> p (h n)"), ACT.Exp))
            step(sc.mul(negA[:].rearrange("p h n -> p (h n)"), negA[:].rearrange("p h n -> p (h n)"), -1.0))
            step(sc.activation(coef[:, 1, :], w["omega"][:], ACT.Abs))
            step(sc.activation(coef[:, 1, :], coef[:, 1, :], ACT.Exp, scale=-1.0))
            sc.activation(coef[:, 1, :], coef[:, 1, :], ACT.Ln, bias=1.0).then_inc(S["omega_ln"], 1)
            for g in range(NG):
                act.wait_ge(S["dl_exp"], g + 1)
                sc.activation(tmpT[:, :, gcols(g)], tmpT[:, :, gcols(g)], ACT.Ln, bias=1.0).then_inc(S["dl_ln"], 1)

            def b_copy(i):
                act.wait_ge(S["b_bcast"], i + 1)
                if i >= 4:
                    act.wait_ge(S["drive"], i - 3)
                sc.copy(Bsb[:, i % 4, :], bank(4)[:, 0, :]).then_inc(S["b_copied"], 1)

            b_copy(0)
            b_copy(1)
            for g in range(NG):
                act.wait_ge(S["dl_done"], 2 * g + 1)
                for n in range(NS):
                    i, j = g * NS + n, n % 2
                    if i >= 2:
                        act.wait_ge(S["scanned"], i - 1)
                    for m in range(HI):
                        sc.activation(
                            bank(2 * j + m)[:, 0, :].rearrange("p (b t) -> p b t", b=GB)[:, :, 1:T],
                            dT[:, m, gcols(g)].rearrange("p (b t) -> p b t", b=GB)[:, :, 1:T], ACT.Exp,
                            scale=negA[:, m, n:n + 1]).then_inc(S["decay"], 1)
                    if i + 2 < NG * NS:
                        b_copy(i + 2)

            def keys_and_values(i, k_copy, v_copy):
                for g in range(NG):
                    normalize(i, g)
                    k_copy(g)
                    if g:
                        copy_xnT(i, g - 1)
                        v_copy(g - 1)
                copy_xnT(i, NG - 1)
                v_copy(NG - 1)

            def k0_copy(g):
                act.wait_ge(S["k_mm"], g + 1)
                sc.copy(kT[:, gb(g), :], bank(4 + g)[:, 0, 0:GB * LK].rearrange("p (b k) -> p b k", b=GB)).then_inc(S["k_ev"], 1)

            def v0_copy(g):
                act.wait_ge(S["v_mm"], g + 1)
                sc.copy(vS[0:LK, gb(g), :], bank(4 + g)[0:LK, 0, :].rearrange("p (b d) -> p b d", b=GB)).then_inc(S["v_ev"], 1)

            act.wait_ge(S["y_gated"], NG)
            keys_and_values(1, k0_copy, v0_copy)
            for g in range(NG):
                act.wait_ge(S["q_mm"], g + 1)
                sc.activation(qT[:, gcols(g)], bank(4 + g)[:, 0, :], ACT.Identity, bias=w["bq0"][:, 0:1]).then_inc(S["q_ev"], 1)
            for g in range(NG):
                act.wait_ge(S["sc_max"], g + 1)
                for b in range(GB):
                    sc.activation(pr[:, g * GB + b, :], bank(g)[:, 0, b * LK:(b + 1) * LK], ACT.Exp,
                                  bias=small[:, 1, g * GB + b:g * GB + b + 1],
                                  accum_out=small[:, 2, g * GB + b:g * GB + b + 1]).then_inc(S["sc_exp"], 1)
            layer_norm(2)
            for i in range((E + 1) * NG):
                for m in range(M0):
                    k = M0 * i + m
                    act.wait_ge(S["up_mm"], k + 1)
                    if i >= 2:
                        act.wait_ge(S["hid0"], k + 1 - 2 * M0)
                    sc.activation(sh[:, i % 2, m * GT:(m + 1) * GT], bank(m)[:, 0, :], ACT.Silu).then_inc(S["silu0"], 1)
                if i == 1:
                    act.wait_ge(S["rt_sub"], 1)
                    sc.activation(router[:, 1, :, :], router[:, 0, :, :], ACT.Exp).then_inc(S["rt_exp"], 1)
            for g in range(NG):
                normalize(3, g)
                if g == NG - 2:
                    for c in range(NG - 1):
                        copy_xnT(3, c)
            act.wait_ge(S["coef_done"], 1)

            def xz_copy(g):
                for m in range(4):
                    act.wait_ge(S["xz_mm"], 4 * g + m + 1)
                    sc.copy((xi if m < HI else z1)[:, m % HI, gcols(g)], bank(4 + m)[:, 0, :]).then_inc(S["xz_ev"], 1)

            xz_copy(0)
            copy_xnT(3, NG - 1)
            xz_copy(1)
            for g in range(NG):
                for m in range(HI):
                    act.wait_ge(S["l_mm"], HI * g + m + 1)
                    sc.activation(lam[:, m, gcols(g)], bank(m)[:, 0, :], ACT.Sigmoid, bias=w["bl"][:, m:m + 1])\
                        .then_inc(S["l_ev"], 1)
                for m in range(HI):
                    act.wait_ge(S["v2_mm"], HI * g + m + 1)
                    sc.activation(vv[:, m, gcols(g)], bank(2 - 2 * m)[:, 0, :], ACT.Identity, bias=w["bv"][:, m:m + 1])\
                        .then_inc(S["v2_ev"], 1)
                act.wait_ge(S["v2_ev"], HI * (g + 1))
                sc.activation(sq[:, :, gcols(g)], vv[:, :, gcols(g)], ACT.Square).then_inc(S["sq_done"], 1)
                if g + 2 < NG:
                    xz_copy(g + 2)
                for m in range(HI):
                    act.wait_ge(S["l_ev"], HI * g + m + 1)
                    sc.activation(lam[:, m, gcols(g)], lam[:, m, gcols(g)], ACT.Exp, scale=coef[:, 2, m:m + 1])\
                        .then_inc(S["lam_done"], 1)
            for m in range(HI):
                sc.activation(z1[:, m, :], z1[:, m, :], ACT.Silu).then_inc(S["z_silu"], 1)

            def k1_copy(g):
                act.wait_ge(S["hk_mm"], g + 1)
                sc.copy(khl[:, 0, gb(g), :].bitcast(F32R), bank(4 + g)[:, 0, 0:GB * LK].rearrange("p (b k) -> p b k", b=GB))\
                    .then_inc(S["hk_ev"], 1)

            def v1_copy(g):
                act.wait_ge(S["hv_mm"], g + 1)
                sc.copy(v1S[0:LK, gb(g), :], bank(4 + g)[0:LK, 0, :].rearrange("p (b d) -> p b d", b=GB)).then_inc(S["hv_ev"], 1)

            act.wait_ge(S["g1_ready"], NG)
            keys_and_values(4, k1_copy, v1_copy)
            act.wait_ge(S["bo_mm"], 1)
            sc.copy(bo_b, bank(0)[:, 0, 0:P]).then_inc(S["bo_ev"], 1)
            for g in range(NG):
                act.wait_ge(S["hq_mm"], g + 1)
                sc.activation(qhl[:, 0, gcols(g)], bank(4 + g)[:, 0, :], ACT.Identity, bias=w["bq1"][:, 0:1]).then_inc(S["hq_ev"], 1)

            def head_out_copy(b):
                act.wait_ge(S["ho_mm"], b + 1)
                if b:
                    act.wait_ge(S["hw_mm"], b)
                for r in range(4):
                    rows = slice(32 * r, 32 * r + 32)
                    ins = sc.copy(oT[rows, :], bank(6)[rows, 0, r * T:(r + 1) * T])
                ins.then_inc(S["ho_ev"], 1)

            for b in range(-1, B):
                if b >= 1:
                    head_out_copy(b - 1)
                for q in range(2):
                    if b >= 0:
                        act.wait_ge(S["ht_mm"], 2 * b + q + 1)
                        if b:
                            act.wait_ge(S["ho_mm"], b)
                        sc.copy(n1T[0:LK, 8 * q:8 * q + 8, :].rearrange("p (c h) q -> p c (h q)", c=2),
                                bank(4, 2)[0:LK, :, :]).then_inc(S["ht_ev"], 1)
                    if b + 1 < B:
                        c = b + 1
                        act.wait_ge(S["hs_sub"], 2 * c + q + 1)
                        if c:
                            act.wait_ge(S["hs_norm"], 2 * c - 1 + q)
                        sc.activation(e1[:, 8 * q:8 * q + 8, :], p1[:, 8 * q:8 * q + 8, :], ACT.Exp,
                                      scale=float(DK) ** -0.5).then_inc(S["hs_exp"], 1)
                if b % GB == GB - 2 and b > GB:
                    normalize(5, b // GB - 1)
            head_out_copy(B - 1)
            for g in range(NG - 1):
                copy_xnT(5, g)
            normalize(5, NG - 1)
            copy_xnT(5, NG - 1)

            def selu(i, slot, banks, lin_bias, exp_bias, mm_s, act_s):
                for m in range(M1):
                    act.wait_ge(S[mm_s], M1 * i + m + 1)
                    sc.activation(G[:, 0, slot, m * GT:(m + 1) * GT], banks[:, m, :], ACT.Exp, bias=exp_bias[m])
                    sc.activation(G[:, 1, slot, m * GT:(m + 1) * GT], banks[:, m, :], ACT.Relu, bias=lin_bias[m],
                                  scale=SELU_L).then_inc(S[act_s], 1)

            act.wait_ge(S["coef_sp"], 1)
            for g in range(NG):
                if g >= 2:
                    act.wait_ge(S["g_hid"], g - 1)
                selu(g, g % 2, bank(0, M1), [ebs[:, 0, m:m + 1] for m in range(M1)],
                     [w["gate_bi"][:, m:m + 1] for m in range(M1)], "gu_mm", "g_act")
            for i in range(E * NG):
                e = i // NG
                act.wait_ge(S["g_hid"], NG)
                if i >= 2:
                    act.wait_ge(S["hid1"], i - 1)
                selu(i, i % 2, bank(0, M1), [ebs[:, 1 + e, m:m + 1] for m in range(M1)],
                     [w["exp_bi"][:, e, m:m + 1] for m in range(M1)], "up1_mm", "act1")

        @block.vector
        def _(dve):
            v = nc.vector
            step = Chain(dve, S["dve_step"])

            def ln_stats(i, g):
                bs = range(g * GB, (g + 1) * GB)
                for b in bs:
                    ins = v.bn_stats(stats[:, b, :], X[:, b, :])
                step(ins)
                for b in bs:
                    ins = v.bn_aggr(mv[:, b, :], stats[:, b, :])
                step(ins)
                v.tensor_scalar(nmean[:, gb(g)], mv[:, gb(g), 0], -1.0, None, ALU.mult)
                v.tensor_scalar(small[:, 0, gb(g)], mv[:, gb(g), 1], EPS, None, ALU.add).then_inc(S["ln_stats"], 1)

            def ln_norm(i, g):
                dve.wait_ge(S["ln_scale"], i * NG + g + 1)
                for b in range(g * GB + GB // 2, (g + 1) * GB):
                    ins = v.tensor_scalar(xn[:, b, :], X[:, b, :], mv[:, b, 0:1], rstd[:, b:b + 1], ALU.subtract, ALU.mult)
                ins.then_inc(S["ln_xn_b"], 1)

            def ln_lower(i, g):
                dve.wait_ge(S["ln_xnT"], i * NG + g + 1)
                v.tensor_tensor(xhl[:, 1, gcols(g)], bank(ln_bank(i, g))[:, 0, :], xhl[:, 0, gcols(g)].bitcast(F32),
                                ALU.subtract).then_inc(S["ln_lo"], 1)

            def layer_norm(i, complete, beside=lambda g: None):
                for g in range(NG + 2):
                    if g < NG:
                        complete(g)
                        ln_stats(i, g)
                    if 1 <= g <= NG:
                        ln_norm(i, g - 1)
                    if g >= 2 and i in SPLIT:
                        ln_lower(i, g - 2)
                    if g >= 2:
                        beside(g - 2)

            def choose(val, cw):
                v.memset(pair.rearrange("p b e f -> p b (e f)")[:, :, 0:E * E:E + 1], 0.0)
                for e in range(E):
                    if e:
                        ins = v.tensor_tensor(pair[:, :, e, 0:e], val[:, :, 0:e], val[:, :, e:e + 1].broadcast_to([P, B, e]), ALU.is_ge)
                    if e < E - 1:
                        ins = v.tensor_tensor(pair[:, :, e, e + 1:E], val[:, :, e + 1:E],
                                              val[:, :, e:e + 1].broadcast_to([P, B, E - 1 - e]), ALU.is_gt)
                step(ins)
                step(v.tensor_reduce(router[:, 2], pair, AX.X, ALU.add))
                step(v.tensor_scalar(router[:, 3], router[:, 2], 1.5, None, ALU.is_lt))
                step(v.tensor_tensor(router[:, 4], router[:, 3], val, ALU.mult))
                step(v.tensor_reduce(small[:, 3, :], router[:, 4], AX.X, ALU.add))
                step(v.reciprocal(small[:, 1, :], small[:, 3, :]))
                return v.tensor_tensor(cw, router[:, 4], small[:, 1, :].unsqueeze(2).broadcast_to([P, B, E]), ALU.mult)

            def x_ready(g):
                dve.wait_ge(S[f"x_in{g}"], 16)
                if g == NG - 1:
                    dve.wait_ge(S["w_upper"], 1)
                    v.tensor_tensor(whl[:, wslot(0), 1], w["W_in"][:].rearrange("p m n -> p (m n)"),
                                    whl[:, wslot(0), 0].bitcast(F32), ALU.subtract).then_inc(S["w_split"], 1)

            layer_norm(0, x_ready)
            dve.wait_ge(S["w_mamba"], 16 * 8)
            dve.wait_ge(S["const"], 1)
            for m in range(HI):
                v.tensor_scalar(diagD[:, m, :], ident[:], w["D_param"][:, m:m + 1], None, ALU.mult).then_inc(S["diag_ready"], 1)

            def bc_split(g):
                dve.wait_ge(S["bc_mm"], g + 1)
                psBC = bank(4 + g)[0:2 * NS, 0, :]
                rem = yT[0:2 * NS, 0, gcols(g)]
                mid = yT[0:2 * NS, 1, gcols(g)].bitcast(BF16)[:, 0:GT]
                step(v.tensor_copy(bc3[0:32, gcols(g)], psBC))
                step(v.tensor_tensor(rem, psBC, bc3[0:32, gcols(g)], ALU.subtract))
                step(v.tensor_copy(mid, rem))
                v.tensor_copy(bc3[32:64, gcols(g)], mid)
                v.tensor_tensor(bc3[64:96, gcols(g)], rem, mid, ALU.subtract).then_inc(S["bc_split"], 1)

            def relu_delta(g):
                for m in range(HI):
                    dve.wait_ge(S["dl_abs"], HI * g + m + 1)
                    v.tensor_scalar(dT[:, m, gcols(g)], bank(2 * (g % 2) + m)[:, 0, :], w["b_delta"][:, m:m + 1], 0.0,
                                    ALU.add, ALU.max).then_inc(S["dl_relu"], 1)

            def delta_and_drive(g):
                dve.wait_ge(S["dl_ln"], g + 1)
                dve.wait_ge(S["dl_relu"], HI * (g + 1))
                v.tensor_tensor(dT[:, :, gcols(g)], dT[:, :, gcols(g)], tmpT[:, :, gcols(g)], ALU.add).then_inc(S["dl_done"], 1)
                dve.wait_ge(S["dl_done"], 2 * g + 1)
                v.tensor_tensor(duT[:, :, gcols(g)], dT[:, :, gcols(g)], uT[:, :, gcols(g)], ALU.mult).then_inc(S["dl_done"], 1)

            bc_split(0)
            bc_split(1)
            for g in range(NG):
                relu_delta(g)
                if g + 2 < NG:
                    bc_split(g + 2)
            dve.wait_ge(S["dl_relu"], HI * NG)
            for j in range(4):
                ins = v.memset(bank(j)[:, 0, :].rearrange("p (b t) -> p b t", b=GB)[:, :, 0:1], 0.0)
            step(ins)
            delta_and_drive(0)

            def scan(i):
                j = i % 2
                if i >= 2:
                    dve.wait_ge(S["hc"], i - 1)
                dve.wait_ge(S["decay"], HI * i + HI)
                dve.wait_ge(S["drive"], i + 1)
                v.tensor_tensor_scan(hst[:, j, :], bank(2 * j, 2).rearrange("p h n -> p (h n)"), dBu[:, j, :], 0.0,
                                     ALU.mult, ALU.add).then_inc(S["scanned"], 1)

            def gate_y(g):
                dve.wait_ge(S["y_acc"], (g + 1) * NS)
                v.tensor_tensor(yT[:, :, gcols(g)], bank(6, 2), zT[:, :, gcols(g)], ALU.mult).then_inc(S["y_gated"], 1)

            scan(0)
            for i in range(NG * NS):
                g, n, j = i // NS, i % NS, i % 2
                if i + 1 < NG * NS:
                    scan(i + 1)
                dve.wait_ge(S["scanned"], i + 1)
                dve.wait_ge(S["c_bcast"], i + 1)
                if i >= 2:
                    dve.wait_ge(S["y_acc"], i - 1)
                v.tensor_tensor(hC[:, j, :].rearrange("p (h n) -> p h n", h=HI),
                                hst[:, j, :].rearrange("p (h n) -> p h n", h=HI),
                                bank(5).broadcast_to([P, HI, GT]), ALU.mult).then_inc(S["hc"], 1)
                if n == 0 and g:
                    gate_y(g - 1)
                if n == NS // 2 and g + 1 < NG:
                    delta_and_drive(g + 1)
            gate_y(NG - 1)

            def add_out(done, res):
                def complete(g):
                    dve.wait_ge(S[done], g + 1)
                    v.tensor_tensor(X[:, gb(g), :], X[:, gb(g), :], bank(g)[:, 0, :].rearrange("p (b d) -> p b d", b=GB),
                                    ALU.add).then_inc(S[res], 1)
                    dve.wait_ge(S[res], g + 1)
                return complete

            layer_norm(1, add_out("a_out", "a_res"))
            step(v.tensor_scalar(coef[:, 0, :], w["omega"][:], 0.0, None, ALU.max))
            dve.wait_ge(S["omega_ln"], 1)
            step(v.tensor_tensor(coef[:, 3, :], coef[:, 0, :], coef[:, 1, :], ALU.add))
            v.tensor_scalar(coef[:, 2, :], coef[:, 3, :], -8.0, None, ALU.mult).then_inc(S["coef_done"], 1)
            for g in range(NG):
                dve.wait_ge(S["sc_mm"], g + 1)
                v.tensor_reduce(small[:, 1, gb(g)], bank(g)[:, 0, 0:GB * LK].rearrange("p (b k) -> p b k", b=GB), AX.X,
                                ALU.max, negate=True).then_inc(S["sc_max"], 1)
            for g in range(NG):
                dve.wait_ge(S["pt_mm"], g + 1)
                v.tensor_copy(prT[0:LK, gb(g), :], bank(4 + g)[0:LK, 0, :].rearrange("p (b q) -> p b q", b=GB)).then_inc(S["pt_ev"], 1)

            def add_attended(g):
                dve.wait_ge(S["sc_exp"], GB * (g + 1))
                step(v.reciprocal(small[:, 3, gb(g)], small[:, 2, gb(g)]))
                dve.wait_ge(S["pv_mm"], g + 1)
                for b in range(GB):
                    bi = g * GB + b
                    v.scalar_tensor_tensor(X[:, bi, :], bank(g)[:, 0, b * D:(b + 1) * D], small[:, 3, bi:bi + 1], X[:, bi, :],
                                           ALU.mult, ALU.add).then_inc(S["pv_res"], 1)
                dve.wait_ge(S["pv_res"], GB * (g + 1))

            layer_norm(2, add_attended)

            def choose_experts():
                dve.wait_ge(S["rt_mm"], 1)
                lg = bank(7)[:, 0, 0:B * E].rearrange("p (b e) -> p b e", b=B)
                step(v.tensor_reduce(small[:, 1, :], lg, AX.X, ALU.max))
                v.tensor_tensor(router[:, 0], lg, small[:, 1, :].unsqueeze(2).broadcast_to([P, B, E]), ALU.subtract)\
                    .then_inc(S["rt_sub"], 1)
                dve.wait_ge(S["rt_exp"], 1)
                choose(router[:, 1], cw0[:, :, 0:E]).then_inc(S["rt_cw"], 1)
                dve.wait_ge(S["rt_cw"], 1)

            def add_expert(i, cw, e, dn, rs):
                g = i % NG
                dve.wait_ge(S[dn], i + 1)
                for b in range(GB):
                    bi = g * GB + b
                    ins = v.scalar_tensor_tensor(X[:, bi, :], bank(4 + i % 2)[:, 0, b * D:(b + 1) * D], cw[:, bi, e:e + 1],
                                                 X[:, bi, :], ALU.mult, ALU.add)
                ins.then_inc(S[rs], 1)

            for i in range((E + 1) * NG + 1):
                if i < (E + 1) * NG:
                    if i >= 2:
                        dve.wait_ge(S["down0"], i - 1)
                    for m in range(M0):
                        dve.wait_ge(S["silu0"], M0 * i + m + 1)
                        v.tensor_tensor(hidr[:, i % 2, m * GT:(m + 1) * GT], sh[:, i % 2, m * GT:(m + 1) * GT],
                                        bank(2 + m)[:, 0, :], ALU.mult).then_inc(S["hid0"], 1)
                    if i == 1:
                        choose_experts()
                if i >= 1:
                    if i > NG:
                        dve.wait_ge(S["res0"], i - NG)
                    add_expert(i - 1, cw0, (i - 1) // NG, "down0", "res0")
                if i > E * NG:
                    g = i - 1 - E * NG
                    dve.wait_ge(S["res0"], i)
                    ln_stats(3, g)
                    if g:
                        ln_norm(3, g - 1)
            ln_norm(3, NG - 1)
            for g in range(NG):
                ln_lower(3, g)
            tok = lambda buf, g: buf[:, :, gcols(g)].rearrange("p h (b t) -> p h b t", b=GB)

            def shift_v(g):
                dve.wait_ge(S["dots_in"], 2 * (g + 1))
                v.tensor_tensor(tok(vv, g)[:, :, :, 0:T - 1], tok(vv, g)[:, :, :, 1:T], tok(lam, g)[:, :, :, 0:T - 1],
                                ALU.mult).then_inc(S["vl_done"], 1)

            for g in range(NG):
                dve.wait_ge(S["lam_done"], HI * (g + 1))
                step(v.memset(tok(lam, g)[:, :, :, 0:1], 0.0))
                v.scalar_tensor_tensor(nb[:, :, gcols(g)], lam[:, :, gcols(g)], 1.0, xi[:, :, gcols(g)], ALU.subtract,
                                       ALU.mult).then_inc(S["nb_done"], 1)
                dve.wait_ge(S["vv_mm"], g + 1)
                v.reciprocal(rvv[:, gcols(g)], bank(3)[:, 0, :]).then_inc(S["vv_read"], 1)
                dve.wait_ge(S["vv_read"], g + 1)
                step(v.scalar_tensor_tensor(ww[:, :, gcols(g)], vv[:, :, gcols(g)], -2.0,
                                            rvv[:, gcols(g)].unsqueeze(1).broadcast_to([P, HI, GT]), ALU.mult, ALU.mult))
                v.tensor_tensor(ww[:, :, gcols(g)], ww[:, :, gcols(g)], lam[:, :, gcols(g)], ALU.mult).then_inc(S["w_done"], 1)
                if g:
                    shift_v(g - 1)
            shift_v(NG - 1)
            lamvl = G[:, 2:4, :, :]

            def to_next(t):
                src = lamvl.rearrange("p i h (b t) -> p i h b t", b=B)[:, :, :, :, t + 1]
                h = at(xi, t).unsqueeze(1).broadcast_to([P, 2, HI, B])
                return v.tensor_tensor(lm[:, t % 2], src, h, ALU.mult)

            def advance(t, last=False):
                dve.wait_ge(S["r_dot"], t)
                v.tensor_tensor(sdot[:], slot(0, t), acc[:], ALU.add).then_inc(S["r_s"], 1)
                dve.wait_ge(S["r_s"], t)
                v.tensor_tensor(rrec[:], at(ww, t), sdot[:].unsqueeze(1).broadcast_to([P, HI, B]), ALU.mult)\
                    .then_inc(S["r_r"], 1)
                dve.wait_ge(S["r_r"], t)
                dve.wait_ge(S["r_g"], t)
                v.tensor_tensor(at(xi, t), rrec[:], grec[:, t % 2], ALU.add).then_inc(S["r_h"], 1)
                if not last:
                    v.tensor_tensor(acc[:], slot(4, t + 1), sdot[:], ALU.mult).then_inc(S["r_acc"], 1)
                    dve.wait_ge(S["r_h"], t)
                    to_next(t).then_inc(S["r_lm"], 1)
                    dve.wait_ge(S["r_acc"], t)

            dve.wait_ge(S["vl_done"], NG)
            step(v.memset(acc[:], 0.0))
            to_next(0).then_inc(S["r_lm"], 1)
            for t in range(1, T):
                advance(t, last=t == T - 1)
            dve.wait_ge(S["r_h"], T - 1)
            dve.wait_ge(S["z_silu"], HI)
            for g in range(NG):
                v.tensor_tensor(nb[:, :, gcols(g)], xi[:, :, gcols(g)], z1[:, :, gcols(g)], ALU.mult).then_inc(S["g1_ready"], 1)

            def k_lower(g):
                dve.wait_ge(S["hk_ev"], g + 1)
                v.tensor_tensor(khl[:, 1, gb(g), :].bitcast(F32R), bank(4 + g)[:, 0, 0:GB * LK].rearrange("p (b k) -> p b k", b=GB),
                                khl[:, 0, gb(g), :], ALU.subtract).then_inc(S["hk_lo"], 1)

            layer_norm(4, add_out("d_out", "d_res"), k_lower)
            for g in range(NG):
                dve.wait_ge(S["hq_ev"], g + 1)
                v.scalar_tensor_tensor(qhl[:, 1, gcols(g)], bank(4 + g)[:, 0, :], w["bq1"][:, 0:1], qhl[:, 0, gcols(g)].bitcast(F32),
                                       ALU.add, ALU.subtract).then_inc(S["hq_lo"], 1)

            def head_sums(b, q):
                hh = slice(8 * q, 8 * q + 8)
                dve.wait_ge(S["hs_exp"], 2 * b + q + 1)
                step(v.tensor_reduce(small[:, 2, hh], e1[:, hh, :], AX.X, ALU.add))
                if b:
                    dve.wait_ge(S["hs_norm"], 2 * b - 1 + q)
                v.reciprocal(small[:, 3, hh], small[:, 2, hh]).then_inc(S["hs_inv"], 1)

            for b in range(B + 2):
                for q in range(2):
                    if q == 0 and 1 <= b <= B:
                        head_sums(b - 1, 1)
                    if b < B:
                        hh = slice(8 * q, 8 * q + 8)
                        dve.wait_ge(S["hs_mm"], 2 * b + q + 1)
                        sc2 = bank(2 * q, 2)[:, :, 0:HQ * LK].rearrange("p g (j k) -> p g j k", j=HQ)
                        step(v.tensor_reduce(small[:, 1, hh].rearrange("p (g j) -> p g j", j=HQ), sc2, AX.X, ALU.max))
                        if b:
                            dve.wait_ge(S["hs_exp"], 2 * b - 1 + q)
                        for r in range(2):
                            h4 = slice(8 * q + HQ * r, 8 * q + HQ * r + HQ)
                            ins = v.tensor_tensor(p1[:, h4, :], sc2[:, r],
                                                  small[:, 1, h4].unsqueeze(2).broadcast_to([P, HQ, LK]), ALU.subtract)
                        ins.then_inc(S["hs_sub"], 1)
                    if q and b < B:
                        head_sums(b, 0)
                if b >= 2:
                    c = b - 2
                    dve.wait_ge(S["hw_mm"], c + 1)
                    if c == 0:
                        dve.wait_ge(S["bo_add"], 1)
                    v.tensor_tensor(X[:, c, :], X[:, c, :], bank(7)[:, 0, 0:P], ALU.add).then_inc(S["hw_res"], 1)
                    if c % GB == GB - 1:
                        dve.wait_ge(S["hw_res"], c + 1)
                        ln_stats(5, c // GB)
                    elif c % GB == GB - 2 and c > GB:
                        ln_norm(5, c // GB - 1)
            ln_norm(5, NG - 1)
            for g in range(NG):
                ln_lower(5, g)
            dve.wait_ge(S["w_gate"], 16 * 6)
            v.tensor_scalar(ebs[:, 0, :], w["gate_bi"][:], SELU_L, None, ALU.mult)
            v.tensor_scalar(ebs[:, 1:, :], w["exp_bi"][:], SELU_L, None, ALU.mult).then_inc(S["coef_sp"], 1)

            def selu_sum(i, slot, a_s, h_s):
                for q in range(2):
                    half = slice(q * GT * M1 // 2, (q + 1) * GT * M1 // 2)
                    dve.wait_ge(S[a_s], M1 * i + (q + 1) * M1 // 2)
                    step(v.tensor_scalar(G[:, 0, slot, half], G[:, 0, slot, half], 1.0, 1.0, ALU.min, ALU.subtract))
                    ins = v.scalar_tensor_tensor(G[:, 2, slot, half], G[:, 0, slot, half], SELU_LA, G[:, 1, slot, half], ALU.mult,
                                                 ALU.add)
                ins.then_inc(S[h_s], 1)

            v.memset(pair, 0.0)
            for g in range(NG):
                if g >= 2:
                    dve.wait_ge(S["gl_mm"], g - 1)
                selu_sum(g, g % 2, "g_act", "g_hid")
            le = router[:, 5]
            for g in range(NG):
                dve.wait_ge(S["gl_mm"], g + 1)
                for b in range(g * GB, (g + 1) * GB):
                    v.max(top[:, b, :], bank(4 + g)[:, 0, (b % GB) * D:(b % GB + 1) * D])
                v.tensor_copy(le[:, gb(g), :], bank(4 + g)[:, 0, :].rearrange("p (b d) -> p b d", b=GB)[:, :, 0:E])\
                    .then_inc(S["gl_read"], 1)
            selu_sum(0, 0, "act1", "hid1")
            dve.wait_ge(S["gl_read"], NG)
            for e in range(1, E):
                ins = v.tensor_tensor(pair[:, :, e, 0:e], le[:, :, 0:e], le[:, :, e:e + 1].broadcast_to([P, B, e]), ALU.is_equal)
            step(ins)
            step(v.tensor_reduce(router[:, 2], pair, AX.X, ALU.add))
            for k in range(2):
                step(v.tensor_tensor(router[:, 3], top[:, :, k:k + 1].broadcast_to([P, B, E]), le, ALU.is_gt))
                step(v.tensor_tensor(router[:, 2], router[:, 2], router[:, 3], ALU.add))
            selu_sum(1, 1, "act1", "hid1")
            step(v.tensor_scalar(router[:, 3], router[:, 2], 1.5, None, ALU.is_lt))
            step(v.tensor_tensor(router[:, 4], router[:, 3], le, ALU.mult))
            step(v.tensor_tensor(small[:, 3, :], top[:, :, 0], top[:, :, 1], ALU.add))
            step(v.reciprocal(small[:, 1, :], small[:, 3, :]))
            v.tensor_tensor(cw1[:], router[:, 4], small[:, 1, :].unsqueeze(2).broadcast_to([P, B, E]), ALU.mult).then_inc(S["gl_cw"], 1)
            dve.wait_ge(S["gl_cw"], 1)

            for i in range(E * NG + 1):
                if 2 <= i < E * NG:
                    dve.wait_ge(S["down1"], i - 1)
                    selu_sum(i, i % 2, "act1", "hid1")
                if i >= 1:
                    if i > NG:
                        dve.wait_ge(S["res1"], i - NG)
                    add_expert(i - 1, cw1, (i - 1) // NG, "down1", "res1")
                g, turn = divmod(i - EB, 2)
                if 0 <= g < NG and turn == 0:
                    dve.wait_ge(S["wt_mm"], g + 1)
                    v.tensor_copy(cwT[:, gb(g), :], bank(6)[0:E, 0, :].rearrange("p (b t) -> p b t", b=GB)).then_inc(S["wt_ev"], 1)
                elif 0 <= g < NG:
                    dve.wait_ge(S["eb_mm"], g + 1)
                    dve.wait_ge(S["res1"], i)
                    v.tensor_tensor(X[:, gb(g), :], X[:, gb(g), :], bank(7)[:, 0, :].rearrange("p (b d) -> p b d", b=GB),
                                    ALU.add).then_inc(S["eb_res"], 1)
                    dve.wait_ge(S["eb_res"], g + 1)

        @block.tensor
        def _(pe):
            mm = nc.tensor.matmul

            def transpose_xn(i, g):
                for b in range(GB):
                    if b % (GB // 2) == 0:
                        pe.wait_ge(S["ln_xn_b" if b else "ln_xn_a"], i * NG + g + 1)
                    ins = nc.tensor.transpose(bank(ln_bank(i, g))[:, 0, b * T:(b + 1) * T], xn[:, g * GB + b, :], ident[:])
                ins.then_inc(S["ln_tr"], 1)

            def down(ks, lhs, rhs, o):
                for b in range(GB):
                    for k in range(ks):
                        ins = mm(bank(o)[:, 0, b * D:(b + 1) * D], lhs(k, b), rhs(k), start=k == 0, stop=k == ks - 1)
                return ins

            def up(out, n, m, g):
                for k, (i, j) in enumerate(PARTS):
                    ins = mm(out, whl[:, wslot(n), i, m * P:(m + 1) * P], xhl[:, j, gcols(g)], start=k == 0, stop=k == 2)
                return ins

            pe.wait_ge(S["const"], 1)
            transpose_xn(0, 0)
            pe.wait_ge(S["w_mamba"], 16 * 8)
            for g in range(NG):
                if g + 1 < NG:
                    transpose_xn(0, g + 1)
                pe.wait_ge(S["w_split"], 1)
                pe.wait_ge(S["ln_lo"], g + 1)
                for m in range(4):
                    if g:
                        pe.wait_ge(S["in_silu"], 4 * g - 3 + m)
                    up(bank(4 + m)[:, 0, :], 0, m, g).then_inc(S["in_mm"], 1)
            for g in range(NG):
                pe.wait_ge(S["in_silu"], 4 * (NG - 1) + g + 1)
                pe.wait_ge(S["in_silu"], 4 * g + HI)
                for k in range(HI):
                    ins = mm(bank(4 + g)[0:2 * NS, 0, :], w["W_BC"][:, k, :], uT[:, k, gcols(g)], start=k == 0, stop=k == HI - 1)
                ins.then_inc(S["bc_mm"], 1)
            for g in range(NG):
                for m in range(HI):
                    if g >= 2:
                        pe.wait_ge(S["dl_abs"], HI * (g - 2) + m + 1)
                        pe.wait_ge(S["dl_relu"], HI * (g - 2) + m + 1)
                    for k in range(HI):
                        ins = mm(bank(2 * (g % 2) + m)[:, 0, :], w["W_delta"][:, k, m * P:(m + 1) * P], uT[:, k, gcols(g)],
                                 start=k == 0, stop=k == HI - 1)
                    ins.then_inc(S["dl_mm"], 1)
            pe.wait_ge(S["const_rest"], 1)
            pe.wait_ge(S["bc_split"], NG)
            pe.wait_ge(S["diag_ready"], HI)

            def broadcast(bank_i, r, g, s):
                mm(bank(bank_i)[:, 0, :], sel[:, r, :], bc3[:, gcols(g)], start=True, stop=True).then_inc(S[s], 1)

            def b_row(i):
                if i:
                    pe.wait_ge(S["b_copied"], i)
                broadcast(4, i % NS, i // NS, "b_bcast")

            def c_row(i):
                if i:
                    pe.wait_ge(S["hc"], i)
                broadcast(5, i % NS + NS, i // NS, "c_bcast")

            def y_sum(i):
                pe.wait_ge(S["hc"], i + 1)
                for m in range(HI):
                    ins = mm(bank(6 + m)[:, 0, :], ident[:], hC[:, i % 2, m * GT:(m + 1) * GT], start=False,
                             stop=i % NS == NS - 1, skip_group_check=True)
                ins.then_inc(S["y_acc"], 1)

            for i in range(3):
                b_row(i)
            for i in range(NG * NS):
                g, n = divmod(i, NS)
                if i + 3 < NG * NS:
                    b_row(i + 3)
                c_row(i)
                if n == 1:
                    if g:
                        pe.wait_ge(S["y_gated"], g)
                    for m in range(HI):
                        mm(bank(6 + m)[:, 0, :], diagD[:, m, :], uT[:, m, gcols(g)], start=True, stop=False, skip_group_check=True)
                if i:
                    y_sum(i - 1)
            y_sum(NG * NS - 1)
            for g in range(NG):
                pe.wait_ge(S["y_gated"], NG)
                down(HI, lambda k, b: yT[:, k, (g * GB + b) * T:(g * GB + b + 1) * T], lambda k: w["W_out"][:, k, :], g)\
                    .then_inc(S["a_out"], 1)
            pe.wait_ge(S["w_ctx"], 16 * 6)
            for g in range(NG):
                mm(bank(4 + g)[:, 0, 0:GB * LK], w["Wk0"][:], w["ctxT"][:, gb(g), :].rearrange("p b k -> p (b k)"),
                   start=True, stop=True).then_inc(S["k_mm"], 1)
            for g in range(NG):
                transpose_xn(1, g)
                pe.wait_ge(S["k_ev"], g + 1)
                for b in range(GB):
                    ins = mm(bank(4 + g)[0:LK, 0, b * D:(b + 1) * D], w["ctxT"][:, g * GB + b, :], w["Wv0"][:], start=True, stop=True)
                ins.then_inc(S["v_mm"], 1)
            for g in range(NG):
                pe.wait_ge(S["v_ev"], g + 1)
                pe.wait_ge(S["ln_xnT"], NG + g + 1)
                mm(bank(4 + g)[:, 0, :], w["Wq0"][:], xnT[:, gcols(g)], start=True, stop=True).then_inc(S["q_mm"], 1)
            for g in range(NG):
                pe.wait_ge(S["q_ev"], g + 1)
                for b in range(GB):
                    bi = g * GB + b
                    ins = mm(bank(g)[:, 0, b * LK:(b + 1) * LK], qT[:, bi * T:(bi + 1) * T], kT[:, bi, :], start=True, stop=True)
                ins.then_inc(S["sc_mm"], 1)
            for g in range(NG):
                pe.wait_ge(S["sc_exp"], GB * (g + 1))
                pe.wait_ge(S["v_ev"], g + 1)
                for b in range(GB):
                    ins = nc.tensor.transpose(bank(4 + g)[0:LK, 0, b * T:(b + 1) * T], pr[:, g * GB + b, :], ident[:])
                ins.then_inc(S["pt_mm"], 1)
            for g in range(NG):
                pe.wait_ge(S["pt_ev"], g + 1)
                for b in range(GB):
                    ins = mm(bank(g)[:, 0, b * D:(b + 1) * D], prT[0:LK, g * GB + b, :], vS[0:LK, g * GB + b, :], start=True, stop=True)
                ins.then_inc(S["pv_mm"], 1)
            transpose_xn(2, 0)
            for g in range(NG):
                if g + 1 < NG:
                    transpose_xn(2, g + 1)
                pe.wait_ge(S["ln_xnT"], 2 * NG + g + 1)
                for b in range(g * GB, (g + 1) * GB):
                    ins = mm(bank(7)[:, 0, b * E:(b + 1) * E], xnT[:, b * T:(b + 1) * T], w["router0"][:], start=True, stop=True)
            ins.then_inc(S["rt_mm"], 1)
            for i in range((E + 1) * NG + 1):
                e, g = divmod(i, NG)
                if i < (E + 1) * NG:
                    if g == 0:
                        pe.wait_ge(S["w_split"], N_E0 + e + 1)
                    if i == 0:
                        pe.wait_ge(S["ln_lo"], 2 * NG)
                    for m in range(M0):
                        if i:
                            pe.wait_ge(S["silu0"], M0 * (i - 1) + m + 1)
                        up(bank(m)[:, 0, :], N_E0 + e, m, g)
                        if i:
                            pe.wait_ge(S["hid0"], M0 * (i - 1) + m + 1)
                        up(bank(2 + m)[:, 0, :], N_E0 + e, M0 + m, g).then_inc(S["up_mm"], 1)
                if i >= 1:
                    c = i - 1
                    pe.wait_ge(S["hid0"], M0 * (c + 1))
                    if c >= 2:
                        pe.wait_ge(S["res0"], c - 1)
                    sl = (c // NG) % 2
                    down(M0, lambda k, b: hidr[:, c % 2, k * GT + b * T:k * GT + (b + 1) * T],
                         lambda k: ew0[:, sl, 2, k * D:(k + 1) * D], 4 + c % 2).then_inc(S["down0"], 1)
            for g in range(NG - 1):
                transpose_xn(3, g)
            pe.wait_ge(S["w_lru"], 16 * 6)
            pe.wait_ge(S["w_split"], N_WIN1 + 1)

            def xz(g):
                pe.wait_ge(S["ln_lo"], 2 * NG + g + 1)
                if g == 0:
                    pe.wait_ge(S["res0"], (E + 1) * NG)
                for m in range(4):
                    if g:
                        pe.wait_ge(S["xz_ev"], 4 * g - 3 + m)
                    up(bank(4 + m)[:, 0, :], N_WIN1, m, g).then_inc(S["xz_mm"], 1)

            def lam_or_v(g, wt, banks, done, freed):
                for m in range(HI):
                    if freed[m][1] > 0:
                        pe.wait_ge(S[freed[m][0]], freed[m][1])
                    for k in range(HI):
                        ins = mm(bank(banks[m])[:, 0, :], wt[:, k, m * P:(m + 1) * P], xi[:, k, gcols(g)],
                                 start=k == 0, stop=k == HI - 1)
                    ins.then_inc(S[done], 1)

            def v_dot_v(g):
                pe.wait_ge(S["sq_done"], g + 1)
                if g:
                    pe.wait_ge(S["vv_read"], g)
                for k in range(HI):
                    ins = mm(bank(3)[:, 0, :], ones[:], sq[:, k, gcols(g)], start=k == 0, stop=k == HI - 1)
                ins.then_inc(S["vv_mm"], 1)

            xz(0)
            transpose_xn(3, NG - 1)
            xz(1)
            for g in range(NG):
                pe.wait_ge(S["xz_ev"], 4 * g + HI)
                if g == 0:
                    pe.wait_ge(S["ln_lo"], 3 * NG)
                lam_or_v(g, w["Wl"], (0, 1), "l_mm", (("v2_ev", HI * g), ("l_ev", HI * g)))
                lam_or_v(g, w["Wv"], (2, 0), "v2_mm", (("v2_ev", HI * g - 1), ("l_ev", HI * g + 1)))
                if g + 2 < NG:
                    xz(g + 2)
                v_dot_v(g)
            for first, lhs, buf in ((0, nones, vb), (4, ones, vw)):
                pe.wait_ge(S["dots_sum"], 2 * NG - (buf is vb))
                for r in range(4):
                    if buf is vb and r == 3:
                        pe.wait_ge(S["vv_read"], NG)
                    rhs = buf[:, 0, :].rearrange("p (b c r) -> p r c b", b=B, r=4)[:, r]
                    ins = mm(bank(first + r)[:, 0, :].rearrange("p (c b) -> p c b", b=B), lhs[:], rhs, start=True, stop=True)
            ins.then_inc(S["r_dot"], 1)

            def dot(t):
                pe.wait_ge(S["r_lm"], t - 1)
                for h in range(HI):
                    ins = mm(slot(0, t), ones[:], lm[:, t % 2, 1, h, :], start=False, stop=h == HI - 1, skip_group_check=True)
                ins.then_inc(S["r_dot"], 1)

            for t in range(2, T):
                dot(t)
            for g in range(NG):
                pe.wait_ge(S["g1_ready"], g + 1)
                down(HI, lambda k, b: nb[:, k, (g * GB + b) * T:(g * GB + b + 1) * T], lambda k: w["Wout1"][:, k, :], g)\
                    .then_inc(S["d_out"], 1)
            pe.wait_ge(S["w_att"], 16 * 6)
            for g in range(NG):
                mm(bank(4 + g)[:, 0, 0:GB * LK], w["Wk1"][:], w["ctxT"][:, gb(g), :].rearrange("p b k -> p (b k)"),
                   start=True, stop=True).then_inc(S["hk_mm"], 1)
            for g in range(NG):
                transpose_xn(4, g)
                pe.wait_ge(S["hk_lo"], g + 1)
                for b in range(GB):
                    ins = mm(bank(4 + g)[0:LK, 0, b * D:(b + 1) * D], w["ctxT"][:, g * GB + b, :], w["Wv1"][:], start=True, stop=True)
                ins.then_inc(S["hv_mm"], 1)
            for g in range(NG):
                pe.wait_ge(S["hv_ev"], g + 1)
                pe.wait_ge(S["ln_xnT"], 4 * NG + g + 1)
                mm(bank(4 + g)[:, 0, :], w["Wq1"][:], xnT[:, gcols(g)], start=True, stop=True).then_inc(S["hq_mm"], 1)
                if g == 0:
                    mm(bank(0)[:, 0, 0:P], ones[0:1, :], w["bo1"][:], start=True, stop=True).then_inc(S["bo_mm"], 1)
            pe.wait_ge(S["bo_ev"], 1)

            def head_scores(b, q):
                pe.wait_ge(S["kz_ready"], b + 1)
                for r in range(2 * q, 2 * q + 2):
                    rows = slice(32 * r, 32 * r + 32)
                    for n, (i, j) in enumerate(((0, 0), (0, 1), (1, 0))):
                        ins = mm(bank(r)[:, 0, 0:HQ * LK], qhl[rows, i, b * T:(b + 1) * T], kz[rows, b % 2, j, :],
                                 start=n == 0, stop=n == 2)
                ins.then_inc(S["hs_mm"], 1)

            def head_values(b):
                pe.wait_ge(S["ht_ev"], 2 * b + 2)
                pe.wait_ge(S["vz_ready"], b + 1)
                if b:
                    pe.wait_ge(S["ho_ev"], b)
                for j in range(HQ):
                    ins = mm(bank(6)[:, 0, :].rearrange("p (r q) -> p r q", r=4), vz[0:LK, b % 2, j, :],
                             n1T[0:LK].rearrange("p (r j) q -> p j r q", j=HQ)[:, j], start=j == 0, stop=j == HQ - 1)
                ins.then_inc(S["ho_mm"], 1)

            def head_out(b):
                pe.wait_ge(S["ho_ev"], b + 1)
                if b:
                    pe.wait_ge(S["hw_res"], b)
                mm(bank(7)[:, 0, 0:P], oT, w["Wo1"][:], start=True, stop=True).then_inc(S["hw_mm"], 1)

            pe.wait_ge(S["hq_lo"], 1)
            head_scores(0, 0)
            head_scores(0, 1)
            pe.wait_ge(S["hq_lo"], NG)
            for b in range(B):
                for q in range(2):
                    if b < B - 1:
                        pe.wait_ge(S["hs_sub"], 2 * b + q + 1)
                        head_scores(b + 1, q)
                    if b:
                        head_out(b - 1) if q else head_values(b - 1)
                    pe.wait_ge(S["hs_norm"], 2 * b + q + 1)
                    if 2 * b + q:
                        pe.wait_ge(S["ht_ev"], 2 * b + q)
                    for h in range(8):
                        ins = nc.tensor.transpose(bank(4 + h // 4)[0:LK, 0, (h % 4) * T:(h % 4 + 1) * T], n1[:, 8 * q + h, :], ident[:])
                    ins.then_inc(S["ht_mm"], 1)
            head_values(B - 1)
            head_out(B - 1)
            for g in range(NG - 1):
                transpose_xn(5, g)
            pe.wait_ge(S["w_gate"], 16 * 6)

            def logits(g):
                pe.wait_ge(S["g_hid"], g + 1)
                for b in range(GB):
                    o = bank(4 + g)[:, 0, b * D:(b + 1) * D]
                    for m in range(M1):
                        mm(o, G[:, 2, g % 2, m * GT + b * T:m * GT + (b + 1) * T], w["gate_wo"][:, m, :], start=m == 0, stop=False)
                    ins = mm(o, ones[0:1, :], w["gate_bo"][:], start=False, stop=True)
                ins.then_inc(S["gl_mm"], 1)

            pe.wait_ge(S["w_split"], N_GATE + 1)
            for g in range(NG):
                pe.wait_ge(S["ln_lo"], 3 * NG + g + 1)
                if g == 0:
                    pe.wait_ge(S["hs_sub"], 2 * B)
                for m in range(M1):
                    if g:
                        pe.wait_ge(S["g_act"], M1 * (g - 1) + m + 1)
                    up(bank(m)[:, 0, :], N_GATE, m, g).then_inc(S["gu_mm"], 1)
                if g == 0:
                    transpose_xn(5, NG - 1)
                if g:
                    logits(g - 1)
            logits(NG - 1)
            for i in range(E * NG + 1):
                e, g = divmod(i, NG)
                if i < E * NG:
                    if g == 0:
                        pe.wait_ge(S["w_split"], N_E1 + e + 1)
                    for m in range(M1):
                        if i:
                            pe.wait_ge(S["act1"], M1 * (i - 1) + m + 1)
                        else:
                            pe.wait_ge(S["g_act"], M1 * NG)
                        up(bank(m)[:, 0, :], N_E1 + e, m, g).then_inc(S["up1_mm"], 1)
                if i >= 1:
                    c = i - 1
                    pe.wait_ge(S["hid1"], c + 1)
                    if c == 0:
                        pe.wait_ge(S["gl_read"], NG)
                    if c >= 2:
                        pe.wait_ge(S["res1"], c - 1)
                    sl = (c // NG) % 2
                    down(M1, lambda k, b: G[:, 2, c % 2, k * GT + b * T:k * GT + (b + 1) * T],
                         lambda k: ew1[:, sl, 1, k * D:(k + 1) * D], 4 + c % 2).then_inc(S["down1"], 1)
                g, turn = divmod(i - EB, 2)
                if 0 <= g < NG and turn == 0:
                    pe.wait_ge(S["gl_cw"], 1)
                    for b in range(GB):
                        ins = nc.tensor.transpose(bank(6)[0:E, 0, b * T:(b + 1) * T], cw1[:, g * GB + b, :], ident[:])
                    ins.then_inc(S["wt_mm"], 1)
                elif 0 <= g < NG:
                    pe.wait_ge(S["wt_ev"], g + 1)
                    if g:
                        pe.wait_ge(S["eb_res"], g)
                    for b in range(GB):
                        ins = mm(bank(7)[:, 0, b * D:(b + 1) * D], cwT[:, g * GB + b, :], w["exp_bo"][:], start=True, stop=True)
                    ins.then_inc(S["eb_mm"], 1)


def kernel(**inputs):
    import numpy as _np
    import concourse.bacc as _bacc
    from concourse import mybir as _mybir
    from concourse.bass_utils import run_bass_kernel_spmd as _run

    I = {k: _np.asarray(v) for k, v in inputs.items()}
    ctx = _np.ones((DC + 1, B, LK), _np.float32)
    ctx[0:DC] = I["ctx_512"].transpose(2, 0, 1)
    lay = {"x": I["x"], "ctxT": ctx}
    for name in ("W_in", "W_delta", "b_delta", "A_log", "D_param", "W_out"):
        lay[name] = I["L0_attn_" + name]
    lay["W_BC"] = _np.concatenate([I["L0_attn_W_B"], I["L0_attn_W_C"]], 1)
    for l, x in ((0, "L0_xattn_"), (1, "L1_xattn_")):
        lay[f"Wq{l}"], lay[f"bq{l}"] = I[x + "Wq"], I[x + "bq"]
        lay[f"Wk{l}"] = _np.concatenate([I[x + "Wk"], I[x + "bk"][None]], 0)
        lay[f"Wv{l}"] = _np.concatenate([I[x + "Wv"], I[x + "bv"][None]], 0)
    lay["Wo1"], lay["bo1"] = I["L1_xattn_Wo"], I["L1_xattn_bo"]
    lay["router0"] = I["L0_ffn_w_router"]
    for name in ("w1", "w3", "w2", "sw1", "sw3", "sw2"):
        lay[name] = I["L0_ffn_" + name]
    lay["omega"] = I["L1_attn_omega"].reshape(DI)
    lay["bl"], lay["bv"] = I["L1_attn_bl"], I["L1_attn_bv"]
    for name, src in (("Win1", "Win"), ("Wl", "Wl"), ("Wv", "Wv"), ("Wout1", "Wout")):
        lay[name] = I["L1_attn_" + src].T
    for name in ("gate_wi", "gate_bi", "gate_wo", "gate_bo", "exp_wi", "exp_wo", "exp_bo"):
        lay[name] = I["L1_ffn_" + name]
    lay["exp_bi"] = I["L1_ffn_exp_bi"].reshape(E, M1, P).transpose(2, 0, 1)

    for name in ("b_delta", "D_param", "omega", "bl", "bv", "bq0", "bq1", "gate_bi"):
        lay[name] = lay[name].reshape(-1, P).T

    nc = _bacc.Bacc("TRN2", target_bir_lowering=False, num_devices=1)
    arrays, args = {}, {}
    for name, v in lay.items():
        v = _np.ascontiguousarray(v)
        arrays[f"in_{name}_dram"] = v
        args[name] = nc.dram_tensor(f"in_{name}_dram", v.shape, _mybir.dt.from_np(v.dtype), kind="ExternalInput").ap()
    res = nc.dram_tensor("out_0_dram", (B, T, D), F32, kind="ExternalOutput").ap()
    decoder_program(nc, args, res)
    r = _run(nc, [arrays], core_ids=[0])
    return r.results[0]["out_0_dram"]
```
